# Optimizing a Trainium2 kernel written in Bass

```python
import numpy as np
import jax
import jax.numpy as jnp

def _softmax(x, axis=-1):
    return jax.nn.softmax(x, axis=axis)

def _gelu(x):
    return jax.nn.gelu(x, approximate=True)

def _silu(x):
    return jax.nn.silu(x)

def _sigmoid(x):
    return jax.nn.sigmoid(x)

def _layernorm(x, axis=-1, eps=1e-05):
    m = jnp.mean(x, axis=axis, keepdims=True)
    v = jnp.var(x, axis=axis, keepdims=True)
    return (x - m) / jnp.sqrt(v + eps)

def _scatter_add(tgt, idx, src, axis=0):
    return tgt.at[idx].add(src)

def _segment_sum(src, seg, n):
    return jax.ops.segment_sum(src, seg, n)
kernel_name = 'mk_adj_ffn_d2_adj_r2_3308dd'

def setup_inputs(seed: int=0):
    np.random.seed(seed)
    _w = jnp.asarray

    def _rec_inputs():
        import jax
        import jax.numpy as jnp
        _gk = jax.random.key(seed)
        x = -0.0005207 + 1.001 * jax.random.normal(jax.random.fold_in(_gk, 1), (4096, 128), jnp.float32)
        _w = (1.0 + jnp.arange(4096, dtype=jnp.float32)) ** (-0.5)
        _w = _w / _w.mean()
        _pij = jnp.clip(0.000488281 * _w[:, None] * _w[None, :], 0.0, 1.0)
        _a = jax.random.uniform(jax.random.fold_in(_gk, 2), (4096, 4096)) < _pij
        adj = _a.astype(jnp.int32)
        return (x, adj)
    x, adj = _rec_inputs()

    def _L0_gnn_setup():
        import jax, jax.numpy as jnp
        import numpy as np
        N, D = (4096, 128)
        NEG_BIG = -9000000000000000.0
        key = jax.random.key(seed)
        k1, k2, k3 = jax.random.split(key, 3)
        h = jax.random.normal(k1, (N, D), dtype=jnp.float32)
        adj = jax.random.randint(k2, (N, N), 0, 2, dtype=jnp.int32)
        bound = np.sqrt(6.0 / (2 * D + 1)).astype(np.float32)
        a = jax.random.uniform(k3, (2 * D, 1), dtype=jnp.float32, minval=-bound, maxval=bound)
        return {'h': h, 'adj': adj, 'a': a}
    _L0_gnn_all = _L0_gnn_setup()
    _L0_gnn_in = {k: v for k, v in _L0_gnn_all.items() if k in ('a',)}
    del _L0_gnn_all

    def _L0_ffn_setup():
        import jax, jax.numpy as jnp
        import numpy as np
        N_EXPERTS = 8
        TOP_K = 2
        key = jax.random.key(seed)
        ks = jax.random.split(key, 5)
        B, T, C, E, H = (8, 1024, 128, 8, 341)
        scale = 1.0 / np.sqrt(C)
        return {'x': jax.random.normal(ks[0], (B, T, C), dtype=jnp.float32), 'router_w': jax.random.normal(ks[1], (E, C), dtype=jnp.float32) * scale, 'w1': jax.random.normal(ks[2], (E, H, C), dtype=jnp.float32) * scale, 'w2': jax.random.normal(ks[3], (E, C, H), dtype=jnp.float32) * (1.0 / np.sqrt(H)), 'w3': jax.random.normal(ks[4], (E, H, C), dtype=jnp.float32) * scale}
    _L0_ffn_all = _L0_ffn_setup()
    _L0_ffn_in = {k: v for k, v in _L0_ffn_all.items() if k in ('router_w', 'w1', 'w2', 'w3')}
    del _L0_ffn_all

    def _L1_gnn_setup():
        import jax, jax.numpy as jnp
        import numpy as np
        N = 4096
        IN_F = 128
        OUT_F = 128
        ALPHA = 0.2
        NEG_INF = -1000000000000.0

        def _xavier(key, shape, gain=1.414):
            fan_in, fan_out = (shape[0], shape[1])
            bound = gain * np.sqrt(6.0 / (fan_in + fan_out))
            return jax.random.uniform(key, shape, jnp.float32, -bound, bound)
        key = jax.random.key(seed)
        k1, k2, k3, k4 = jax.random.split(key, 4)
        inp = jax.random.normal(k1, (N, IN_F), jnp.float32)
        adj = jax.random.randint(k2, (N, N), 0, 2, jnp.int32)
        W = _xavier(k3, (IN_F, OUT_F))
        a = _xavier(k4, (2 * OUT_F, 1))
        return {'inp': inp, 'adj': adj, 'W': W, 'a': a}
    _L1_gnn_all = _L1_gnn_setup()
    _L1_gnn_in = {k: v for k, v in _L1_gnn_all.items() if k in ('W', 'a')}
    del _L1_gnn_all

    def _L1_ffn_setup():
        import jax, jax.numpy as jnp
        import numpy as np
        C = 128
        HID = 512
        E = 8
        TEMP = 1.0
        key = jax.random.key(seed)
        ks = jax.random.split(key, 7)
        x = jax.random.normal(ks[0], (8, 8192, C), dtype=jnp.float32)
        W1 = jax.random.normal(ks[1], (C, HID), dtype=jnp.float32) * 0.02
        b1 = jnp.zeros((HID,), dtype=jnp.float32)
        Wg = jax.random.normal(ks[2], (HID, E), dtype=jnp.float32) * 0.02
        bg = jnp.zeros((E,), dtype=jnp.float32)
        Wd = jax.random.normal(ks[3], (E, HID, C), dtype=jnp.float32) * 0.02
        bd = jnp.zeros((E, C), dtype=jnp.float32)
        return {'x': x, 'W1': W1, 'b1': b1, 'Wg': Wg, 'bg': bg, 'Wd': Wd, 'bd': bd}
    _L1_ffn_all = _L1_ffn_setup()
    _L1_ffn_in = {k: v for k, v in _L1_ffn_all.items() if k in ('W1', 'b1', 'Wg', 'bg', 'Wd', 'bd')}
    del _L1_ffn_all
    return {'x': x, 'adj': adj, 'L0_gnn_a': _L0_gnn_in['a'], 'L0_ffn_router_w': _L0_ffn_in['router_w'], 'L0_ffn_w1': _L0_ffn_in['w1'], 'L0_ffn_w2': _L0_ffn_in['w2'], 'L0_ffn_w3': _L0_ffn_in['w3'], 'L1_gnn_W': _L1_gnn_in['W'], 'L1_gnn_a': _L1_gnn_in['a'], 'L1_ffn_W1': _L1_ffn_in['W1'], 'L1_ffn_b1': _L1_ffn_in['b1'], 'L1_ffn_Wg': _L1_ffn_in['Wg'], 'L1_ffn_bg': _L1_ffn_in['bg'], 'L1_ffn_Wd': _L1_ffn_in['Wd'], 'L1_ffn_bd': _L1_ffn_in['bd']}

def reference(x, adj, L0_gnn_a, L0_ffn_router_w, L0_ffn_w1, L0_ffn_w2, L0_ffn_w3, L1_gnn_W, L1_gnn_a, L1_ffn_W1, L1_ffn_b1, L1_ffn_Wg, L1_ffn_bg, L1_ffn_Wd, L1_ffn_bd):
    import jax
    import jax.numpy as jnp

    def _L0_gnn_ref(h, adj, a):
        import jax, jax.numpy as jnp
        import numpy as np
        N, D = (4096, 128)
        NEG_BIG = -9000000000000000.0
        d = h.shape[1]
        h1 = h @ a[:d]
        h2 = h @ a[d:]
        e = jax.nn.leaky_relu(h1 + h2.T, negative_slope=0.01)
        attention = jnp.where(adj > 0, e, NEG_BIG)
        attention = jax.nn.softmax(attention, axis=1)
        return attention @ h

    def _L0_ffn_ref(x, router_w, w1, w2, w3):
        import jax, jax.numpy as jnp
        import numpy as np
        N_EXPERTS = 8
        TOP_K = 2
        B, T, C = x.shape
        flat = x.reshape(-1, C)
        logits = flat @ router_w.T
        probs = jax.nn.softmax(logits, axis=-1)
        topk_probs, topk_idx = jax.lax.top_k(probs, TOP_K)
        topk_probs = topk_probs / (jnp.sum(topk_probs, axis=-1, keepdims=True) + 1e-09)
        onehot = jax.nn.one_hot(topk_idx, N_EXPERTS, dtype=flat.dtype)
        gates = jnp.einsum('nk,nke->ne', topk_probs, onehot)
        h1 = jnp.einsum('nc,ehc->neh', flat, w1)
        h3 = jnp.einsum('nc,ehc->neh', flat, w3)
        h = jax.nn.silu(h1) * h3
        y = jnp.einsum('neh,ech->nec', h, w2)
        out = jnp.einsum('ne,nec->nc', gates, y)
        return out.reshape(B, T, C)

    def _L1_gnn_ref(inp, adj, W, a):
        import jax, jax.numpy as jnp
        import numpy as np
        N = 4096
        IN_F = 128
        OUT_F = 128
        ALPHA = 0.2
        NEG_INF = -1000000000000.0

        def _xavier(key, shape, gain=1.414):
            fan_in, fan_out = (shape[0], shape[1])
            bound = gain * np.sqrt(6.0 / (fan_in + fan_out))
            return jax.random.uniform(key, shape, jnp.float32, -bound, bound)
        h = inp @ W
        a1 = a[:OUT_F, 0]
        a2 = a[OUT_F:, 0]
        s1 = h @ a1
        s2 = h @ a2
        e = jax.nn.leaky_relu(s1[:, None] + s2[None, :], negative_slope=ALPHA)
        att = jnp.where(adj > 0, e, NEG_INF)
        att = jax.nn.softmax(att, axis=1)
        h_prime = att @ h
        return jax.nn.elu(h_prime)

    def _L1_ffn_ref(x, W1, b1, Wg, bg, Wd, bd):
        import jax, jax.numpy as jnp
        import numpy as np
        C = 128
        HID = 512
        E = 8
        TEMP = 1.0
        orig_shape = x.shape
        xf = x.reshape(-1, orig_shape[-1])
        H = jax.nn.gelu(xf @ W1 + b1, approximate=False)
        probs = jax.nn.softmax((H @ Wg + bg) / TEMP, axis=-1)
        assign = jnp.argmax(probs, axis=-1)
        out = jnp.zeros_like(xf)
        for e in range(Wd.shape[0]):
            y = H @ Wd[e] + bd[e]
            sel = (assign == e)[:, None]
            out = out + jnp.where(sel, probs[:, e:e + 1] * y, 0.0)
        return out.reshape(orig_shape)
    x = x + _L0_gnn_ref(_layernorm(x, axis=-1), adj, L0_gnn_a)
    x = x + _L0_ffn_ref(_layernorm(x, axis=-1)[None], L0_ffn_router_w, L0_ffn_w1, L0_ffn_w2, L0_ffn_w3)[0]
    x = x + _L1_gnn_ref(_layernorm(x, axis=-1), adj, L1_gnn_W, L1_gnn_a)
    x = x + _L1_ffn_ref(_layernorm(x, axis=-1)[None], L1_ffn_W1, L1_ffn_b1, L1_ffn_Wg, L1_ffn_bg, L1_ffn_Wd, L1_ffn_bd)[0]
    return x

_drawn_inputs = setup_inputs


def setup_inputs(seed=0):
    import zlib

    import numpy as np

    out = dict(_drawn_inputs(seed))
    spreads = {'L1_ffn_b1': (0.0, 0.8), 'L1_ffn_bg': (0.0, 0.673), 'L1_ffn_bd': (0.0, 0.8)}
    factors = {'L1_ffn_W1': 6.3, 'L1_ffn_Wg': 6.088, 'L1_ffn_Wd': 8.0}
    for name, (base, spread) in spreads.items():
        noise = np.random.default_rng([zlib.crc32(name.encode()), seed]).standard_normal(out[name].shape)
        drawn = base * np.exp(spread * noise) if base else spread * noise
        out[name] = jnp.asarray(drawn.astype(out[name].dtype))
    for name, factor in factors.items():
        out[name] = (out[name] * factor).astype(out[name].dtype)
    return out
```

```python
from contextlib import ExitStack

import concourse.bass as bass
from concourse import mybir

F32 = mybir.dt.float32
F32R = mybir.dt.float32r
BF16 = mybir.dt.bfloat16
I32 = mybir.dt.int32
ALU = mybir.AluOpType
ACT = mybir.ActivationFunctionType
AX = mybir.AxisListType

P = 128
N = 4096
C = 128
TILES = N // P
GROUP = 4
GROUPS = TILES // GROUP
GN = GROUP * P
HALF = N // 2
EPS = 1e-5
MASKED = 2.0 ** 100
E8 = 8
HID0 = 341
ROWS0 = E8 * HID0
CH0 = -(-ROWS0 // P)
HID1 = 512
CH1 = HID1 // P

ACT_UNITS = (0, 1, 3)
DVE_UNITS = (2,)


def wait(eng, sem, value):
    if not isinstance(value, int) or value > 0:
        eng.wait_ge(sem, value)


def wait_apart(eng, sem, value, passed):
    eng.wait_ge(sem, value)
    eng.sem_inc(passed, 1)


class Chain:

    def __init__(self, eng, sem, base):
        self.eng, self.sem, self.base, self.n = eng, sem, base, 0

    def __call__(self, instruction):
        instruction.then_inc(self.sem, 1)
        self.n += 1
        self.eng.wait_ge(self.sem, self.base + self.n)


def prepare(nc, tag, x_sb, ident, power, hrow, s1, s2b, a_rep, a1, w):
    with ExitStack() as ctx:
        def sem(name):
            return ctx.enter_context(nc.semaphore(tag + name))

        def buf(name, shape, dt=F32):
            return ctx.enter_context(nc.sbuf_tensor(tag + name, shape, dt))

        def psum(name, shape):
            return ctx.enter_context(nc.psum_tensor(tag + name, shape, F32))

        stats = buf("stats", [P, 2, GROUP, 6])
        mv = buf("mv", [P, 2, GROUP, 2])
        rstd = buf("rstd", [P, 2, GROUP])
        xn = buf("xn", [P, 2, GROUP, C])
        xT = buf("xT", [P, 2, GN])
        hT = buf("hT", [P, 2, GN])
        ps_t = psum("ps_t", [P, 2, GN])
        ps_s2 = psum("ps_s2", [P, 2, GN])
        ps_s1 = psum("ps_s1", [P, 2, GN])
        ps_hT = psum("ps_hT", [P, GN])
        ps_h = psum("ps_h", [P, GN])
        chain = sem("chain")
        var_ready = sem("var_ready")
        eps_added = sem("eps_added")
        rstd_ready = sem("rstd_ready")
        xn_ready = sem("xn_ready")
        turned = sem("turned")
        xT_ready = sem("xT_ready")
        hT_made = sem("hT_made")
        h_made = sem("h_made")
        hT_ready = sem("hT_ready")
        h_ready = sem("h_ready")
        s_made = sem("s_made")
        s_kept = sem("s_kept")
        passed_dve = sem("passed_dve")
        passed_pool = sem("passed_pool")
        block = ctx.enter_context(nc.Block())

        def groups(eng, step):
            step(0, 0)
            step(1, 1)
            with eng.Fori(1, GROUPS // 2 - 1) as j:
                step(2 * j, 0)
                step(2 * j + 1, 1)
            step(GROUPS - 2, 0)
            step(GROUPS - 1, 1)

        @block.vector
        def _(dve):
            def statistics(g, b):
                for k in range(GROUP):
                    last = nc.vector.bn_stats(stats[:, b, k, :], x_sb[:, bass.ds(g * GROUP + k, 1), :].rearrange("p a c -> p (a c)"))
                last.then_inc(chain, 1)
                wait_apart(dve, chain, 2 * g + 1, passed_dve)
                for k in range(GROUP):
                    last = nc.vector.bn_aggr(mv[:, b, k, :], stats[:, b, k, :])
                last.then_inc(chain, 1)
                dve.wait_ge(chain, 2 * g + 2)
                nc.vector.tensor_copy(rstd[:, b, :], mv[:, b, :, 1]).then_inc(var_ready, 1)

            def step(g, b):
                if not (isinstance(g, int) and g == GROUPS - 1):
                    statistics(g + 1, 1 - b)
                dve.wait_ge(rstd_ready, g + 1)
                wait(dve, turned, g - 1)
                if w is None:
                    wait(dve, h_ready, g - 1)
                for k in range(GROUP):
                    last = nc.vector.tensor_scalar(xn[:, b, k, :], x_sb[:, bass.ds(g * GROUP + k, 1), :].rearrange("p a c -> p (a c)"),
                                                   mv[:, b, k, 0:1], rstd[:, b, k:k + 1], ALU.subtract, ALU.mult)
                last.then_inc(xn_ready, 1)
                dve.wait_ge(turned, g + 1)
                wait(dve, s_made, g - 1)
                nc.vector.tensor_copy(xT[:, b, :], ps_t[:, b, :]).then_inc(xT_ready, 1)
                if w is not None:
                    dve.wait_ge(hT_made, g + 1)
                    nc.vector.tensor_copy(hT[:, b, :], ps_hT[:, :]).then_inc(hT_ready, 1)
                dve.wait_ge(s_made, g + 1)
                nc.vector.tensor_copy(s1[:, bass.ds(g * GROUP, GROUP)], ps_s1[:, b, 0:GROUP])
                nc.vector.tensor_copy(s2b[:, bass.ds(g * GN, GN)], ps_s2[:, b, :]).then_inc(s_kept, 1)

            statistics(0, 0)
            groups(dve, step)

        @block.gpsimd
        def _(pool):
            def step(g, b):
                wait_apart(pool, var_ready, g + 1, passed_pool)
                nc.gpsimd.tensor_scalar(rstd[:, b, :], rstd[:, b, :], EPS, None, ALU.add).then_inc(eps_added, 1)
                pool.wait_ge(eps_added, g + 1)
                nc.gpsimd.tensor_tensor(rstd[:, b, :], rstd[:, b, :], power[:, 0:GROUP], ALU.pow).then_inc(rstd_ready, 1)

            groups(pool, step)

        @block.scalar
        def _(act):
            def step(g, b):
                rows = hrow[:, bass.ds(g * GROUP, GROUP), :]
                if w is None:
                    act.wait_ge(xn_ready, g + 1)
                    nc.scalar.copy(rows, xn[:, b, :, :]).then_inc(h_ready, 1)
                else:
                    act.wait_ge(h_made, g + 1)
                    nc.scalar.copy(rows, ps_h[:, :].rearrange("p (k c) -> p k c", k=GROUP)).then_inc(h_ready, 1)

            groups(act, step)

        @block.tensor
        def _(pe):
            def step(g, b):
                pe.wait_ge(xn_ready, g + 1)
                wait(pe, xT_ready, g - 1)
                for k in range(GROUP):
                    last = nc.tensor.transpose(ps_t[:, b, k * P:(k + 1) * P], xn[:, b, k, :], ident[:, :])
                last.then_inc(turned, 1)
                pe.wait_ge(xT_ready, g + 1)
                src = xT
                if w is not None:
                    wait(pe, hT_ready, g)
                    nc.tensor.matmul(ps_hT[:, :], w[:, :], xT[:, b, :], start=True, stop=True).then_inc(hT_made, 1)
                    wait(pe, h_ready, g)
                    for k in range(GROUP):
                        last = nc.tensor.matmul(ps_h[:, k * C:(k + 1) * C], xT[:, b, k * P:(k + 1) * P], w[:, :],
                                                start=True, stop=True)
                    last.then_inc(h_made, 1)
                    pe.wait_ge(hT_ready, g + 1)
                    src = hT
                wait(pe, s_kept, g - 1)
                nc.tensor.matmul(ps_s2[:, b, :], a_rep[:, :], src[:, b, :], start=True, stop=True)
                for k in range(GROUP):
                    last = nc.tensor.matmul(ps_s1[:, b, k:k + 1], src[:, b, k * P:(k + 1) * P], a1[:, 0:1],
                                            start=True, stop=True)
                last.then_inc(s_made, 1)

            groups(pe, step)


def attend(nc, tag, adj, x_sb, ident, hrow, s1, s2b, slope, elu):
    with ExitStack() as ctx:
        def sem(name):
            return ctx.enter_context(nc.semaphore(tag + name))

        def buf(name, shape, dt=F32):
            return ctx.enter_context(nc.sbuf_tensor(tag + name, shape, dt))

        adj_in = buf("adj_in", [P, 4, HALF], I32)
        mask = buf("mask", [P, 2, HALF], BF16)
        t = buf("t", [P, 2, N])
        u = buf("u", [P, 2, HALF])
        v = buf("v", [P, 2, HALF])
        pT = buf("pT", [P, 8, GN])
        oT = buf("oT", [P, 2, P])
        half_max = buf("half_max", [P, 2])
        m_col = buf("m_col", [P, 4])
        bias_u = buf("bias_u", [P, 2])
        bias_v = buf("bias_v", [P, 2])
        half_sum = buf("half_sum", [P, 2])
        row_sum = buf("row_sum", [P, 1])
        inv_sum = buf("inv_sum", [P, 2])
        y = buf("y", [P, 2, C])
        y_neg = buf("y_neg", [P, 2, C])
        y_exp = buf("y_exp", [P, 2, C])
        ps_pT = [ctx.enter_context(nc.psum_tensor(f"{tag}ps_pT{m}", [P, GN], F32)) for m in range(4)]
        ps_o = [ctx.enter_context(nc.psum_tensor(f"{tag}ps_o{m}", [P, GN], F32)) for m in range(2)]
        ps_row = ctx.enter_context(nc.psum_tensor(f"{tag}ps_row", [P, GN], F32))

        adj_landed = [sem(f"adj_landed{k}") for k in range(4)]
        mask_ready = sem("mask_ready")
        t_done = sem("t_done")
        bias_chain = sem("bias_chain")
        sum_chain = sem("sum_chain")
        elu_chain = sem("elu_chain")
        bias_ready = sem("bias_ready")
        exp_done = sem("exp_done")
        p_ready = sem("p_ready")
        turned = sem("turned")
        moved_act = sem("moved_act")
        moved_dve = sem("moved_dve")
        block_used = sem("block_used")
        oT_ready = sem("oT_ready")
        o_row = sem("o_row")
        o_taken = sem("o_taken")
        y_ready = sem("y_ready")
        y_exped = sem("y_exped")
        passed_dve = sem("passed_dve")
        passed_pool = sem("passed_pool")
        block = ctx.enter_context(nc.Block())

        def tiles(eng, step):
            step(0, 0, 0)
            with eng.Fori(0, TILES // 2 - 1) as j:
                step(2 * j + 1, j, 1)
                step(2 * j + 2, j + 1, 0)
            step(TILES - 1, TILES // 2 - 1, 1)

        @block.sync
        def _(sp):
            def load(i, pair, parity):
                for q in range(2):
                    k = 2 * parity + q
                    wait(sp, mask_ready, 2 * i + q - 3)
                    sp.dma_start(adj_in[:, k, :], adj[bass.ds(i * P, P), q * HALF:(q + 1) * HALF]).then_inc(adj_landed[k], 16)

            load(0, 0, 0)
            load(1, 0, 1)
            with sp.Fori(0, TILES // 2 - 1) as j:
                load(2 * j + 2, j + 1, 0)
                load(2 * j + 3, j + 1, 1)

        @block.gpsimd
        def _(pool):
            def step(i, pair, parity):
                for q in range(2):
                    k = 2 * parity + q
                    wait(pool, t_done, 2 * i + q - 1)
                    wait_apart(pool, adj_landed[k], 16 * pair + 16, passed_pool)
                    nc.gpsimd.tensor_scalar(mask[:, q, :], adj_in[:, k, :], -1.0, MASKED, ALU.add, ALU.mult).then_inc(mask_ready, 1)

            tiles(pool, step)

        def move(eng, copy, done, i, q, m):
            eng.wait_ge(turned, 8 * i + 4 * q + m + 1)
            wait(eng, block_used, 8 * i - 8 + 4 * q + m + 1)
            copy(pT[:, 4 * q + m, :], ps_pT[m][:, :]).then_inc(done, 1)

        @block.scalar
        def _(act):
            def exps(i, parity, q):
                cols = slice(q * HALF, (q + 1) * HALF)
                act.wait_ge(bias_ready, i + 1)
                wait(act, turned, 8 * i - 4 + 4 * q)
                nc.scalar.activation(u[:, q, :], t[:, parity, cols], ACT.Exp, bias=bias_u[:, parity:parity + 1],
                                     scale=1.0).then_inc(exp_done, 1)
                nc.scalar.activation(v[:, q, :], t[:, parity, cols], ACT.Exp, bias=bias_v[:, parity:parity + 1],
                                     scale=slope).then_inc(exp_done, 1)

            def moves(i, q):
                for m in ACT_UNITS:
                    move(act, nc.scalar.copy, moved_act, i, q, m)

            def take_oT(i, parity):
                act.wait_ge(block_used, 8 * i + 8)
                wait(act, o_row, i)
                nc.scalar.copy(oT[:, parity, :], ps_o[parity][:, 0:P]).then_inc(oT_ready, 1)

            def y_exponential(i, parity):
                act.wait_ge(y_ready, i + 1)
                nc.scalar.activation(y_exp[:, parity, :], y_neg[:, parity, :], ACT.Exp).then_inc(y_exped, 1)

            def step(i, pair, parity):
                exps(i, parity, 0)
                if not (isinstance(i, int) and i == 0):
                    moves(i - 1, 1)
                exps(i, parity, 1)
                moves(i, 0)
                if not (isinstance(i, int) and i == 0):
                    take_oT(i - 1, 1 - parity)

            step(0, 0, 0)
            step(1, 0, 1)
            with act.Fori(1, TILES // 2) as j:
                for parity in range(2):
                    step(2 * j + parity, j, parity)
                    if elu:
                        y_exponential(2 * j + parity - 2, parity)
            moves(TILES - 1, 1)
            take_oT(TILES - 1, 1)
            if elu:
                for i in (TILES - 2, TILES - 1):
                    y_exponential(i, i % 2)

        @block.vector
        def _(dve):
            def logits(i, parity, q):
                cols = slice(q * HALF, (q + 1) * HALF)
                wait(dve, exp_done, 4 * i - 4)
                wait_apart(dve, mask_ready, 2 * i + q + 1, passed_dve)
                nc.vector.tensor_tensor_reduce(t[:, parity, cols], mask[:, q, :], s2b[:, cols], 1.0, -3.0e38,
                                               ALU.add, ALU.max, half_max[:, q:q + 1]).then_inc(t_done, 1)

            def biases(i, parity):
                link = Chain(dve, bias_chain, 4 * i)
                one = s1[:, bass.ds(i, 1)]
                b = slice(parity, parity + 1)
                dve.wait_ge(t_done, 2 * i + 2)
                link(nc.vector.tensor_tensor(m_col[:, 0:1], half_max[:, 0:1], half_max[:, 1:2], ALU.max))
                link(nc.vector.tensor_tensor(m_col[:, 1:2], m_col[:, 0:1], one, ALU.add))
                link(nc.vector.scalar_tensor_tensor(m_col[:, 2:3], m_col[:, 1:2], slope, m_col[:, 1:2], ALU.mult, ALU.max))
                link(nc.vector.tensor_tensor(bias_u[:, b], one, m_col[:, 2:3], ALU.subtract))
                nc.vector.scalar_tensor_tensor(bias_v[:, b], one, slope, m_col[:, 2:3], ALU.mult, ALU.subtract).then_inc(bias_ready, 1)

            def probabilities(i, q):
                dve.wait_ge(exp_done, 4 * i + 2 * q + 2)
                nc.vector.scalar_tensor_tensor(u[:, q, :], u[:, q, :], 1.0, v[:, q, :], ALU.mult, ALU.max,
                                               accum_out=half_sum[:, q:q + 1]).then_inc(p_ready, 1)

            def inverse(i, parity):
                link = Chain(dve, sum_chain, 2 * i)
                dve.wait_ge(p_ready, 2 * i + 2)
                link(nc.vector.tensor_tensor(row_sum[:, :], half_sum[:, 0:1], half_sum[:, 1:2], ALU.add))
                link(nc.vector.reciprocal(inv_sum[:, parity:parity + 1], row_sum[:, :]))

            def moves(i, q):
                for m in DVE_UNITS:
                    move(dve, nc.vector.tensor_copy, moved_dve, i, q, m)

            def finish(i, parity):
                row = x_sb[:, bass.ds(i, 1), :].rearrange("p a c -> p (a c)")
                scale = inv_sum[:, parity:parity + 1]
                dve.wait_ge(o_row, i + 1)
                if not elu:
                    nc.vector.scalar_tensor_tensor(row, ps_row[:, 0:C], scale, row, ALU.mult, ALU.add).then_inc(o_taken, 1)
                    return
                nc.vector.tensor_scalar(y[:, parity, :], ps_row[:, 0:C], scale, None, ALU.mult).then_inc(o_taken, 1)
                dve.wait_ge(o_taken, i + 1)
                nc.vector.tensor_scalar(y_neg[:, parity, :], y[:, parity, :], 0.0, None, ALU.min).then_inc(y_ready, 1)

            def finish_elu(i, parity):
                row = x_sb[:, bass.ds(i, 1), :].rearrange("p a c -> p (a c)")
                dve.wait_ge(y_exped, i + 1)
                nc.vector.scalar_tensor_tensor(y[:, parity, :], y[:, parity, :], 0.0, y_exp[:, parity, :],
                                               ALU.max, ALU.add).then_inc(elu_chain, 1)
                dve.wait_ge(elu_chain, i + 1)
                nc.vector.scalar_tensor_tensor(row, y[:, parity, :], -1.0, row, ALU.add, ALU.add)

            def step(i, pair, parity, first=False, last=False, ended=2):
                if not last:
                    logits(i + 1, 1 - parity, 0)
                if not first:
                    moves(i - 1, 1)
                probabilities(i, 0)
                if not last:
                    logits(i + 1, 1 - parity, 1)
                    biases(i + 1, 1 - parity)
                if ended >= 2:
                    if elu and ended >= 3:
                        finish_elu(i - 3, 1 - parity)
                    finish(i - 2, parity)
                moves(i, 0)
                probabilities(i, 1)
                inverse(i, parity)

            logits(0, 0, 0)
            logits(0, 0, 1)
            biases(0, 0)
            step(0, 0, 0, first=True, ended=0)
            step(1, 0, 1, ended=1)
            step(2, 1, 0, ended=2)
            with dve.Fori(0, TILES // 2 - 2) as j:
                step(2 * j + 3, j + 1, 1, ended=3)
                step(2 * j + 4, j + 2, 0, ended=3)
            step(TILES - 1, TILES // 2 - 1, 1, last=True, ended=3)
            moves(TILES - 1, 1)
            for i in (TILES - 2, TILES - 1):
                if elu:
                    finish_elu(i - 1, (i - 1) % 2)
                finish(i, i % 2)
            if elu:
                finish_elu(TILES - 1, (TILES - 1) % 2)

        @block.tensor
        def _(pe):
            def turn(i, q):
                h = 2 * i + q
                pe.wait_ge(p_ready, h + 1)
                for m in range(4):
                    if m in ACT_UNITS:
                        wait(pe, moved_act, (h - 1) * len(ACT_UNITS) + ACT_UNITS.index(m) + 1)
                    else:
                        wait(pe, moved_dve, (h - 1) * len(DVE_UNITS) + DVE_UNITS.index(m) + 1)
                    for k in range(4):
                        last = nc.tensor.transpose(ps_pT[m][:, k * P:(k + 1) * P],
                                                   u[:, q, (4 * m + k) * P:(4 * m + k + 1) * P], ident[:, :])
                    last.then_inc(turned, 1)

            def multiply(i, parity, q):
                h = 2 * i + q
                if q == 0:
                    wait(pe, oT_ready, i - 1)
                for m in range(4):
                    if m in ACT_UNITS:
                        pe.wait_ge(moved_act, h * len(ACT_UNITS) + ACT_UNITS.index(m) + 1)
                    else:
                        pe.wait_ge(moved_dve, h * len(DVE_UNITS) + DVE_UNITS.index(m) + 1)
                    for k in range(4):
                        keys = 16 * q + 4 * m + k
                        last = nc.tensor.matmul(ps_o[parity][:, 0:P], hrow[:, keys, :], pT[:, 4 * q + m, k * P:(k + 1) * P],
                                                start=(keys == 0), stop=(keys == TILES - 1))
                    last.then_inc(block_used, 1)

            def back_to_rows(i, parity):
                pe.wait_ge(oT_ready, i + 1)
                wait(pe, o_taken, i)
                nc.tensor.transpose(ps_row[:, 0:C], oT[:, parity, :], ident[:, :]).then_inc(o_row, 1)

            def step(i, pair, parity, first=False):
                turn(i, 0)
                if not first:
                    multiply(i - 1, 1 - parity, 1)
                turn(i, 1)
                multiply(i, parity, 0)
                if not first:
                    back_to_rows(i - 1, 1 - parity)

            step(0, 0, 0, first=True)
            step(1, 0, 1)
            with pe.Fori(1, TILES // 2) as j:
                step(2 * j, j, 0)
                step(2 * j + 1, j, 1)
            multiply(TILES - 1, 1, 1)
            back_to_rows(TILES - 1, 1)


def split_weights(nc, jobs):
    with ExitStack() as ctx:
        stages, landed = [], []
        for name, shape, loads, hi, lo in jobs:
            stages.append(ctx.enter_context(nc.sbuf_tensor(name + "_stage", shape, F32)))
            landed.append(ctx.enter_context(nc.semaphore(name + "_landed")))
        hi_ready = ctx.enter_context(nc.semaphore("split_hi_ready" + jobs[0][0]))
        lo_ready = ctx.enter_context(nc.semaphore("split_lo_ready" + jobs[0][0]))
        block = ctx.enter_context(nc.Block())

        @block.sync
        def _(sp):
            for n, (name, shape, loads, hi, lo) in enumerate(jobs):
                for view, dram in loads:
                    sp.dma_start(view(stages[n]), dram).then_inc(landed[n], 16)

        @block.scalar
        def _(act):
            for n, (name, shape, loads, hi, lo) in enumerate(jobs):
                act.wait_ge(landed[n], 16 * len(loads))
                for view, _ in loads:
                    last = nc.scalar.copy(view(hi), view(stages[n]))
                last.then_inc(hi_ready, 1)

        @block.vector
        def _(dve):
            for n, (name, shape, loads, hi, lo) in enumerate(jobs):
                dve.wait_ge(landed[n], 16 * len(loads))
                dve.wait_ge(hi_ready, n + 1)
                for view, _ in loads:
                    nc.vector.tensor_tensor(view(lo), view(stages[n]), view(hi).bitcast(F32), ALU.subtract).then_inc(lo_ready, 1)


def three_passes(nc, out, a_hi, a_lo, b_hi, b_lo, start=True, stop=True):
    nc.tensor.matmul(out, a_hi, b_hi, start=start, stop=False)
    nc.tensor.matmul(out, a_hi, b_lo, start=False, stop=False)
    return nc.tensor.matmul(out, a_lo, b_hi, start=False, stop=stop)


class Normaliser:

    def __init__(self, nc, buf, sem, x_sb, power, ident, ps_misc):
        self.nc, self.x, self.power, self.ident, self.ps = nc, x_sb, power, ident, ps_misc
        self.stats = buf("stats", [P, GROUP, 6])
        self.mv = buf("mv", [P, GROUP, 2])
        self.rstd = buf("rstd", [P, GROUP])
        self.xn = buf("xn", [P, GROUP, C])
        self.xT_hi = buf("xT_hi", [P, 2, GN], F32R)
        self.xT_lo = buf("xT_lo", [P, 2, GN], F32R)
        self.chain = sem("norm_chain")
        self.var_ready = sem("var_ready")
        self.eps_added = sem("eps_added")
        self.rstd_ready = sem("rstd_ready")
        self.xn_ready = sem("xn_ready")
        self.turned = sem("xn_turned")
        self.xT_hi_ready = sem("xT_hi_ready")
        self.xT_lo_ready = sem("xT_lo_ready")
        self.passed_dve = sem("norm_passed_dve")
        self.passed_pool = sem("norm_passed_pool")

    def tile(self, g, k):
        return self.x[:, bass.ds(g * GROUP + k, 1), :].rearrange("p a c -> p (a c)")

    def statistics(self, dve, g):
        for k in range(GROUP):
            last = self.nc.vector.bn_stats(self.stats[:, k, :], self.tile(g, k))
        last.then_inc(self.chain, 1)
        wait_apart(dve, self.chain, 2 * g + 1, self.passed_dve)
        for k in range(GROUP):
            last = self.nc.vector.bn_aggr(self.mv[:, k, :], self.stats[:, k, :])
        last.then_inc(self.chain, 1)
        dve.wait_ge(self.chain, 2 * g + 2)
        self.nc.vector.tensor_copy(self.rstd[:, :], self.mv[:, :, 1]).then_inc(self.var_ready, 1)

    def root(self, pool, g):
        wait_apart(pool, self.var_ready, g + 1, self.passed_pool)
        self.nc.gpsimd.tensor_scalar(self.rstd[:, :], self.rstd[:, :], EPS, None, ALU.add).then_inc(self.eps_added, 1)
        pool.wait_ge(self.eps_added, g + 1)
        self.nc.gpsimd.tensor_tensor(self.rstd[:, :], self.rstd[:, :], self.power[:, 0:GROUP], ALU.pow).then_inc(self.rstd_ready, 1)

    def scale(self, dve, g):
        dve.wait_ge(self.rstd_ready, g + 1)
        wait(dve, self.turned, g)
        for k in range(GROUP):
            last = self.nc.vector.tensor_scalar(self.xn[:, k, :], self.tile(g, k), self.mv[:, k, 0:1],
                                                self.rstd[:, k:k + 1], ALU.subtract, ALU.mult)
        last.then_inc(self.xn_ready, 1)

    def turn(self, pe, g):
        pe.wait_ge(self.xn_ready, g + 1)
        for k in range(GROUP):
            last = self.nc.tensor.transpose(self.ps[:, k * P:(k + 1) * P], self.xn[:, k, :], self.ident[:, :])
        last.then_inc(self.turned, 1)

    def take_hi(self, act, g, b):
        act.wait_ge(self.turned, g + 1)
        self.nc.scalar.copy(self.xT_hi[:, b, :], self.ps[:, :]).then_inc(self.xT_hi_ready, 1)

    def take_lo(self, dve, g, b):
        dve.wait_ge(self.xT_hi_ready, g + 1)
        self.nc.vector.tensor_tensor(self.xT_lo[:, b, :], self.ps[:, :], self.xT_hi[:, b, :].bitcast(F32),
                                     ALU.subtract).then_inc(self.xT_lo_ready, 1)


class Gates:

    def __init__(self, nc, buf, sem, ident, rank, ps_logits, ps_turn, top, bias=None):
        self.nc, self.ident, self.rank, self.ps_l, self.ps_t = nc, ident, rank, ps_logits, ps_turn
        self.top, self.bias = top, bias
        wide = [P, GROUP, E8]
        self.logits, self.e, self.probs = buf("logits", wide), buf("expo", wide), buf("probs", wide)
        self.eq, self.oh, self.rest = buf("eq", wide), buf("one_hot", wide), buf("rest", wide)
        self.oh2, self.gate = buf("one_hot2", wide), buf("gate", wide)
        self.m, self.s, self.inv = buf("gmax", [P, GROUP]), buf("gsum", [P, GROUP]), buf("ginv", [P, GROUP])
        self.p1, self.p2, self.km = buf("p1", [P, GROUP]), buf("p2", [P, GROUP]), buf("kmax", [P, GROUP])
        self.parts = buf("gate_parts", [P, GROUP, 2 * E8], F32R)
        self.gT = buf("gate_T", [2 * E8, 2, GN], F32R)
        self.chain = sem("gate_chain")
        self.logits_made = sem("logits_made")
        self.shifted = sem("shifted")
        self.exped = sem("gate_exped")
        self.parts_ready = sem("gate_parts_ready")
        self.turned = sem("gate_turned")
        self.gT_ready = sem("gate_T_ready")
        self.links_before = 1 if bias is None else 2
        self.links_after = 10 if top == 1 else 18

    def over(self, a):
        return a[:, :].unsqueeze(2).to_broadcast([P, GROUP, E8])

    def shift(self, dve, g):
        link = Chain(dve, self.chain, (self.links_before + self.links_after) * g)
        v = self.nc.vector
        dve.wait_ge(self.logits_made, g + 1)
        view = self.ps_l[:, 0:GROUP * E8].rearrange("p (k e) -> p k e", k=GROUP)
        if self.bias is not None:
            link(v.tensor_tensor(self.logits[:, :, :], view, self.bias[:, :, :], ALU.add))
            view = self.logits[:, :, :]
        link(v.tensor_reduce(self.m[:, :], view, AX.X, ALU.max))
        v.tensor_tensor(self.logits[:, :, :], view, self.over(self.m), ALU.subtract).then_inc(self.shifted, 1)
        assert link.n == self.links_before

    def exponential(self, act, g):
        act.wait_ge(self.shifted, g + 1)
        self.nc.scalar.activation(self.e[:, :, :], self.logits[:, :, :], ACT.Exp).then_inc(self.exped, 1)

    def choose(self, dve, g):
        link = Chain(dve, self.chain, (self.links_before + self.links_after) * g + self.links_before)
        v = self.nc.vector
        dve.wait_ge(self.exped, g + 1)
        link(v.tensor_reduce(self.s[:, :], self.e[:, :, :], AX.X, ALU.add))
        link(v.reciprocal(self.inv[:, :], self.s[:, :]))
        link(v.tensor_tensor(self.probs[:, :, :], self.e[:, :, :], self.over(self.inv), ALU.mult))

        def first_largest(src, p, oh):
            link(v.tensor_reduce(p[:, :], src[:, :, :], AX.X, ALU.max))
            link(v.tensor_tensor(self.eq[:, :, :], src[:, :, :], self.over(p), ALU.is_equal))
            link(v.tensor_tensor(self.eq[:, :, :], self.eq[:, :, :], self.rank[:, :, :], ALU.mult))
            link(v.tensor_reduce(self.km[:, :], self.eq[:, :, :], AX.X, ALU.max))
            link(v.tensor_tensor(oh[:, :, :], self.eq[:, :, :], self.over(self.km), ALU.is_equal))

        first_largest(self.probs, self.p1, self.oh)
        if self.top == 1:
            hot = v.tensor_tensor(self.gate[:, :, :], self.oh[:, :, :], self.probs[:, :, :], ALU.mult)
        else:
            link(v.scalar_tensor_tensor(self.rest[:, :, :], self.oh[:, :, :], -2.0, self.probs[:, :, :], ALU.mult, ALU.add))
            first_largest(self.rest, self.p2, self.oh2)
            v.tensor_tensor(self.oh[:, :, :], self.oh[:, :, :], self.oh2[:, :, :], ALU.add)
            link(v.scalar_tensor_tensor(self.s[:, :], self.p1[:, :], 1e-9, self.p2[:, :], ALU.add, ALU.add))
            v.tensor_tensor(self.probs[:, :, :], self.oh[:, :, :], self.probs[:, :, :], ALU.mult)
            link(v.reciprocal(self.inv[:, :], self.s[:, :]))
            hot = v.tensor_tensor(self.gate[:, :, :], self.probs[:, :, :], self.over(self.inv), ALU.mult)
        hot.then_inc(self.chain, 1)
        link.n += 1
        dve.wait_ge(self.chain, link.base + link.n)
        wait(dve, self.turned, g)
        link(v.tensor_copy(self.parts[:, :, 0:E8], self.gate[:, :, :]))
        v.tensor_tensor(self.parts[:, :, E8:2 * E8], self.gate[:, :, :], self.parts[:, :, 0:E8].bitcast(F32),
                        ALU.subtract).then_inc(self.parts_ready, 1)
        assert link.n == self.links_after, link.n

    def turn(self, pe, g):
        pe.wait_ge(self.parts_ready, g + 1)
        for k in range(GROUP):
            last = self.nc.tensor.transpose(self.ps_t[0:2 * E8, k * P:(k + 1) * P], self.parts[:, k, :].bitcast(F32),
                                            self.ident[:, :])
        last.then_inc(self.turned, 1)

    def take(self, dve, g, b):
        dve.wait_ge(self.turned, g + 1)
        self.nc.vector.tensor_copy(self.gT[:, b, :], self.ps_t[0:2 * E8, :]).then_inc(self.gT_ready, 1)


def mix_silu(nc, ins, x_sb, ident, power, out):
    with ExitStack() as ctx:
        def sem(name):
            return ctx.enter_context(nc.semaphore("mix0_" + name))

        def buf(name, shape, dt=F32):
            return ctx.enter_context(nc.sbuf_tensor("mix0_" + name, shape, dt))

        def psum(name):
            return ctx.enter_context(nc.psum_tensor("mix0_" + name, [P, GN], F32))

        w1 = [buf(n, [P, ROWS0], F32R) for n in ("w1_hi", "w1_lo")]
        w3 = [buf(n, [P, ROWS0], F32R) for n in ("w3_hi", "w3_lo")]
        w2 = [buf(n, [P, CH0, C], F32R) for n in ("w2_hi", "w2_lo")]
        wr = [buf(n, [P, E8], F32R) for n in ("wr_hi", "wr_lo")]
        owner = [buf(n, [2 * E8, ROWS0], F32R) for n in ("owner_hi", "owner_lo")]
        rank = buf("rank", [P, GROUP, E8])
        full = ROWS0 // P * P
        tail = ROWS0 - full
        whole = lambda a: a[:, :]
        split_weights(nc, [
            ("mix0_wr", [P, E8], [(whole, ins["L0_ffn_router_w"])], *wr),
            ("mix0_w1", [P, ROWS0], [(whole, ins["L0_ffn_w1"])], *w1),
            ("mix0_w3", [P, ROWS0], [(whole, ins["L0_ffn_w3"])], *w3),
            ("mix0_owner", [2 * E8, ROWS0], [(whole, ins["owner"])], *owner),
            ("mix0_w2", [P, CH0, C],
             [(lambda a: a[:, 0:CH0 - 1, :], ins["L0_ffn_w2"][0:full, :].rearrange("(h p) c -> p h c", p=P)),
              (lambda a: a[0:tail, CH0 - 1, :], ins["L0_ffn_w2"][full:ROWS0, :])], *w2),
        ])
        s = buf("s", [P, 2, GN])
        a = buf("a", [P, 2, GN])
        ag = buf("ag", [P, 2, GN])
        ag_hi = buf("ag_hi", [P, 4, GN], F32R)
        ag_lo = buf("ag_lo", [P, 4, GN], F32R)
        yT = buf("yT", [P, GN])
        ps_h1 = [psum(f"h1_{i}") for i in range(2)]
        ps_h3 = [psum(f"h3_{i}") for i in range(2)]
        ps_g = [psum(f"g_{i}") for i in range(2)]
        ps_y, ps_misc = psum("y"), psum("misc")
        norm = Normaliser(nc, buf, sem, x_sb, power, ident, ps_misc)
        gates = Gates(nc, buf, sem, ident, rank, ps_misc, ps_misc, top=2)
        rank_landed = sem("rank_landed")
        h1_made = sem("h1_made")
        h3_made = sem("h3_made")
        silu_done = sem("silu_done")
        a_done = sem("a_done")
        ag_done = sem("ag_done")
        hi_done = sem("hi_done")
        lo_done = sem("lo_done")
        y_added = sem("y_added")
        yT_ready = sem("yT_ready")
        y_turned = sem("y_turned")
        y_taken = sem("y_taken")
        block = ctx.enter_context(nc.Block())

        rows = lambda c: P if c < CH0 - 1 else tail

        def groups(eng, step):
            step(0, 0, True, False)
            step(1, 1, False, False)
            with eng.Fori(1, GROUPS // 2 - 1) as j:
                step(2 * j, 0, False, False)
                step(2 * j + 1, 1, False, False)
            step(GROUPS - 2, 0, False, False)
            step(GROUPS - 1, 1, False, True)

        @block.sync
        def _(sp):
            sp.dma_start(rank[:, :, :], ins["rank"]).then_inc(rank_landed, 16)

        @block.tensor
        def _(pe):
            def logits(g, b):
                pe.wait_ge(norm.xT_lo_ready, g + 1)
                for k in range(GROUP):
                    tok = slice(k * P, (k + 1) * P)
                    last = three_passes(nc, ps_misc[:, k * E8:(k + 1) * E8], norm.xT_hi[:, b, tok], norm.xT_lo[:, b, tok],
                                        wr[0][:, :], wr[1][:, :])
                last.then_inc(gates.logits_made, 1)

            def hidden(g, b, c):
                n, i, m = CH0 * g + c, c % 2, rows(c)
                units = slice(c * P, c * P + m)
                if c == 0:
                    pe.wait_ge(norm.xT_lo_ready, g + 1)
                wait(pe, silu_done, n - 1)
                three_passes(nc, ps_h1[i][0:m, :], w1[0][:, units], w1[1][:, units],
                             norm.xT_hi[:, b, :], norm.xT_lo[:, b, :]).then_inc(h1_made, 1)
                wait(pe, ag_done, n - 1)
                three_passes(nc, ps_h3[i][0:m, :], w3[0][:, units], w3[1][:, units],
                             norm.xT_hi[:, b, :], norm.xT_lo[:, b, :])
                if c == 0:
                    pe.wait_ge(gates.gT_ready, g + 1)
                nc.tensor.matmul(ps_g[i][0:m, :], owner[0][:, units], gates.gT[:, b, :], start=True, stop=True).then_inc(h3_made, 1)

            def add(g, c):
                n, m, slot = CH0 * g + c, rows(c), None
                i = (CH0 * (add_parity[0]) + c) % 4
                pe.wait_ge(hi_done, n + 1)
                pe.wait_ge(lo_done, n + 1)
                if c == 0:
                    wait(pe, yT_ready, g)
                three_passes(nc, ps_y[:, :], w2[0][0:m, c, :], w2[1][0:m, c, :], ag_hi[0:m, i, :], ag_lo[0:m, i, :],
                             start=(c == 0), stop=(c == CH0 - 1)).then_inc(y_added, 1)

            add_parity = [0]

            def y_to_rows(g):
                pe.wait_ge(yT_ready, g + 1)
                for k in range(GROUP):
                    last = nc.tensor.transpose(ps_misc[:, k * P:(k + 1) * P], yT[:, k * P:(k + 1) * P], ident[:, :])
                last.then_inc(y_turned, 1)

            def step(g, b, first, last):
                for c in range(CH0):
                    hidden(g, b, c)
                    if c >= 2:
                        add_parity[0] = b
                        add(g, c - 2)
                    elif not first:
                        add_parity[0] = 1 - b
                        add(g - 1, CH0 - 2 + c)
                    if c == 3 and not first:
                        y_to_rows(g - 1)
                    if last:
                        continue
                    if c == 9:
                        wait(pe, y_taken, g)
                        norm.turn(pe, g + 1)
                    if c == 12:
                        logits(g + 1, 1 - b)
                    if c == 20:
                        gates.turn(pe, g + 1)

            norm.turn(pe, 0)
            logits(0, 0)
            gates.turn(pe, 0)
            groups(pe, step)
            add_parity[0] = 1
            add(GROUPS - 1, CH0 - 2)
            add(GROUPS - 1, CH0 - 1)
            y_to_rows(GROUPS - 1)

        @block.scalar
        def _(act):
            def split_hi(g, b, c):
                n, m = CH0 * g + c, rows(c)
                act.wait_ge(ag_done, n + 1)
                wait(act, y_added, n - 3)
                nc.scalar.copy(ag_hi[0:m, (CH0 * b + c) % 4, :], ag[0:m, c % 2, :]).then_inc(hi_done, 1)

            def step(g, b, first, last):
                for c in range(CH0):
                    n, m = CH0 * g + c, rows(c)
                    act.wait_ge(h1_made, n + 1)
                    wait(act, a_done, n - 1)
                    nc.scalar.activation(s[0:m, c % 2, :], ps_h1[c % 2][0:m, :], ACT.Silu).then_inc(silu_done, 1)
                    if c >= 1:
                        split_hi(g, b, c - 1)
                    elif not first:
                        split_hi(g - 1, 1 - b, CH0 - 1)
                    if last:
                        continue
                    if c == 10:
                        norm.take_hi(act, g + 1, 1 - b)
                    if c == 14:
                        gates.exponential(act, g + 1)

            norm.take_hi(act, 0, 0)
            gates.exponential(act, 0)
            groups(act, step)
            split_hi(GROUPS - 1, 1, CH0 - 1)

        @block.gpsimd
        def _(pool):
            def step(g, b, first, last):
                for c in range(CH0):
                    n, m, i = CH0 * g + c, rows(c), (CH0 * b + c) % 4
                    pool.wait_ge(hi_done, n + 1)
                    wait(pool, y_added, n - 3)
                    nc.gpsimd.tensor_tensor(ag_lo[0:m, i, :], ag[0:m, c % 2, :], ag_hi[0:m, i, :].bitcast(F32),
                                            ALU.subtract).then_inc(lo_done, 1)
                    if c == 6 and not last:
                        norm.root(pool, g + 1)

            norm.root(pool, 0)
            groups(pool, step)

        @block.vector
        def _(dve):
            def take_y(g):
                dve.wait_ge(y_added, CH0 * g + CH0)
                wait(dve, y_turned, g)
                nc.vector.tensor_copy(yT[:, :], ps_y[:, :]).then_inc(yT_ready, 1)

            def finish(g):
                group = x_sb[:, bass.ds(g * GROUP, GROUP), :]
                dve.wait_ge(y_turned, g + 1)
                nc.vector.tensor_tensor(group, ps_misc[:, :].rearrange("p (k c) -> p k c", k=GROUP), group,
                                        ALU.add).then_inc(y_taken, 1)

            def step(g, b, first, last):
                for c in range(CH0):
                    n, m, i = CH0 * g + c, rows(c), c % 2
                    dve.wait_ge(silu_done, n + 1)
                    dve.wait_ge(h3_made, n + 1)
                    nc.vector.tensor_tensor(a[0:m, i, :], ps_h3[i][0:m, :], s[0:m, i, :], ALU.mult).then_inc(a_done, 1)
                    dve.wait_ge(a_done, n + 1)
                    wait(dve, lo_done, n - 1)
                    nc.vector.tensor_tensor(ag[0:m, i, :], ps_g[i][0:m, :], a[0:m, i, :], ALU.mult).then_inc(ag_done, 1)
                    if not first:
                        if c == 1:
                            take_y(g - 1)
                        if c == 4:
                            finish(g - 1)
                    if last:
                        continue
                    if c == 5:
                        norm.statistics(dve, g + 1)
                    if c == 7:
                        norm.scale(dve, g + 1)
                    if c == 11:
                        norm.take_lo(dve, g + 1, 1 - b)
                    if c == 13:
                        gates.shift(dve, g + 1)
                    if c == 16:
                        gates.choose(dve, g + 1)
                    if c == 21:
                        gates.take(dve, g + 1, 1 - b)

            norm.statistics(dve, 0)
            norm.scale(dve, 0)
            norm.take_lo(dve, 0, 0)
            gates.shift(dve, 0)
            dve.wait_ge(rank_landed, 16)
            gates.choose(dve, 0)
            gates.take(dve, 0, 0)
            groups(dve, step)
            take_y(GROUPS - 1)
            finish(GROUPS - 1)


def mix_gelu(nc, ins, x_sb, ident, power, out):
    with ExitStack() as ctx:
        def sem(name):
            return ctx.enter_context(nc.semaphore("mix1_" + name))

        def buf(name, shape, dt=F32):
            return ctx.enter_context(nc.sbuf_tensor("mix1_" + name, shape, dt))

        def psum(name):
            return ctx.enter_context(nc.psum_tensor("mix1_" + name, [P, GN], F32))

        w1 = [buf(n, [P, HID1], F32R) for n in ("w1_hi", "w1_lo")]
        wg = [buf(n, [P, CH1, E8], F32R) for n in ("wg_hi", "wg_lo")]
        wd = [buf(n, [P, E8, CH1, C], F32R) for n in ("wd_hi", "wd_lo")]
        bd = [buf(n, [2 * E8, C], F32R) for n in ("bd_hi", "bd_lo")]
        each = [buf(n, [2 * E8, E8 * P], F32R) for n in ("each_hi", "each_lo")]
        rank = buf("rank", [P, GROUP, E8])
        b1 = buf("b1", [P, CH1])
        bg = buf("bg", [P, GROUP, E8])
        whole = lambda a: a[:, :]
        split_weights(nc, [
            ("mix1_w1", [P, HID1], [(whole, ins["L1_ffn_W1"])], *w1),
            ("mix1_wg", [P, CH1, E8], [(lambda a: a[:, :, :], ins["L1_ffn_Wg"].rearrange("(k p) e -> p k e", p=P))], *wg),
            ("mix1_each", [2 * E8, E8 * P], [(whole, ins["each"])], *each),
            ("mix1_bd", [2 * E8, C], [(whole, ins["bd_twice"])], *bd),
            ("mix1_wd", [P, E8, CH1, C], [(lambda a: a[:, :, :, :], ins["L1_ffn_Wd"].rearrange("e (k p) c -> p e k c", p=P))], *wd),
        ])
        H = buf("H", [P, 2, GN])
        H_hi = buf("H_hi", [P, 2, CH1, GN], F32R)
        H_lo = buf("H_lo", [P, 2, CH1, GN], F32R)
        spread = buf("spread", [P, 2, GN])
        scaled = buf("scaled", [P, 2, GN])
        acc = buf("acc", [P, GN])
        ps_y = [psum(f"y_{i}") for i in range(2)]
        ps_g = [psum(f"g_{i}") for i in range(2)]
        ps_h = [psum(f"h_{i}") for i in range(2)]
        ps_misc, ps_row = psum("misc"), psum("row")
        norm = Normaliser(nc, buf, sem, x_sb, power, ident, ps_misc)
        gates = Gates(nc, buf, sem, ident, rank, ps_misc, ps_misc, top=1, bias=bg)
        small_landed = sem("small_landed")
        h_made = sem("h_made")
        gelu_done = sem("gelu_done")
        hi_done = sem("hi_done")
        lo_done = sem("lo_done")
        y_made = sem("y_made")
        g_made = sem("g_made")
        spread_done = sem("spread_done")
        scaled_done = sem("scaled_done")
        acc_done = sem("acc_done")
        bias_made = sem("bias_made")
        acc_ready = sem("acc_ready")
        acc_turned = sem("acc_turned")
        x_done = sem("x_done")
        out_stored = sem("out_stored")
        block = ctx.enter_context(nc.Block())

        def groups(eng, step):
            step(0, 0, True, False)
            step(1, 1, False, False)
            with eng.Fori(1, GROUPS // 2 - 1) as j:
                step(2 * j, 0, False, False)
                step(2 * j + 1, 1, False, False)
            step(GROUPS - 2, 0, False, False)
            step(GROUPS - 1, 1, False, True)

        @block.sync
        def _(sp):
            sp.dma_start(rank[:, :, :], ins["rank"]).then_inc(small_landed, 16)
            sp.dma_start(b1[:, :], ins["b1_cols"]).then_inc(small_landed, 16)
            sp.dma_start(bg[:, :, :], ins["bg_rows"]).then_inc(small_landed, 16)
            rows = out.rearrange("(t p) c -> p t c", p=P)

            def store(g):
                sp.wait_ge(x_done, g + 1)
                sp.dma_start(rows[:, bass.ds(g * GROUP, GROUP), :], x_sb[:, bass.ds(g * GROUP, GROUP), :]).then_inc(out_stored, 16)

            with sp.Fori(0, GROUPS) as g:
                store(g)
            sp.wait_ge(out_stored, 16 * GROUPS)

        @block.tensor
        def _(pe):
            def hidden(g, b, k):
                n = CH1 * g + k
                wait(pe, gelu_done, n - 1)
                if k == 0:
                    pe.wait_ge(norm.xT_lo_ready, g + 1)
                units = slice(k * P, (k + 1) * P)
                three_passes(nc, ps_h[k % 2][:, :], w1[0][:, units], w1[1][:, units], norm.xT_hi[:, b, :],
                             norm.xT_lo[:, b, :]).then_inc(h_made, 1)

            def logits(g, b):
                pe.wait_ge(hi_done, CH1 * g + CH1)
                pe.wait_ge(lo_done, CH1 * g + CH1)
                for t in range(GROUP):
                    tok = slice(t * P, (t + 1) * P)
                    for k in range(CH1):
                        last = three_passes(nc, ps_misc[:, t * E8:(t + 1) * E8], H_hi[:, b, k, tok], H_lo[:, b, k, tok],
                                            wg[0][:, k, :], wg[1][:, k, :], start=(k == 0), stop=(k == CH1 - 1))
                last.then_inc(gates.logits_made, 1)

            def expert(g, b, e):
                n, i = E8 * g + e, e % 2
                wait(pe, spread_done, n - 1)
                if e == 0:
                    pe.wait_ge(gates.gT_ready, g + 1)
                nc.tensor.matmul(ps_g[i][:, :], each[0][:, e * P:(e + 1) * P], gates.gT[:, b, :], start=True,
                                 stop=True).then_inc(g_made, 1)
                wait(pe, scaled_done, n - 1)
                for k in range(CH1):
                    last = three_passes(nc, ps_y[i][:, :], wd[0][:, e, k, :], wd[1][:, e, k, :], H_hi[:, b, k, :],
                                        H_lo[:, b, k, :], start=(k == 0), stop=(k == CH1 - 1))
                last.then_inc(y_made, 1)

            def expert_bias(g, b):
                wait(pe, x_done, g)
                nc.tensor.matmul(ps_row[:, :], bd[0][:, :], gates.gT[:, b, :], start=True, stop=False)
                nc.tensor.matmul(ps_row[:, :], bd[1][:, :], gates.gT[:, b, :], start=False, stop=True).then_inc(bias_made, 1)

            def to_rows(g):
                pe.wait_ge(acc_ready, g + 1)
                for k in range(GROUP):
                    last = nc.tensor.transpose(ps_row[:, k * P:(k + 1) * P], acc[:, k * P:(k + 1) * P], ident[:, :])
                last.then_inc(acc_turned, 1)

            def step(g, b, first, last):
                for e in range(E8):
                    if e == 1 and not first:
                        to_rows(g - 1)
                    expert(g, b, e)
                    if e == 3:
                        expert_bias(g, b)
                    if last:
                        continue
                    if e == 1:
                        norm.turn(pe, g + 1)
                    if e in (2, 3):
                        hidden(g + 1, 1 - b, 2 * e - 4)
                        hidden(g + 1, 1 - b, 2 * e - 3)
                    if e == 5:
                        logits(g + 1, 1 - b)
                    if e == 7:
                        gates.turn(pe, g + 1)

            norm.turn(pe, 0)
            for k in range(CH1):
                hidden(0, 0, k)
            logits(0, 0)
            gates.turn(pe, 0)
            groups(pe, step)
            to_rows(GROUPS - 1)

        @block.scalar
        def _(act):
            def activate(g, b, k):
                n = CH1 * g + k
                act.wait_ge(h_made, n + 1)
                wait(act, lo_done, n - 1)
                nc.scalar.activation(H[:, k % 2, :], ps_h[k % 2][:, :], ACT.Gelu, bias=b1[:, k:k + 1], scale=1.0).then_inc(gelu_done, 1)
                act.wait_ge(gelu_done, n + 1)
                nc.scalar.copy(H_hi[:, b, k, :], H[:, k % 2, :]).then_inc(hi_done, 1)

            def step(g, b, first, last):
                for e in range(E8):
                    n = E8 * g + e
                    act.wait_ge(g_made, n + 1)
                    wait(act, scaled_done, n - 1)
                    nc.scalar.copy(spread[:, e % 2, :], ps_g[e % 2][:, :]).then_inc(spread_done, 1)
                    if last:
                        continue
                    if e == 1:
                        norm.take_hi(act, g + 1, 1 - b)
                    if e in (2, 3):
                        activate(g + 1, 1 - b, 2 * e - 4)
                        activate(g + 1, 1 - b, 2 * e - 3)
                    if e == 5:
                        gates.exponential(act, g + 1)

            norm.take_hi(act, 0, 0)
            act.wait_ge(small_landed, 48)
            for k in range(CH1):
                activate(0, 0, k)
            gates.exponential(act, 0)
            groups(act, step)

        @block.gpsimd
        def _(pool):
            def split_lo(g, b, k):
                pool.wait_ge(hi_done, CH1 * g + k + 1)
                nc.gpsimd.tensor_tensor(H_lo[:, b, k, :], H[:, k % 2, :], H_hi[:, b, k, :].bitcast(F32),
                                        ALU.subtract).then_inc(lo_done, 1)

            def step(g, b, first, last):
                if last:
                    return
                norm.root(pool, g + 1)
                for k in range(CH1):
                    split_lo(g + 1, 1 - b, k)

            norm.root(pool, 0)
            for k in range(CH1):
                split_lo(0, 0, k)
            groups(pool, step)

        @block.vector
        def _(dve):
            def finish(g):
                group = x_sb[:, bass.ds(g * GROUP, GROUP), :]
                dve.wait_ge(acc_turned, g + 1)
                nc.vector.tensor_tensor(group, ps_row[:, :].rearrange("p (k c) -> p k c", k=GROUP), group,
                                        ALU.add).then_inc(x_done, 1)

            def step(g, b, first, last):
                for e in range(E8):
                    n, i = E8 * g + e, e % 2
                    if not last and e == 0:
                        norm.statistics(dve, g + 1)
                    dve.wait_ge(spread_done, n + 1)
                    dve.wait_ge(y_made, n + 1)
                    if e == 0:
                        wait(dve, acc_turned, g)
                        nc.vector.tensor_tensor(acc[:, :], ps_y[i][:, :], spread[:, i, :], ALU.mult).then_inc(scaled_done, 1)
                        dve.wait_ge(scaled_done, n + 1)
                    else:
                        nc.vector.tensor_tensor(scaled[:, i, :], ps_y[i][:, :], spread[:, i, :], ALU.mult).then_inc(scaled_done, 1)
                        dve.wait_ge(scaled_done, n + 1)
                        wait(dve, acc_done, (E8 - 1) * g + e - 1)
                        nc.vector.tensor_tensor(acc[:, :], acc[:, :], scaled[:, i, :], ALU.add).then_inc(acc_done, 1)
                    if e == E8 - 1:
                        dve.wait_ge(acc_done, (E8 - 1) * g + e)
                        dve.wait_ge(bias_made, g + 1)
                        nc.vector.tensor_tensor(acc[:, :], ps_row[:, :], acc[:, :], ALU.add).then_inc(acc_ready, 1)
                    if e == 1 and not first:
                        finish(g - 1)
                    if last:
                        continue
                    if e == 0:
                        norm.scale(dve, g + 1)
                    if e == 1:
                        norm.take_lo(dve, g + 1, 1 - b)
                    if e == 5:
                        gates.shift(dve, g + 1)
                    if e == 6:
                        gates.choose(dve, g + 1)
                    if e == 7:
                        gates.take(dve, g + 1, 1 - b)

            norm.statistics(dve, 0)
            norm.scale(dve, 0)
            norm.take_lo(dve, 0, 0)
            dve.wait_ge(small_landed, 48)
            gates.shift(dve, 0)
            gates.choose(dve, 0)
            gates.take(dve, 0, 0)
            groups(dve, step)
            finish(GROUPS - 1)


def load_constants(nc, ins, x_sb, ident, power, cols):
    with ExitStack() as ctx:
        landed = ctx.enter_context(nc.semaphore("constants_landed"))
        col_landed = ctx.enter_context(nc.semaphore("columns_landed"))
        power_filled = ctx.enter_context(nc.semaphore("power_filled"))
        filled = ctx.enter_context(nc.semaphore("columns_filled"))
        block = ctx.enter_context(nc.Block())

        @block.sync
        def _(sp):
            sp.dma_start(x_sb[:, :, :], ins["x"].rearrange("(t p) c -> p t c", p=P)).then_inc(landed, 16)
            sp.dma_start(ident[:, :], ins["identity"]).then_inc(landed, 16)
            sp.dma_start(cols["w"][:, :], ins["L1_gnn_W"]).then_inc(landed, 16)
            for layer in ("L0", "L1"):
                a = ins[layer + "_gnn_a"]
                sp.dma_start(cols[layer + "a1"][:, :], a[0:C, :]).then_inc(col_landed, 16)
                sp.dma_start(cols[layer + "a2"][:, :], a[C:2 * C, :]).then_inc(col_landed, 16)
            sp.wait_ge(landed, 48)
            sp.wait_ge(col_landed, 64)

        @block.gpsimd
        def _(pool):
            nc.gpsimd.memset(power[:, :], -0.5).then_inc(power_filled, 1)
            pool.wait_ge(power_filled, 1)

        @block.vector
        def _(dve):
            for layer in ("L0", "L1"):
                nc.vector.memset(cols[layer + "rep"][:, :], 0.0).then_inc(filled, 1)
            dve.wait_ge(filled, 2)
            dve.wait_ge(col_landed, 64)
            for layer in ("L0", "L1"):
                nc.vector.tensor_scalar(cols[layer + "rep"][:, :], cols[layer + "rep"][:, :], cols[layer + "a2"][:, 0:1],
                                        None, ALU.add).then_inc(filled, 1)
            dve.wait_ge(filled, 4)


def build(nc, ins, out):
    with ExitStack() as ctx:
        def buf(name, shape, dt=F32):
            return ctx.enter_context(nc.sbuf_tensor(name, shape, dt))

        x_sb = buf("x_sb", [P, TILES, C])
        ident = buf("ident", [P, P])
        power = buf("power", [P, GROUP])
        cols = {"w": buf("gnn_w", [P, C])}
        for layer in ("L0", "L1"):
            cols[layer + "a1"] = buf(layer + "a1", [P, 1])
            cols[layer + "a2"] = buf(layer + "a2", [P, 1])
            cols[layer + "rep"] = buf(layer + "rep", [P, P])
        load_constants(nc, ins, x_sb, ident, power, cols)
        for layer, slope, w in (("L0", 0.01, None), ("L1", 0.2, cols["w"])):
            with ExitStack() as inner:
                hrow = inner.enter_context(nc.sbuf_tensor(layer + "hrow", [P, TILES, C], F32))
                s1 = inner.enter_context(nc.sbuf_tensor(layer + "s1", [P, TILES], F32))
                s2b = inner.enter_context(nc.sbuf_tensor(layer + "s2b", [P, N], F32))
                prepare(nc, layer + "prep_", x_sb, ident, power, hrow, s1, s2b, cols[layer + "rep"], cols[layer + "a1"], w)
                attend(nc, layer + "att_", ins["adj"], x_sb, ident, hrow, s1, s2b, slope, elu=w is not None)
            mixture = mix_silu if w is None else mix_gelu
            mixture(nc, ins, x_sb, ident, power, out)


def kernel(**inputs):
    import numpy as np
    import concourse.bacc as bacc
    from concourse.bass_utils import run_bass_kernel_spmd

    a = {k: np.ascontiguousarray(v) for k, v in inputs.items()}
    for name in ("w1", "w3"):
        a["L0_ffn_" + name] = np.ascontiguousarray(a["L0_ffn_" + name].reshape(ROWS0, C).T)
    a["L0_ffn_w2"] = np.ascontiguousarray(a["L0_ffn_w2"].transpose(0, 2, 1).reshape(ROWS0, C))
    a["L0_ffn_router_w"] = np.ascontiguousarray(a["L0_ffn_router_w"].T)
    a["identity"] = np.eye(P, dtype=np.float32)
    owner = (np.arange(ROWS0) // HID0)[None, :] == np.arange(E8)[:, None]
    a["owner"] = np.concatenate([owner, owner]).astype(np.float32)
    each = np.repeat(np.eye(E8, dtype=np.float32), P, axis=1)
    a["each"] = np.concatenate([each, each])
    a["bd_twice"] = np.concatenate([a["L1_ffn_bd"], a["L1_ffn_bd"]])
    a["b1_cols"] = np.ascontiguousarray(a["L1_ffn_b1"].reshape(CH1, P).T)
    a["bg_rows"] = np.ascontiguousarray(np.broadcast_to(a["L1_ffn_bg"], (P, GROUP, E8)))
    a["rank"] = np.tile(np.arange(E8, 0, -1, dtype=np.float32), (P, GROUP, 1))

    nc = bacc.Bacc("TRN2", target_bir_lowering=False, num_devices=1)
    arrays, ins = {}, {}
    for name, value in a.items():
        arrays["in_" + name] = value
        ins[name] = nc.dram_tensor("in_" + name, value.shape, mybir.dt.from_np(value.dtype), kind="ExternalInput").ap()
    out = nc.dram_tensor("out", (N, C), F32, kind="ExternalOutput").ap()
    build(nc, ins, out)
    r = run_bass_kernel_spmd(nc, [arrays], core_ids=[0])
    return r.results[0]["out"]
```

```python
from contextlib import ExitStack

import concourse.bass as bass
from concourse import mybir

F32 = mybir.dt.float32
F32R = mybir.dt.float32r
BF16 = mybir.dt.bfloat16
I32 = mybir.dt.int32
ALU = mybir.AluOpType
ACT = mybir.ActivationFunctionType
AX = mybir.AxisListType

P = 128
N = 4096
C = 128
TILES = N // P
GROUP = 4
GROUPS = TILES // GROUP
GN = GROUP * P
HALF = N // 2
EPS = 1e-5
MASKED = 2.0 ** 100
E8 = 8
HID0 = 341
ROWS0 = E8 * HID0
CH0 = -(-ROWS0 // P)
PAD0 = CH0 * P
HID1 = 512
CH1 = HID1 // P

LAG = 3
POOL_ADDS = HALF * 5 // 8


def wait(eng, sem, value):
    if not isinstance(value, int) or value > 0:
        eng.wait_ge(sem, value)


def wait_apart(eng, sem, value, passed):
    eng.wait_ge(sem, value)
    eng.sem_inc(passed, 1)


class Chain:

    def __init__(self, eng, sem, base):
        self.eng, self.sem, self.base, self.n = eng, sem, base, 0

    def __call__(self, instruction):
        instruction.then_inc(self.sem, 1)
        self.n += 1
        self.eng.wait_ge(self.sem, self.base + self.n)


class Adjacency:

    def __init__(self, nc, ctx, tag, adj, passed):
        self.nc, self.adj, self.passed = nc, adj, passed
        self.rows = ctx.enter_context(nc.sbuf_tensor(tag + "adj_in", [P, 4, HALF], I32))
        self.mask = ctx.enter_context(nc.sbuf_tensor(tag + "mask", [P, 2, HALF], BF16))
        self.landed = [ctx.enter_context(nc.semaphore(f"{tag}adj_landed{k}")) for k in range(4)]
        self.mask_ready = ctx.enter_context(nc.semaphore(tag + "mask_ready"))
        self.t_done = ctx.enter_context(nc.semaphore(tag + "t_done"))

    def load(self, sp, i, parity):
        for q in range(2):
            k = 2 * parity + q
            wait(sp, self.mask_ready, 2 * i + q - 3)
            sp.dma_start(self.rows[:, k, :], self.adj[bass.ds(i * P, P), q * HALF:(q + 1) * HALF]).then_inc(self.landed[k], 16)

    def make_mask(self, pool, i, pair, parity, q):
        wait(pool, self.t_done, 2 * i + q - 1)
        wait_apart(pool, self.landed[2 * parity + q], 16 * pair + 16, self.passed[1])
        self.nc.gpsimd.tensor_scalar(self.mask[:, q, :], self.rows[:, 2 * parity + q, :], -1.0, MASKED, ALU.add,
                                     ALU.mult).then_inc(self.mask_ready, 1)


def prepare(nc, tag, passed, x_sb, x_landed, adjacency, ident, power, hrow, s1, s2b, a_rep, a1, w):
    with ExitStack() as ctx:
        def sem(name):
            return ctx.enter_context(nc.semaphore(tag + name))

        def buf(name, shape, dt=F32):
            return ctx.enter_context(nc.sbuf_tensor(tag + name, shape, dt))

        def psum(name, shape):
            return ctx.enter_context(nc.psum_tensor(tag + name, shape, F32))

        stats = buf("stats", [P, 2, GROUP, 6])
        mv = buf("mv", [P, 2, GROUP, 2])
        rstd = buf("rstd", [P, 2, GROUP])
        xn = buf("xn", [P, 2, GROUP, C])
        xT = buf("xT", [P, 2, GN])
        hT = buf("hT", [P, 2, GN])
        ps_t = psum("ps_t", [P, 2, GN])
        ps_s2 = psum("ps_s2", [P, 2, GN])
        ps_s1 = psum("ps_s1", [P, 2, GN])
        ps_hT = psum("ps_hT", [P, GN])
        ps_h = psum("ps_h", [P, GN])
        chain = sem("chain")
        var_ready = sem("var_ready")
        eps_added = sem("eps_added")
        rstd_ready = sem("rstd_ready")
        xn_ready = sem("xn_ready")
        turned = sem("turned")
        xT_ready = sem("xT_ready")
        hT_made = sem("hT_made")
        h_made = sem("h_made")
        hT_ready = sem("hT_ready")
        h_ready = sem("h_ready")
        s_made = sem("s_made")
        s_kept = sem("s_kept")
        block = ctx.enter_context(nc.Block())

        def tile(g, k):
            return x_sb[:, bass.ds(g * GROUP + k, 1), :].rearrange("p a c -> p (a c)")

        def groups(eng, step):
            step(0, 0)
            step(1, 1)
            with eng.Fori(1, GROUPS // 2 - 1) as j:
                step(2 * j, 0)
                step(2 * j + 1, 1)
            step(GROUPS - 2, 0)
            step(GROUPS - 1, 1)

        @block.vector
        def _(dve):
            def statistics(g, b):
                if x_landed and isinstance(g, int) and g in x_landed:
                    wait_apart(dve, x_landed[g], 16, passed[0])
                for k in range(GROUP):
                    last = nc.vector.bn_stats(stats[:, b, k, :], tile(g, k))
                last.then_inc(chain, 1)
                wait_apart(dve, chain, 2 * g + 1, passed[0])
                for k in range(GROUP):
                    last = nc.vector.bn_aggr(mv[:, b, k, :], stats[:, b, k, :])
                last.then_inc(chain, 1)
                dve.wait_ge(chain, 2 * g + 2)
                nc.vector.tensor_copy(rstd[:, b, :], mv[:, b, :, 1]).then_inc(var_ready, 1)

            def scale(g, b):
                dve.wait_ge(rstd_ready, g + 1)
                wait(dve, turned, g - 1)
                if w is None:
                    wait(dve, h_ready, g - 1)
                for k in range(GROUP):
                    last = nc.vector.tensor_scalar(xn[:, b, k, :], tile(g, k), mv[:, b, k, 0:1], rstd[:, b, k:k + 1],
                                                   ALU.subtract, ALU.mult)
                last.then_inc(xn_ready, 1)

            def keep(g, b):
                dve.wait_ge(s_made, g + 1)
                nc.vector.tensor_copy(s1[:, bass.ds(g * GROUP, GROUP)], ps_s1[:, b, 0:GROUP])
                nc.vector.tensor_copy(s2b[:, bass.ds(g * GN, GN)], ps_s2[:, b, :]).then_inc(s_kept, 1)

            def step(g, b):
                if not (isinstance(g, int) and g == GROUPS - 1):
                    scale(g + 1, 1 - b)
                if not (isinstance(g, int) and g >= GROUPS - 2):
                    statistics(g + 2, b)
                if not (isinstance(g, int) and g == 0):
                    keep(g - 1, 1 - b)
                if x_landed and isinstance(g, int) and g == 1:
                    wait_apart(dve, x_landed[4], 16, passed[0])

            statistics(0, 0)
            statistics(1, 1)
            scale(0, 0)
            groups(dve, step)
            keep(GROUPS - 1, 1)

        @block.gpsimd
        def _(pool):
            def step(g, b):
                wait_apart(pool, var_ready, g + 1, passed[1])
                nc.gpsimd.tensor_scalar(rstd[:, b, :], rstd[:, b, :], EPS, None, ALU.add).then_inc(eps_added, 1)
                pool.wait_ge(eps_added, g + 1)
                nc.gpsimd.tensor_tensor(rstd[:, b, :], rstd[:, b, :], power[:, 0:GROUP], ALU.pow).then_inc(rstd_ready, 1)

            groups(pool, step)
            for q in range(2):
                adjacency.make_mask(pool, 0, 0, 0, q)

        @block.sync
        def _(sp):
            adjacency.load(sp, 0, 0)
            adjacency.load(sp, 1, 1)

        @block.scalar
        def _(act):
            def take_xT(g, b):
                act.wait_ge(turned, g + 1)
                wait(act, s_made, g - 1)
                nc.scalar.copy(xT[:, b, :], ps_t[:, b, :]).then_inc(xT_ready, 1)

            def step(g, b):
                rows = hrow[:, bass.ds(g * GROUP, GROUP), :]
                if w is None:
                    act.wait_ge(xn_ready, g + 1)
                    nc.scalar.copy(rows, xn[:, b, :, :]).then_inc(h_ready, 1)
                if not (isinstance(g, int) and g == GROUPS - 1):
                    take_xT(g + 1, 1 - b)
                if w is not None:
                    act.wait_ge(hT_made, g + 1)
                    wait(act, s_made, g - 1)
                    nc.scalar.copy(hT[:, b, :], ps_hT[:, :]).then_inc(hT_ready, 1)
                    act.wait_ge(h_made, g + 1)
                    nc.scalar.copy(rows, ps_h[:, :].rearrange("p (k c) -> p k c", k=GROUP)).then_inc(h_ready, 1)

            take_xT(0, 0)
            groups(act, step)

        @block.tensor
        def _(pe):
            def turn(g, b):
                pe.wait_ge(xn_ready, g + 1)
                wait(pe, xT_ready, g - 1)
                for k in range(GROUP):
                    last = nc.tensor.transpose(ps_t[:, b, k * P:(k + 1) * P], xn[:, b, k, :], ident[:, :])
                last.then_inc(turned, 1)

            def step(g, b):
                if not (isinstance(g, int) and g == GROUPS - 1):
                    turn(g + 1, 1 - b)
                pe.wait_ge(xT_ready, g + 1)
                src = xT
                if w is not None:
                    wait(pe, hT_ready, g)
                    nc.tensor.matmul(ps_hT[:, :], w[:, :], xT[:, b, :], start=True, stop=True).then_inc(hT_made, 1)
                    wait(pe, h_ready, g)
                    for k in range(GROUP):
                        last = nc.tensor.matmul(ps_h[:, k * C:(k + 1) * C], xT[:, b, k * P:(k + 1) * P], w[:, :],
                                                start=True, stop=True)
                    last.then_inc(h_made, 1)
                    pe.wait_ge(hT_ready, g + 1)
                    src = hT
                wait(pe, s_kept, g - 1)
                nc.tensor.matmul(ps_s2[:, b, :], a_rep[:, :], src[:, b, :], start=True, stop=True)
                for k in range(GROUP):
                    last = nc.tensor.matmul(ps_s1[:, b, k:k + 1], src[:, b, k * P:(k + 1) * P], a1[:, 0:1],
                                            start=True, stop=True)
                last.then_inc(s_made, 1)

            turn(0, 0)
            groups(pe, step)


def attend(nc, tag, passed, adjacency, ahead, ahead_landed, x_sb, ident, hrow, s1, s2b, slope, elu):
    with ExitStack() as ctx:
        def sem(name):
            return ctx.enter_context(nc.semaphore(tag + name))

        def buf(name, shape, dt=F32):
            return ctx.enter_context(nc.sbuf_tensor(tag + name, shape, dt))

        mask, mask_ready, t_done = adjacency.mask, adjacency.mask_ready, adjacency.t_done
        t = buf("t", [P, 2, HALF])
        r = buf("r", [P, 2, HALF])
        p = buf("p", [P, 4, HALF])
        pT = buf("pT", [P, 8, GN])
        oT = buf("oT", [P, 2, P])
        neg_s1 = buf("neg_s1", [P, TILES])
        half_max = buf("half_max", [P, 2])
        m_col = buf("m_col", [P, 3])
        bias = buf("bias", [P, 2])
        half_sum = buf("half_sum", [P, 2 * TILES])
        row_sum = buf("row_sum", [P, 1])
        inv_sum = buf("inv_sum", [P, 2])
        y = buf("y", [P, 2, C])
        y_neg = buf("y_neg", [P, 2, C])
        y_exp = buf("y_exp", [P, 2, C])
        z = buf("z", [P, 2, C])
        ps_pT = [ctx.enter_context(nc.psum_tensor(f"{tag}ps_pT{m}", [P, GN], F32)) for m in range(4)]
        ps_o = [ctx.enter_context(nc.psum_tensor(f"{tag}ps_o{m}", [P, GN], F32)) for m in range(2)]
        ps_row = [ctx.enter_context(nc.psum_tensor(f"{tag}ps_row{m}", [P, GN], F32)) for m in range(2)]

        negated = sem("negated")
        r_ready = sem("r_ready")
        w_pool = sem("w_pool")
        w_dve = sem("w_dve")
        bias_chain = sem("bias_chain")
        sum_chain = sem("sum_chain")
        inv_ready = sem("inv_ready")
        elu_chain = sem("elu_chain")
        bias_ready = sem("bias_ready")
        p_ready = sem("p_ready")
        turned = sem("turned")
        moved = sem("moved")
        block_used = sem("block_used")
        oT_ready = sem("oT_ready")
        o_row = sem("o_row")
        o_taken = sem("o_taken")
        y_chain = sem("y_chain")
        y_exped = sem("y_exped")
        block = ctx.enter_context(nc.Block())

        @block.sync
        def _(sp):
            for view, dram in ahead:
                sp.dma_start(view, dram).then_inc(ahead_landed, 16)
            with sp.Fori(0, TILES // 2 - 1) as j:
                adjacency.load(sp, 2 * j + 2, 0)
                adjacency.load(sp, 2 * j + 3, 1)

        def slot_free(eng, h):
            wait(eng, turned, 4 * h - 12)

        @block.gpsimd
        def _(pool):
            def add(i, parity, q):
                h = 2 * i + q
                pool.wait_ge(r_ready, h + 1)
                slot_free(pool, h)
                nc.gpsimd.tensor_tensor(p[:, 2 * parity + q, 0:POOL_ADDS], t[:, q, 0:POOL_ADDS], r[:, q, 0:POOL_ADDS],
                                        ALU.add).then_inc(w_pool, 1)

            def step(i, pair, parity):
                for q in range(2):
                    add(i - 1, 1 - parity, q)
                    adjacency.make_mask(pool, i, pair, parity, q)

            step(1, 0, 1)
            step(2, 1, 0)
            with pool.Fori(1, TILES // 2 - 1) as j:
                step(2 * j + 1, j, 1)
                step(2 * j + 2, j + 1, 0)
            step(TILES - 1, TILES // 2 - 1, 1)
            add(TILES - 1, 1, 0)
            add(TILES - 1, 1, 1)

        @block.scalar
        def _(act):
            def exponential(i, parity, q):
                h = 2 * i + q
                act.wait_ge(bias_ready, i + 1)
                act.wait_ge(w_pool, h + 1)
                act.wait_ge(w_dve, h + 1)
                slot = p[:, 2 * parity + q, :]
                nc.scalar.activation(slot, slot, ACT.Exp, bias=bias[:, parity:parity + 1], scale=slope,
                                     accum_out=half_sum[:, bass.ds(h, 1)]).then_inc(p_ready, 1)

            def moves(i, q):
                for m in range(4):
                    act.wait_ge(turned, 8 * i + 4 * q + m + 1)
                    wait(act, block_used, 8 * i - 8 + 4 * q + m + 1)
                    nc.scalar.copy(pT[:, 4 * q + m, :], ps_pT[m][:, :]).then_inc(moved, 1)

            def take_oT(i, parity):
                act.wait_ge(block_used, 8 * i + 8)
                wait(act, o_row, i - 1)
                nc.scalar.copy(oT[:, parity, :], ps_o[parity][:, 0:P]).then_inc(oT_ready, 1)

            def y_exponential(i, parity):
                y_i, y_neg_i = y[:, parity, :], y_neg[:, parity, :]
                act.wait_ge(inv_ready, i + 1)
                act.wait_ge(o_row, i + 1)
                wait(act, elu_chain, i - 1)
                nc.scalar.activation(y_i, ps_row[parity][:, 0:C], ACT.Copy, scale=inv_sum[:, parity:parity + 1]).then_inc(o_taken, 1)
                act.wait_ge(o_taken, i + 1)
                nc.scalar.activation(y_neg_i, y_i, ACT.Relu, scale=-1.0).then_inc(y_chain, 1)
                act.wait_ge(y_chain, i + 1)
                nc.scalar.activation(y_exp[:, parity, :], y_neg_i, ACT.Exp, scale=-1.0).then_inc(y_exped, 1)

            def step(i, parity, before=1):
                exponential(i, parity, 0)
                if before >= 1:
                    moves(i - 1, 1)
                exponential(i, parity, 1)
                moves(i, 0)
                if before >= 1:
                    take_oT(i - 1, 1 - parity)
                if elu and before >= 3:
                    y_exponential(i - 3, 1 - parity)

            for i in range(4):
                step(i, i % 2, before=i)
            with act.Fori(2, TILES // 2) as j:
                step(2 * j, 0, before=3)
                step(2 * j + 1, 1, before=3)
            moves(TILES - 1, 1)
            take_oT(TILES - 1, 1)
            if elu:
                for i in range(TILES - 3, TILES):
                    y_exponential(i, i % 2)

        @block.vector
        def _(dve):
            def logits(i, parity, q):
                h = 2 * i + q
                cols = slice(q * HALF, (q + 1) * HALF)
                wait(dve, w_pool, h - 1)
                wait_apart(dve, mask_ready, h + 1, passed[0])
                nc.vector.tensor_tensor_reduce(t[:, q, :], mask[:, q, :], s2b[:, cols], 1.0, -3.0e38,
                                               ALU.add, ALU.max, half_max[:, q:q + 1]).then_inc(t_done, 1)
                link = Chain(dve, bias_chain, 3 * i)
                one = s1[:, bass.ds(i, 1)]
                dve.wait_ge(t_done, h + 1)
                if q == 1:
                    nc.vector.tensor_tensor(m_col[:, 0:1], half_max[:, 0:1], half_max[:, 1:2], ALU.max).then_inc(bias_chain, 1)
                nc.vector.tensor_scalar(r[:, q, :], t[:, q, :], neg_s1[:, bass.ds(i, 1)], (1 - slope) / slope,
                                        ALU.max, ALU.mult).then_inc(r_ready, 1)
                if q == 1:
                    dve.wait_ge(bias_chain, 3 * i + 1)
                    link.n = 1
                    link(nc.vector.tensor_tensor(m_col[:, 1:2], m_col[:, 0:1], one, ALU.add))
                    link(nc.vector.scalar_tensor_tensor(m_col[:, 2:3], m_col[:, 1:2], slope, m_col[:, 1:2], ALU.mult, ALU.max))
                    wait(dve, p_ready, 2 * i - 2)
                    nc.vector.tensor_tensor(bias[:, parity:parity + 1], one, m_col[:, 2:3], ALU.subtract).then_inc(bias_ready, 1)
                dve.wait_ge(r_ready, h + 1)
                slot_free(dve, h)
                nc.vector.tensor_tensor(p[:, 2 * parity + q, POOL_ADDS:HALF], t[:, q, POOL_ADDS:HALF], r[:, q, POOL_ADDS:HALF],
                                        ALU.add).then_inc(w_dve, 1)

            def inverse(i, parity):
                dve.wait_ge(p_ready, 2 * i + 2)
                if elu:
                    wait(dve, o_taken, i - 1)
                nc.vector.tensor_tensor(row_sum[:, :], half_sum[:, bass.ds(2 * i, 1)], half_sum[:, bass.ds(2 * i + 1, 1)],
                                        ALU.add).then_inc(sum_chain, 1)
                dve.wait_ge(sum_chain, i + 1)
                nc.vector.reciprocal(inv_sum[:, parity:parity + 1], row_sum[:, :]).then_inc(inv_ready, 1)

            def finish(i, parity):
                row = x_sb[:, bass.ds(i, 1), :].rearrange("p a c -> p (a c)")
                dve.wait_ge(inv_ready, i + 1)
                dve.wait_ge(o_row, i + 1)
                nc.vector.scalar_tensor_tensor(row, ps_row[parity][:, 0:C], inv_sum[:, parity:parity + 1], row, ALU.mult,
                                               ALU.add).then_inc(o_taken, 1)

            def elu_value(i, parity):
                dve.wait_ge(y_exped, i + 1)
                nc.vector.scalar_tensor_tensor(z[:, parity, :], y_exp[:, parity, :], -1.0, y[:, parity, :],
                                               ALU.add, ALU.max).then_inc(elu_chain, 1)

            def finish_elu(i, parity):
                row = x_sb[:, bass.ds(i, 1), :].rearrange("p a c -> p (a c)")
                dve.wait_ge(elu_chain, i + 1)
                nc.vector.tensor_tensor(row, z[:, parity, :], row, ALU.add)

            def step(i, parity, before=5):
                if before >= 3:
                    inverse(i - 3, 1 - parity)
                if elu and before >= 5:
                    elu_value(i - 5, 1 - parity)
                logits(i, parity, 0)
                if before >= 3 and not elu:
                    finish(i - 3, 1 - parity)
                if elu and before >= 5:
                    finish_elu(i - 5, 1 - parity)
                logits(i, parity, 1)

            nc.vector.tensor_scalar(neg_s1[:, :], s1[:, :], -1.0, None, ALU.mult).then_inc(negated, 1)
            dve.wait_ge(negated, 1)
            for i in range(6):
                step(i, i % 2, before=i)
            with dve.Fori(3, TILES // 2) as j:
                step(2 * j, 0)
                step(2 * j + 1, 1)
            for i in range(TILES - 3, TILES):
                inverse(i, i % 2)
                if elu:
                    elu_value(i - 2, i % 2)
                    finish_elu(i - 2, i % 2)
                else:
                    finish(i, i % 2)
            if elu:
                for i in (TILES - 2, TILES - 1):
                    elu_value(i, i % 2)
                    finish_elu(i, i % 2)

        @block.tensor
        def _(pe):
            def turn(i, parity, q):
                h = 2 * i + q
                pe.wait_ge(p_ready, h + 1)
                for m in range(4):
                    wait(pe, moved, 4 * h - 4 + m + 1)
                    for k in range(4):
                        keys = (4 * m + k) * P
                        last = nc.tensor.transpose(ps_pT[m][:, k * P:(k + 1) * P], p[:, 2 * parity + q, keys:keys + P],
                                                   ident[:, :])
                    last.then_inc(turned, 1)

            def multiply(i, parity, q):
                h = 2 * i + q
                if q == 0:
                    wait(pe, oT_ready, i - 1)
                for m in range(4):
                    pe.wait_ge(moved, 4 * h + m + 1)
                    for k in range(4):
                        keys = 16 * q + 4 * m + k
                        last = nc.tensor.matmul(ps_o[parity][:, 0:P], hrow[:, keys, :], pT[:, 4 * q + m, k * P:(k + 1) * P],
                                                start=(keys == 0), stop=(keys == TILES - 1))
                    last.then_inc(block_used, 1)

            def back_to_rows(i, parity):
                pe.wait_ge(oT_ready, i + 1)
                wait(pe, o_taken, i - 1)
                nc.tensor.transpose(ps_row[parity][:, 0:C], oT[:, parity, :], ident[:, :]).then_inc(o_row, 1)

            def step(i, parity, first=False):
                turn(i, parity, 0)
                if not first:
                    multiply(i - 1, 1 - parity, 1)
                turn(i, parity, 1)
                multiply(i, parity, 0)
                if not first:
                    back_to_rows(i - 1, 1 - parity)

            step(0, 0, first=True)
            step(1, 1)
            with pe.Fori(1, TILES // 2) as j:
                step(2 * j, 0)
                step(2 * j + 1, 1)
            multiply(TILES - 1, 1, 1)
            back_to_rows(TILES - 1, 1)


def every(a):
    return a[(slice(None),) * len(a.shape)]


def three_passes(nc, out, a_hi, a_lo, b_hi, b_lo, start=True, stop=True):
    nc.tensor.matmul(out, a_hi, b_hi, start=start, stop=False)
    nc.tensor.matmul(out, a_hi, b_lo, start=False, stop=False)
    return nc.tensor.matmul(out, a_lo, b_hi, start=False, stop=stop)


class Split:

    def __init__(self, nc, sem, operands, on_pool=()):
        self.nc, self.operands, self.on_pool = nc, operands, on_pool
        self.hi_ready, self.lo_dve, self.lo_pool = sem("split_hi_ready"), sem("split_lo_dve"), sem("split_lo_pool")

    def hi(self, act, n):
        stage, hi, lo, landed, count = self.operands[n]
        act.wait_ge(landed, count)
        self.nc.scalar.copy(every(hi), every(stage)).then_inc(self.hi_ready, 1)

    def low_count(self, n):
        return sum(self.operands[k][2] is not None and (k in self.on_pool) == (n in self.on_pool) for k in range(n + 1))

    def lo(self, eng, n):
        stage, hi, lo, landed, count = self.operands[n]
        on_pool = n in self.on_pool
        maker, done = (self.nc.gpsimd, self.lo_pool) if on_pool else (self.nc.vector, self.lo_dve)
        eng.wait_ge(landed, count)
        eng.wait_ge(self.hi_ready, n + 1)
        maker.tensor_tensor(every(lo), every(stage), every(hi).bitcast(F32), ALU.subtract).then_inc(done, 1)

    def wait_for(self, pe, n):
        pe.wait_ge(self.hi_ready, n + 1)
        if self.operands[n][2] is not None:
            pe.wait_ge(self.lo_pool if n in self.on_pool else self.lo_dve, self.low_count(n))


class Normaliser:

    def __init__(self, nc, passed, buf, sem, x_sb, power, ident, ps_misc):
        self.nc, self.x, self.power, self.ident, self.ps = nc, x_sb, power, ident, ps_misc
        self.stats = buf("stats", [P, GROUP, 6])
        self.mv = buf("mv", [P, GROUP, 2])
        self.rstd = buf("rstd", [P, GROUP])
        self.xn = buf("xn", [P, GROUP, C])
        self.xT_hi = buf("xT_hi", [P, 2, GN], F32R)
        self.xT_lo = buf("xT_lo", [P, 2, GN], F32R)
        self.chain = sem("norm_chain")
        self.var_ready = sem("var_ready")
        self.eps_added = sem("eps_added")
        self.rstd_ready = sem("rstd_ready")
        self.xn_ready = sem("xn_ready")
        self.turned = sem("xn_turned")
        self.xT_hi_ready = sem("xT_hi_ready")
        self.xT_lo_ready = sem("xT_lo_ready")
        self.passed = passed

    def tile(self, g, k):
        return self.x[:, bass.ds(g * GROUP + k, 1), :].rearrange("p a c -> p (a c)")

    def statistics(self, dve, g):
        for k in range(GROUP):
            last = self.nc.vector.bn_stats(self.stats[:, k, :], self.tile(g, k))
        last.then_inc(self.chain, 1)
        wait_apart(dve, self.chain, 2 * g + 1, self.passed[0])
        for k in range(GROUP):
            last = self.nc.vector.bn_aggr(self.mv[:, k, :], self.stats[:, k, :])
        last.then_inc(self.chain, 1)
        dve.wait_ge(self.chain, 2 * g + 2)
        self.nc.vector.tensor_copy(self.rstd[:, :], self.mv[:, :, 1]).then_inc(self.var_ready, 1)

    def root(self, pool, g):
        wait_apart(pool, self.var_ready, g + 1, self.passed[1])
        self.nc.gpsimd.tensor_scalar(self.rstd[:, :], self.rstd[:, :], EPS, None, ALU.add).then_inc(self.eps_added, 1)
        pool.wait_ge(self.eps_added, g + 1)
        self.nc.gpsimd.tensor_tensor(self.rstd[:, :], self.rstd[:, :], self.power[:, 0:GROUP], ALU.pow).then_inc(self.rstd_ready, 1)

    def scale(self, dve, g):
        dve.wait_ge(self.rstd_ready, g + 1)
        wait(dve, self.turned, g)
        for k in range(GROUP):
            last = self.nc.vector.tensor_scalar(self.xn[:, k, :], self.tile(g, k), self.mv[:, k, 0:1],
                                                self.rstd[:, k:k + 1], ALU.subtract, ALU.mult)
        last.then_inc(self.xn_ready, 1)

    def turn(self, pe, g):
        pe.wait_ge(self.xn_ready, g + 1)
        for k in range(GROUP):
            last = self.nc.tensor.transpose(self.ps[:, k * P:(k + 1) * P], self.xn[:, k, :], self.ident[:, :])
        last.then_inc(self.turned, 1)

    def take_hi(self, act, g, b):
        act.wait_ge(self.turned, g + 1)
        self.nc.scalar.copy(self.xT_hi[:, b, :], self.ps[:, :]).then_inc(self.xT_hi_ready, 1)

    def take_lo(self, dve, g, b):
        dve.wait_ge(self.xT_hi_ready, g + 1)
        self.nc.vector.tensor_tensor(self.xT_lo[:, b, :], self.ps[:, :], self.xT_hi[:, b, :].bitcast(F32),
                                     ALU.subtract).then_inc(self.xT_lo_ready, 1)


class Gates:

    def __init__(self, nc, buf, sem, ident, rank, ps_misc, top, bias=None):
        self.nc, self.ident, self.rank, self.ps = nc, ident, rank, ps_misc
        self.top, self.bias = top, bias
        wide = [P, GROUP, E8]
        self.logits, self.e, self.probs = buf("logits", wide), buf("expo", wide), buf("probs", wide)
        self.eq, self.oh, self.rest = buf("eq", wide), buf("one_hot", wide), buf("rest", wide)
        self.oh2, self.gate = buf("one_hot2", wide), buf("gate", wide)
        self.m, self.s, self.inv = buf("gmax", [P, GROUP]), buf("gsum", [P, GROUP]), buf("ginv", [P, GROUP])
        self.p1, self.p2, self.km = buf("p1", [P, GROUP]), buf("p2", [P, GROUP]), buf("kmax", [P, GROUP])
        self.logits_T = buf("logits_T", [P, GN])
        self.parts = buf("gate_parts", [P, GROUP, P], F32R)
        self.gT = buf("gate_T", [2 * E8, 2, GN], F32R)
        self.chain = sem("gate_chain")
        self.zeroed = sem("gate_parts_zeroed")
        self.logits_made = sem("logits_made")
        self.logits_taken = sem("logits_taken")
        self.logits_turned = sem("logits_turned")
        self.shifted = sem("shifted")
        self.exped = sem("gate_exped")
        self.parts_ready = sem("gate_parts_ready")
        self.turned = sem("gate_turned")
        self.gT_ready = sem("gate_T_ready")
        self.links_before = 1 if bias is None else 2
        self.links_after = 10 if top == 1 else 18

    def over(self, a):
        return a[:, :].unsqueeze(2).to_broadcast([P, GROUP, E8])

    def zero(self, dve):
        self.nc.vector.memset(self.parts[:, :, :].bitcast(F32), 0.0).then_inc(self.zeroed, 1)
        dve.wait_ge(self.zeroed, 1)

    def take_logits(self, act, g):
        act.wait_ge(self.logits_made, g + 1)
        self.nc.scalar.copy(self.logits_T[:, :], self.ps[:, :]).then_inc(self.logits_taken, 1)

    def turn_logits(self, pe, g):
        pe.wait_ge(self.logits_taken, g + 1)
        for k in range(GROUP):
            last = self.nc.tensor.transpose(self.ps[:, k * P:(k + 1) * P], self.logits_T[:, k * P:(k + 1) * P],
                                            self.ident[:, :])
        last.then_inc(self.logits_turned, 1)

    def shift(self, dve, g):
        link = Chain(dve, self.chain, (self.links_before + self.links_after) * g)
        v = self.nc.vector
        dve.wait_ge(self.logits_turned, g + 1)
        view = self.ps[:, :].rearrange("p (k c) -> p k c", k=GROUP)[:, :, 0:E8]
        if self.bias is not None:
            link(v.tensor_tensor(self.logits[:, :, :], view, self.bias[:, :, :], ALU.add))
            view = self.logits[:, :, :]
        link(v.tensor_reduce(self.m[:, :], view, AX.X, ALU.max))
        v.tensor_tensor(self.logits[:, :, :], view, self.over(self.m), ALU.subtract).then_inc(self.shifted, 1)
        assert link.n == self.links_before

    def exponential(self, act, g):
        act.wait_ge(self.shifted, g + 1)
        self.nc.scalar.activation(self.e[:, :, :], self.logits[:, :, :], ACT.Exp).then_inc(self.exped, 1)

    def choose(self, dve, g):
        link = Chain(dve, self.chain, (self.links_before + self.links_after) * g + self.links_before)
        v = self.nc.vector
        dve.wait_ge(self.exped, g + 1)
        link(v.tensor_reduce(self.s[:, :], self.e[:, :, :], AX.X, ALU.add))
        link(v.reciprocal(self.inv[:, :], self.s[:, :]))
        link(v.tensor_tensor(self.probs[:, :, :], self.e[:, :, :], self.over(self.inv), ALU.mult))

        def first_largest(src, p, oh):
            link(v.tensor_reduce(p[:, :], src[:, :, :], AX.X, ALU.max))
            link(v.tensor_tensor(self.eq[:, :, :], src[:, :, :], self.over(p), ALU.is_equal))
            link(v.tensor_tensor(self.eq[:, :, :], self.eq[:, :, :], self.rank[:, :, :], ALU.mult))
            link(v.tensor_reduce(self.km[:, :], self.eq[:, :, :], AX.X, ALU.max))
            link(v.tensor_tensor(oh[:, :, :], self.eq[:, :, :], self.over(self.km), ALU.is_equal))

        first_largest(self.probs, self.p1, self.oh)
        if self.top == 1:
            hot = v.tensor_tensor(self.gate[:, :, :], self.oh[:, :, :], self.probs[:, :, :], ALU.mult)
        else:
            link(v.scalar_tensor_tensor(self.rest[:, :, :], self.oh[:, :, :], -2.0, self.probs[:, :, :], ALU.mult, ALU.add))
            first_largest(self.rest, self.p2, self.oh2)
            v.tensor_tensor(self.oh[:, :, :], self.oh[:, :, :], self.oh2[:, :, :], ALU.add)
            link(v.scalar_tensor_tensor(self.s[:, :], self.p1[:, :], 1e-9, self.p2[:, :], ALU.add, ALU.add))
            v.tensor_tensor(self.probs[:, :, :], self.oh[:, :, :], self.probs[:, :, :], ALU.mult)
            link(v.reciprocal(self.inv[:, :], self.s[:, :]))
            hot = v.tensor_tensor(self.gate[:, :, :], self.probs[:, :, :], self.over(self.inv), ALU.mult)
        hot.then_inc(self.chain, 1)
        link.n += 1
        dve.wait_ge(self.chain, link.base + link.n)
        wait(dve, self.turned, g)
        link(v.tensor_copy(self.parts[:, :, 0:E8], self.gate[:, :, :]))
        v.tensor_tensor(self.parts[:, :, E8:2 * E8], self.gate[:, :, :], self.parts[:, :, 0:E8].bitcast(F32),
                        ALU.subtract).then_inc(self.parts_ready, 1)
        assert link.n == self.links_after, link.n

    def turn(self, pe, g):
        pe.wait_ge(self.parts_ready, g + 1)
        for k in range(GROUP):
            last = self.nc.tensor.transpose(self.ps[:, k * P:(k + 1) * P], self.parts[:, k, :].bitcast(F32),
                                            self.ident[:, :])
        last.then_inc(self.turned, 1)

    def take(self, dve, g, b):
        dve.wait_ge(self.turned, g + 1)
        self.nc.vector.tensor_copy(self.gT[:, b, :], self.ps[0:2 * E8, :]).then_inc(self.gT_ready, 1)


def mix_silu(nc, passed, ins, ahead, ahead_landed, x_sb, ident, power, out):
    with ExitStack() as ctx:
        def sem(name):
            return ctx.enter_context(nc.semaphore("mix0_" + name))

        def buf(name, shape, dt=F32):
            return ctx.enter_context(nc.sbuf_tensor("mix0_" + name, shape, dt))

        def psum(name):
            return ctx.enter_context(nc.psum_tensor("mix0_" + name, [P, GN], F32))

        wr, w1, w3, w2 = ([buf(name + part, shape, F32R) for part in ("_hi", "_lo")] for name, shape in
                          (("wr", [P, P]), ("w1", [P, PAD0]), ("w3", [P, PAD0]), ("w2", [P, CH0, C])))
        owner = buf("owner", [2 * E8, PAD0], F32R)
        w2_stage, owner_stage = buf("w2_stage", [P, CH0, C]), buf("owner_stage", [2 * E8, PAD0])
        rank = buf("rank", [P, GROUP, E8])
        owner_landed, w2_landed = sem("owner_landed"), sem("w2_landed")
        split = Split(nc, sem, [(ahead[0], *wr, ahead_landed, 48), (ahead[1], *w1, ahead_landed, 48),
                                (ahead[2], *w3, ahead_landed, 48), (w2_stage, *w2, w2_landed, 16),
                                (owner_stage, owner, None, owner_landed, 16)], on_pool=(2, 3))
        WR, W1, W3, W2, OWNER = range(5)
        s = buf("s", [P, 2, GN])
        a = buf("a", [P, 2, GN])
        ag = buf("ag", [P, 2, GN])
        ag_hi = buf("ag_hi", [P, 4, GN], F32R)
        ag_lo = buf("ag_lo", [P, 4, GN], F32R)
        yT = buf("yT", [P, GN])
        ps_h1 = [psum(f"h1_{i}") for i in range(2)]
        ps_h3 = [psum(f"h3_{i}") for i in range(2)]
        ps_g = [psum(f"g_{i}") for i in range(2)]
        ps_y, ps_misc = psum("y"), psum("misc")
        norm = Normaliser(nc, passed, buf, sem, x_sb, power, ident, ps_misc)
        gates = Gates(nc, buf, sem, ident, rank, ps_misc, top=2)
        rank_landed = sem("rank_landed")
        h1_made = sem("h1_made")
        h3_made = sem("h3_made")
        silu_done = sem("silu_done")
        a_done = sem("a_done")
        ag_done = sem("ag_done")
        hi_done = sem("hi_done")
        lo_done = sem("lo_done")
        y_added = sem("y_added")
        yT_ready = sem("yT_ready")
        y_turned = sem("y_turned")
        y_taken = sem("y_taken")
        block = ctx.enter_context(nc.Block())

        def groups(eng, step):
            step(0, 0, True, False)
            step(1, 1, False, False)
            with eng.Fori(1, GROUPS // 2 - 1) as j:
                step(2 * j, 0, False, False)
                step(2 * j + 1, 1, False, False)
            step(GROUPS - 2, 0, False, False)
            step(GROUPS - 1, 1, False, True)

        @block.sync
        def _(sp):
            sp.dma_start(every(owner_stage), ins["owner"]).then_inc(owner_landed, 16)
            sp.dma_start(every(w2_stage), ins["L0_ffn_w2"].rearrange("(h p) c -> p h c", p=P)).then_inc(w2_landed, 16)
            sp.dma_start(rank[:, :, :], ins["rank"]).then_inc(rank_landed, 16)

        @block.tensor
        def _(pe):
            def logits(g, b):
                pe.wait_ge(norm.xT_lo_ready, g + 1)
                three_passes(nc, ps_misc[:, :], wr[0][:, :], wr[1][:, :], norm.xT_hi[:, b, :],
                             norm.xT_lo[:, b, :]).then_inc(gates.logits_made, 1)

            def hidden(g, b, c):
                n, i = CH0 * g + c, c % 2
                units = slice(c * P, (c + 1) * P)
                if c == 0:
                    pe.wait_ge(norm.xT_lo_ready, g + 1)
                    if isinstance(g, int) and g == 0:
                        split.wait_for(pe, W1)
                        split.wait_for(pe, W3)
                wait(pe, silu_done, n - 1)
                three_passes(nc, ps_h1[i][:, :], w1[0][:, units], w1[1][:, units],
                             norm.xT_hi[:, b, :], norm.xT_lo[:, b, :]).then_inc(h1_made, 1)
                wait(pe, ag_done, n - 1)
                three_passes(nc, ps_h3[i][:, :], w3[0][:, units], w3[1][:, units],
                             norm.xT_hi[:, b, :], norm.xT_lo[:, b, :])
                if c == 0:
                    pe.wait_ge(gates.gT_ready, g + 1)
                    if isinstance(g, int) and g == 0:
                        split.wait_for(pe, OWNER)
                nc.tensor.matmul(ps_g[i][:, :], owner[:, units], gates.gT[:, b, :], start=True, stop=True).then_inc(h3_made, 1)

            def add(g, b, c):
                n, i = CH0 * g + c, (CH0 * b + c) % 4
                pe.wait_ge(hi_done, n + 1)
                pe.wait_ge(lo_done, n + 1)
                if c == 0:
                    wait(pe, yT_ready, g)
                    if isinstance(g, int) and g == 0:
                        split.wait_for(pe, W2)
                three_passes(nc, ps_y[:, :], w2[0][:, c, :], w2[1][:, c, :], ag_hi[:, i, :], ag_lo[:, i, :],
                             start=(c == 0), stop=(c == CH0 - 1)).then_inc(y_added, 1)

            def y_to_rows(g):
                pe.wait_ge(yT_ready, g + 1)
                for k in range(GROUP):
                    last = nc.tensor.transpose(ps_misc[:, k * P:(k + 1) * P], yT[:, k * P:(k + 1) * P], ident[:, :])
                last.then_inc(y_turned, 1)

            def step(g, b, first, last):
                for c in range(CH0):
                    hidden(g, b, c)
                    if c >= LAG:
                        add(g, b, c - LAG)
                    elif not first:
                        add(g - 1, 1 - b, CH0 - LAG + c)
                    if c == 5 and not first:
                        y_to_rows(g - 1)
                    if last:
                        continue
                    if c == 9:
                        wait(pe, y_taken, g)
                        norm.turn(pe, g + 1)
                    if c == 12:
                        logits(g + 1, 1 - b)
                    if c == 14:
                        gates.turn_logits(pe, g + 1)
                    if c == 20:
                        gates.turn(pe, g + 1)

            norm.turn(pe, 0)
            split.wait_for(pe, WR)
            logits(0, 0)
            gates.turn_logits(pe, 0)
            gates.turn(pe, 0)
            groups(pe, step)
            for c in range(CH0 - LAG, CH0):
                add(GROUPS - 1, 1, c)
            y_to_rows(GROUPS - 1)

        @block.scalar
        def _(act):
            def split_hi(g, b, c):
                n = CH0 * g + c
                act.wait_ge(ag_done, n + 1)
                wait(act, y_added, n - 3)
                nc.scalar.copy(ag_hi[:, (CH0 * b + c) % 4, :], ag[:, c % 2, :]).then_inc(hi_done, 1)

            def step(g, b, first, last):
                for c in range(CH0):
                    n = CH0 * g + c
                    act.wait_ge(h1_made, n + 1)
                    wait(act, a_done, n - 1)
                    nc.scalar.activation(s[:, c % 2, :], ps_h1[c % 2][:, :], ACT.Silu).then_inc(silu_done, 1)
                    if c >= 1:
                        split_hi(g, b, c - 1)
                    elif not first:
                        split_hi(g - 1, 1 - b, CH0 - 1)
                    if last:
                        continue
                    if c == 10:
                        norm.take_hi(act, g + 1, 1 - b)
                    if c == 13:
                        gates.take_logits(act, g + 1)
                    if c == 16:
                        gates.exponential(act, g + 1)

            split.hi(act, WR)
            split.hi(act, W1)
            norm.take_hi(act, 0, 0)
            split.hi(act, W3)
            gates.take_logits(act, 0)
            split.hi(act, W2)
            gates.exponential(act, 0)
            split.hi(act, OWNER)
            groups(act, step)
            split_hi(GROUPS - 1, 1, CH0 - 1)

        @block.gpsimd
        def _(pool):
            def step(g, b, first, last):
                for c in range(CH0):
                    n, i = CH0 * g + c, (CH0 * b + c) % 4
                    pool.wait_ge(hi_done, n + 1)
                    wait(pool, y_added, n - 3)
                    nc.gpsimd.tensor_tensor(ag_lo[:, i, :], ag[:, c % 2, :], ag_hi[:, i, :].bitcast(F32),
                                            ALU.subtract).then_inc(lo_done, 1)
                    if c == 6 and not last:
                        norm.root(pool, g + 1)

            norm.root(pool, 0)
            split.lo(pool, W3)
            split.lo(pool, W2)
            groups(pool, step)

        @block.vector
        def _(dve):
            def take_y(g):
                dve.wait_ge(y_added, CH0 * g + CH0)
                wait(dve, y_turned, g)
                nc.vector.tensor_copy(yT[:, :], ps_y[:, :]).then_inc(yT_ready, 1)

            def finish(g):
                group = x_sb[:, bass.ds(g * GROUP, GROUP), :]
                dve.wait_ge(y_turned, g + 1)
                nc.vector.tensor_tensor(group, ps_misc[:, :].rearrange("p (k c) -> p k c", k=GROUP), group,
                                        ALU.add).then_inc(y_taken, 1)

            def step(g, b, first, last):
                for c in range(CH0):
                    n, i = CH0 * g + c, c % 2
                    dve.wait_ge(silu_done, n + 1)
                    dve.wait_ge(h3_made, n + 1)
                    nc.vector.tensor_tensor(a[:, i, :], ps_h3[i][:, :], s[:, i, :], ALU.mult).then_inc(a_done, 1)
                    dve.wait_ge(a_done, n + 1)
                    wait(dve, lo_done, n - 1)
                    nc.vector.tensor_tensor(ag[:, i, :], ps_g[i][:, :], a[:, i, :], ALU.mult).then_inc(ag_done, 1)
                    if not first:
                        if c == 2:
                            take_y(g - 1)
                        if c == 6:
                            finish(g - 1)
                    if last:
                        continue
                    if c == 5:
                        norm.statistics(dve, g + 1)
                    if c == 7:
                        norm.scale(dve, g + 1)
                    if c == 11:
                        norm.take_lo(dve, g + 1, 1 - b)
                    if c == 14:
                        gates.shift(dve, g + 1)
                    if c == 16:
                        gates.choose(dve, g + 1)
                    if c == 21:
                        gates.take(dve, g + 1, 1 - b)

            gates.zero(dve)
            norm.statistics(dve, 0)
            norm.scale(dve, 0)
            split.lo(dve, WR)
            split.lo(dve, W1)
            norm.take_lo(dve, 0, 0)
            gates.shift(dve, 0)
            dve.wait_ge(rank_landed, 16)
            gates.choose(dve, 0)
            gates.take(dve, 0, 0)
            groups(dve, step)
            take_y(GROUPS - 1)
            finish(GROUPS - 1)


def mix_gelu(nc, passed, ins, ahead, ahead_landed, x_sb, ident, power, out):
    with ExitStack() as ctx:
        def sem(name):
            return ctx.enter_context(nc.semaphore("mix1_" + name))

        def buf(name, shape, dt=F32):
            return ctx.enter_context(nc.sbuf_tensor("mix1_" + name, shape, dt))

        def psum(name):
            return ctx.enter_context(nc.psum_tensor("mix1_" + name, [P, GN], F32))

        w1, wg, wd, bd = ([buf(name + part, stage.shape, F32R) for part in ("_hi", "_lo")]
                          for name, stage in zip(("w1", "wg", "wd", "bd"), ahead))
        each = buf("each", ahead[4].shape, F32R)
        split = Split(nc, sem, [(ahead[0], *w1, ahead_landed, 80), (ahead[1], *wg, ahead_landed, 80),
                                (ahead[2], *wd, ahead_landed, 80), (ahead[3], *bd, ahead_landed, 80),
                                (ahead[4], each, None, ahead_landed, 80)])
        W1, WG, WD, BD, EACH = range(5)
        rank = buf("rank", [P, GROUP, E8])
        b1 = buf("b1", [P, CH1])
        bg = buf("bg", [P, GROUP, E8])
        H = buf("H", [P, 2, GN])
        H_hi = buf("H_hi", [P, 2, CH1, GN], F32R)
        H_lo = buf("H_lo", [P, 2, CH1, GN], F32R)
        spread = buf("spread", [P, 2, GN])
        scaled = buf("scaled", [P, 2, GN])
        acc = buf("acc", [P, GN])
        ps_y = [psum(f"y_{i}") for i in range(2)]
        ps_g = [psum(f"g_{i}") for i in range(2)]
        ps_h = [psum(f"h_{i}") for i in range(2)]
        ps_misc, ps_row = psum("misc"), psum("row")
        norm = Normaliser(nc, passed, buf, sem, x_sb, power, ident, ps_misc)
        gates = Gates(nc, buf, sem, ident, rank, ps_misc, top=1, bias=bg)
        small_landed = sem("small_landed")
        h_made = sem("h_made")
        gelu_done = sem("gelu_done")
        hi_done = sem("hi_done")
        lo_done = sem("lo_done")
        y_made = sem("y_made")
        g_made = sem("g_made")
        spread_done = sem("spread_done")
        scaled_done = sem("scaled_done")
        acc_done = sem("acc_done")
        bias_made = sem("bias_made")
        acc_ready = sem("acc_ready")
        acc_turned = sem("acc_turned")
        x_done = sem("x_done")
        out_stored = sem("out_stored")
        block = ctx.enter_context(nc.Block())

        def groups(eng, step):
            step(0, 0, False, True, True)
            step(1, 1, True, True, True)
            with eng.Fori(1, GROUPS // 2 - 1) as j:
                step(2 * j, 0, True, True, True)
                step(2 * j + 1, 1, True, True, True)
            step(GROUPS - 2, 0, True, True, False)
            step(GROUPS - 1, 1, True, False, False)

        @block.sync
        def _(sp):
            sp.dma_start(rank[:, :, :], ins["rank"]).then_inc(small_landed, 16)
            sp.dma_start(b1[:, :], ins["b1_cols"]).then_inc(small_landed, 16)
            sp.dma_start(bg[:, :, :], ins["bg_rows"]).then_inc(small_landed, 16)
            rows = out.rearrange("(t p) c -> p t c", p=P)

            def store(g):
                sp.wait_ge(x_done, g + 1)
                sp.dma_start(rows[:, bass.ds(g * GROUP, GROUP), :], x_sb[:, bass.ds(g * GROUP, GROUP), :]).then_inc(out_stored, 16)

            with sp.Fori(0, GROUPS) as g:
                store(g)
            sp.wait_ge(out_stored, 16 * GROUPS)

        @block.tensor
        def _(pe):
            def hidden(g, b, k):
                n = CH1 * g + k
                wait(pe, gelu_done, n - 1)
                if k == 0:
                    pe.wait_ge(norm.xT_lo_ready, g + 1)
                units = slice(k * P, (k + 1) * P)
                three_passes(nc, ps_h[k % 2][:, :], w1[0][:, units], w1[1][:, units], norm.xT_hi[:, b, :],
                             norm.xT_lo[:, b, :]).then_inc(h_made, 1)

            def logits(g, b):
                pe.wait_ge(hi_done, CH1 * g + CH1)
                pe.wait_ge(lo_done, CH1 * g + CH1)
                for k in range(CH1):
                    last = three_passes(nc, ps_misc[:, :], wg[0][:, k, :], wg[1][:, k, :], H_hi[:, b, k, :], H_lo[:, b, k, :],
                                        start=(k == 0), stop=(k == CH1 - 1))
                last.then_inc(gates.logits_made, 1)

            def expert(g, b, e):
                n, i = E8 * g + e, e % 2
                wait(pe, spread_done, n - 1)
                if e == 0:
                    pe.wait_ge(gates.gT_ready, g + 1)
                nc.tensor.matmul(ps_g[i][:, :], each[:, e * P:(e + 1) * P], gates.gT[:, b, :], start=True,
                                 stop=True).then_inc(g_made, 1)
                wait(pe, scaled_done, n - 1)
                for k in range(CH1):
                    last = three_passes(nc, ps_y[i][:, :], wd[0][:, e, k, :], wd[1][:, e, k, :], H_hi[:, b, k, :],
                                        H_lo[:, b, k, :], start=(k == 0), stop=(k == CH1 - 1))
                last.then_inc(y_made, 1)

            def expert_bias(g, b):
                wait(pe, x_done, g)
                nc.tensor.matmul(ps_row[:, :], bd[0][:, :], gates.gT[:, b, :], start=True, stop=False)
                nc.tensor.matmul(ps_row[:, :], bd[1][:, :], gates.gT[:, b, :], start=False, stop=True).then_inc(bias_made, 1)

            def to_rows(g):
                pe.wait_ge(acc_ready, g + 1)
                for k in range(GROUP):
                    last = nc.tensor.transpose(ps_row[:, k * P:(k + 1) * P], acc[:, k * P:(k + 1) * P], ident[:, :])
                last.then_inc(acc_turned, 1)

            def step(g, b, before, after, after2):
                for e in range(E8):
                    expert(g, b, e)
                    if e == 0 and before:
                        to_rows(g - 1)
                    if e < 2 and after:
                        hidden(g + 1, 1 - b, 2 * e)
                        hidden(g + 1, 1 - b, 2 * e + 1)
                    if e == 2 and after2:
                        norm.turn(pe, g + 2)
                    if e == 3 and after:
                        if after2:
                            pe.wait_ge(norm.xT_lo_ready, g + 3)
                        logits(g + 1, 1 - b)
                    if e == 4 and after:
                        gates.turn_logits(pe, g + 1)
                    if e == 5:
                        expert_bias(g, b)
                    if e == 6 and after:
                        gates.turn(pe, g + 1)

            norm.turn(pe, 0)
            pe.wait_ge(norm.xT_lo_ready, 1)
            norm.turn(pe, 1)
            split.wait_for(pe, W1)
            for k in range(CH1):
                hidden(0, 0, k)
            pe.wait_ge(norm.xT_lo_ready, 2)
            split.wait_for(pe, WG)
            logits(0, 0)
            gates.turn_logits(pe, 0)
            gates.turn(pe, 0)
            for n in (WD, BD, EACH):
                split.wait_for(pe, n)
            groups(pe, step)
            to_rows(GROUPS - 1)

        @block.scalar
        def _(act):
            def activate(g, b, k):
                n = CH1 * g + k
                act.wait_ge(h_made, n + 1)
                wait(act, lo_done, n - 1)
                nc.scalar.activation(H[:, k % 2, :], ps_h[k % 2][:, :], ACT.Gelu, bias=b1[:, k:k + 1], scale=1.0).then_inc(gelu_done, 1)
                act.wait_ge(gelu_done, n + 1)
                nc.scalar.copy(H_hi[:, b, k, :], H[:, k % 2, :]).then_inc(hi_done, 1)

            def step(g, b, before, after, after2):
                for e in range(E8):
                    n = E8 * g + e
                    act.wait_ge(g_made, n + 1)
                    wait(act, scaled_done, n - 1)
                    nc.scalar.copy(spread[:, e % 2, :], ps_g[e % 2][:, :]).then_inc(spread_done, 1)
                    if e < 2 and after:
                        activate(g + 1, 1 - b, 2 * e)
                        activate(g + 1, 1 - b, 2 * e + 1)
                    if e == 2 and after2:
                        norm.take_hi(act, g + 2, b)
                    if e == 3 and after:
                        gates.take_logits(act, g + 1)
                    if e == 5 and after:
                        gates.exponential(act, g + 1)

            split.hi(act, W1)
            split.hi(act, WG)
            norm.take_hi(act, 0, 0)
            split.hi(act, WD)
            split.hi(act, BD)
            norm.take_hi(act, 1, 1)
            act.wait_ge(small_landed, 48)
            for k in range(CH1):
                activate(0, 0, k)
            gates.take_logits(act, 0)
            split.hi(act, EACH)
            gates.exponential(act, 0)
            groups(act, step)

        @block.gpsimd
        def _(pool):
            def split_lo(g, b, k):
                pool.wait_ge(hi_done, CH1 * g + k + 1)
                nc.gpsimd.tensor_tensor(H_lo[:, b, k, :], H[:, k % 2, :], H_hi[:, b, k, :].bitcast(F32),
                                        ALU.subtract).then_inc(lo_done, 1)

            def step(g, b, before, after, after2):
                for k in range(CH1):
                    if after:
                        split_lo(g + 1, 1 - b, k)
                    if k == 0 and after2:
                        norm.root(pool, g + 2)

            norm.root(pool, 0)
            norm.root(pool, 1)
            for k in range(CH1):
                split_lo(0, 0, k)
            groups(pool, step)

        @block.vector
        def _(dve):
            def finish(g):
                group = x_sb[:, bass.ds(g * GROUP, GROUP), :]
                dve.wait_ge(acc_turned, g + 1)
                nc.vector.tensor_tensor(group, ps_row[:, :].rearrange("p (k c) -> p k c", k=GROUP), group,
                                        ALU.add).then_inc(x_done, 1)

            def step(g, b, before, after, after2):
                for e in range(E8):
                    n, i = E8 * g + e, e % 2
                    dve.wait_ge(spread_done, n + 1)
                    dve.wait_ge(y_made, n + 1)
                    if e == 0:
                        wait(dve, acc_turned, g)
                        nc.vector.tensor_tensor(acc[:, :], ps_y[i][:, :], spread[:, i, :], ALU.mult).then_inc(scaled_done, 1)
                        dve.wait_ge(scaled_done, n + 1)
                    else:
                        nc.vector.tensor_tensor(scaled[:, i, :], ps_y[i][:, :], spread[:, i, :], ALU.mult).then_inc(scaled_done, 1)
                        dve.wait_ge(scaled_done, n + 1)
                        wait(dve, acc_done, (E8 - 1) * g + e - 1)
                        nc.vector.tensor_tensor(acc[:, :], acc[:, :], scaled[:, i, :], ALU.add).then_inc(acc_done, 1)
                    if e == E8 - 1:
                        dve.wait_ge(acc_done, (E8 - 1) * g + e)
                        dve.wait_ge(bias_made, g + 1)
                        nc.vector.tensor_tensor(acc[:, :], ps_row[:, :], acc[:, :], ALU.add).then_inc(acc_ready, 1)
                    if e == 0 and before:
                        finish(g - 1)
                    if e == 0 and after2:
                        norm.statistics(dve, g + 2)
                    if e == 1 and after2:
                        norm.scale(dve, g + 2)
                    if e == 2 and after2:
                        norm.take_lo(dve, g + 2, b)
                    if e == 4 and after:
                        gates.shift(dve, g + 1)
                    if e == 5 and after:
                        gates.choose(dve, g + 1)
                    if e == 6 and after:
                        gates.take(dve, g + 1, 1 - b)

            gates.zero(dve)
            norm.statistics(dve, 0)
            norm.scale(dve, 0)
            split.lo(dve, W1)
            split.lo(dve, WG)
            norm.take_lo(dve, 0, 0)
            norm.statistics(dve, 1)
            norm.scale(dve, 1)
            norm.take_lo(dve, 1, 1)
            split.lo(dve, WD)
            split.lo(dve, BD)
            dve.wait_ge(small_landed, 48)
            gates.shift(dve, 0)
            gates.choose(dve, 0)
            gates.take(dve, 0, 0)
            groups(dve, step)
            finish(GROUPS - 1)


def load_constants(nc, ins, x_sb, x_landed, ident, power, cols):
    with ExitStack() as ctx:
        landed = ctx.enter_context(nc.semaphore("constants_landed"))
        col_landed = ctx.enter_context(nc.semaphore("columns_landed"))
        power_filled = ctx.enter_context(nc.semaphore("power_filled"))
        filled = ctx.enter_context(nc.semaphore("columns_filled"))
        block = ctx.enter_context(nc.Block())

        @block.sync
        def _(sp):
            nodes = ins["x"].rearrange("(t p) c -> p t c", p=P)
            starts = sorted(x_landed)

            def load_nodes(g, end):
                tiles = slice(g * GROUP, end * GROUP)
                sp.dma_start(x_sb[:, tiles, :], nodes[:, tiles, :]).then_inc(x_landed[g], 16)

            load_nodes(starts[0], starts[1])
            for layer in ("L0", "L1"):
                a = ins[layer + "_gnn_a"]
                sp.dma_start(cols[layer + "a1"][:, :], a[0:C, :]).then_inc(col_landed, 16)
                sp.dma_start(cols[layer + "a2"][:, :], a[C:2 * C, :]).then_inc(col_landed, 16)
            sp.dma_start(ident[:, :], ins["identity"]).then_inc(landed, 16)
            sp.dma_start(cols["w"][:, :], ins["L1_gnn_W"]).then_inc(landed, 16)
            for g, end in zip(starts[1:], starts[2:] + [GROUPS]):
                load_nodes(g, end)
            sp.wait_ge(landed, 32)
            sp.wait_ge(col_landed, 64)

        @block.gpsimd
        def _(pool):
            nc.gpsimd.memset(power[:, :], -0.5).then_inc(power_filled, 1)
            pool.wait_ge(power_filled, 1)

        @block.vector
        def _(dve):
            for layer in ("L0", "L1"):
                nc.vector.memset(cols[layer + "rep"][:, :], 0.0).then_inc(filled, 1)
            dve.wait_ge(filled, 2)
            dve.wait_ge(col_landed, 64)
            for layer in ("L0", "L1"):
                nc.vector.tensor_scalar(cols[layer + "rep"][:, :], cols[layer + "rep"][:, :], cols[layer + "a2"][:, 0:1],
                                        None, ALU.add).then_inc(filled, 1)
            dve.wait_ge(filled, 4)


def build(nc, ins, out):
    with ExitStack() as ctx:
        def buf(name, shape, dt=F32):
            return ctx.enter_context(nc.sbuf_tensor(name, shape, dt))

        passed = [ctx.enter_context(nc.semaphore(name)) for name in ("passed_dve", "passed_pool")]
        x_sb = buf("x_sb", [P, TILES, C])
        ident = buf("ident", [P, P])
        power = buf("power", [P, GROUP])
        cols = {"w": buf("gnn_w", [P, C])}
        for layer in ("L0", "L1"):
            cols[layer + "a1"] = buf(layer + "a1", [P, 1])
            cols[layer + "a2"] = buf(layer + "a2", [P, 1])
            cols[layer + "rep"] = buf(layer + "rep", [P, P])
        x_landed = {g: ctx.enter_context(nc.semaphore(f"x_landed{g}")) for g in (0, 2, 4)}
        load_constants(nc, ins, x_sb, x_landed, ident, power, cols)
        for layer, slope, w in (("L0", 0.01, None), ("L1", 0.2, cols["w"])):
            with ExitStack() as outer:
                if w is None:
                    ahead = [("wr", [P, P], ins["router_wide"]), ("w1", [P, PAD0], ins["L0_ffn_w1"]),
                             ("w3", [P, PAD0], ins["L0_ffn_w3"])]
                else:
                    ahead = [("w1", [P, HID1], ins["L1_ffn_W1"]),
                             ("wg", [P, CH1, P], ins["gate_wide"].rearrange("(k p) e -> p k e", p=P)),
                             ("wd", [P, E8, CH1, C], ins["L1_ffn_Wd"].rearrange("e (k p) c -> p e k c", p=P)),
                             ("bd", [2 * E8, C], ins["bd_twice"]), ("each", [2 * E8, E8 * P], ins["each"])]
                stages = [outer.enter_context(nc.sbuf_tensor(layer + "ahead_" + name, shape, F32)) for name, shape, _ in ahead]
                ahead_landed = outer.enter_context(nc.semaphore(layer + "ahead_landed"))
                loads = [(every(stage), dram) for stage, (_, _, dram) in zip(stages, ahead)]
                with ExitStack() as inner:
                    hrow = inner.enter_context(nc.sbuf_tensor(layer + "hrow", [P, TILES, C], F32))
                    s1 = inner.enter_context(nc.sbuf_tensor(layer + "s1", [P, TILES], F32))
                    s2b = inner.enter_context(nc.sbuf_tensor(layer + "s2b", [P, N], F32))
                    adjacency = Adjacency(nc, inner, layer, ins["adj"], passed)
                    prepare(nc, layer + "prep_", passed, x_sb, x_landed if w is None else None, adjacency, ident, power,
                            hrow, s1, s2b, cols[layer + "rep"], cols[layer + "a1"], w)
                    attend(nc, layer + "att_", passed, adjacency, loads, ahead_landed, x_sb, ident, hrow, s1, s2b, slope,
                           elu=w is not None)
                mixture = mix_silu if w is None else mix_gelu
                mixture(nc, passed, ins, stages, ahead_landed, x_sb, ident, power, out)


def kernel(**inputs):
    import numpy as np
    import concourse.bacc as bacc
    from concourse.bass_utils import run_bass_kernel_spmd

    a = {k: np.ascontiguousarray(v) for k, v in inputs.items()}

    def filled(rows, count):
        return np.pad(rows, ((0, count - rows.shape[0]), (0, 0)))

    for name in ("w1", "w3"):
        a["L0_ffn_" + name] = np.ascontiguousarray(filled(a["L0_ffn_" + name].reshape(ROWS0, C), PAD0).T)
    a["L0_ffn_w2"] = filled(a["L0_ffn_w2"].transpose(0, 2, 1).reshape(ROWS0, C), PAD0)
    a["router_wide"] = np.ascontiguousarray(filled(a["L0_ffn_router_w"], P).T)
    a["gate_wide"] = np.ascontiguousarray(filled(a["L1_ffn_Wg"].T, P).T)
    a["identity"] = np.eye(P, dtype=np.float32)
    owner = (np.arange(PAD0) // HID0)[None, :] == np.arange(E8)[:, None]
    a["owner"] = np.concatenate([owner, owner]).astype(np.float32)
    each = np.repeat(np.eye(E8, dtype=np.float32), P, axis=1)
    a["each"] = np.concatenate([each, each])
    a["bd_twice"] = np.concatenate([a["L1_ffn_bd"], a["L1_ffn_bd"]])
    a["b1_cols"] = np.ascontiguousarray(a["L1_ffn_b1"].reshape(CH1, P).T)
    a["bg_rows"] = np.ascontiguousarray(np.broadcast_to(a["L1_ffn_bg"], (P, GROUP, E8)))
    a["rank"] = np.tile(np.arange(E8, 0, -1, dtype=np.float32), (P, GROUP, 1))

    nc = bacc.Bacc("TRN2", target_bir_lowering=False, num_devices=1)
    arrays, ins = {}, {}
    for name, value in a.items():
        arrays["in_" + name] = value
        ins[name] = nc.dram_tensor("in_" + name, value.shape, mybir.dt.from_np(value.dtype), kind="ExternalInput").ap()
    out = nc.dram_tensor("out", (N, C), F32, kind="ExternalOutput").ap()
    build(nc, ins, out)
    r = run_bass_kernel_spmd(nc, [arrays], core_ids=[0])
    return r.results[0]["out"]
```

```python
from contextlib import ExitStack

import concourse.bass as bass
from concourse import mybir

F32 = mybir.dt.float32
F32R = mybir.dt.float32r
BF16 = mybir.dt.bfloat16
I32 = mybir.dt.int32
ALU = mybir.AluOpType
ACT = mybir.ActivationFunctionType
AX = mybir.AxisListType

P = 128
N = 4096
C = 128
TILES = N // P
GROUP = 4
GROUPS = TILES // GROUP
GN = GROUP * P
HALF = N // 2
EPS = 1e-5
MASKED = 2.0 ** 100
E8 = 8
HID0 = 341
ROWS0 = E8 * HID0
CH0 = -(-ROWS0 // P)
PAD0 = CH0 * P
HID1 = 512
UNITS = 2 * GROUP
CH1 = HID1 // P

LAG = 3
POOL_ADDS = HALF * 5 // 8


def wait(eng, sem, value):
    if not isinstance(value, int) or value > 0:
        eng.wait_ge(sem, value)


def wait_apart(eng, sem, value, passed):
    eng.wait_ge(sem, value)
    eng.sem_inc(passed, 1)


class Chain:

    def __init__(self, eng, sem, base):
        self.eng, self.sem, self.base, self.n = eng, sem, base, 0

    def __call__(self, instruction):
        instruction.then_inc(self.sem, 1)
        self.n += 1
        self.eng.wait_ge(self.sem, self.base + self.n)


class Adjacency:

    def __init__(self, nc, ctx, tag, adj, passed):
        self.nc, self.adj, self.passed = nc, adj, passed
        self.rows = ctx.enter_context(nc.sbuf_tensor(tag + "adj_in", [P, 4, HALF], I32))
        self.mask = ctx.enter_context(nc.sbuf_tensor(tag + "mask", [P, 2, HALF], BF16))
        self.landed = [ctx.enter_context(nc.semaphore(f"{tag}adj_landed{k}")) for k in range(4)]
        self.mask_ready = ctx.enter_context(nc.semaphore(tag + "mask_ready"))
        self.t_done = ctx.enter_context(nc.semaphore(tag + "t_done"))

    def load(self, sp, i, parity):
        for q in range(2):
            k = 2 * parity + q
            wait(sp, self.mask_ready, 2 * i + q - 3)
            sp.dma_start(self.rows[:, k, :], self.adj[bass.ds(i * P, P), q * HALF:(q + 1) * HALF]).then_inc(self.landed[k], 16)

    def make_mask(self, pool, i, pair, parity, q):
        wait(pool, self.t_done, 2 * i + q - 1)
        wait_apart(pool, self.landed[2 * parity + q], 16 * pair + 16, self.passed[1])
        self.nc.gpsimd.tensor_scalar(self.mask[:, q, :], self.rows[:, 2 * parity + q, :], -1.0, MASKED, ALU.add,
                                     ALU.mult).then_inc(self.mask_ready, 1)


class Terms:

    def __init__(self, nc, ctx, tag, adjacency, s2b, slope, passed):
        self.nc, self.adjacency, self.s2b, self.slope, self.passed = nc, adjacency, s2b, slope, passed
        self.t = ctx.enter_context(nc.sbuf_tensor(tag + "t", [P, 2, HALF], F32))
        self.r = ctx.enter_context(nc.sbuf_tensor(tag + "r", [P, 2, HALF], F32))
        self.neg_s1 = ctx.enter_context(nc.sbuf_tensor(tag + "neg_s1", [P, TILES], F32))
        self.half_max = ctx.enter_context(nc.sbuf_tensor(tag + "half_max", [P, 2], F32))
        self.t_max = ctx.enter_context(nc.sbuf_tensor(tag + "t_max", [P, 1], F32))
        self.r_ready = ctx.enter_context(nc.semaphore(tag + "r_ready"))
        self.max_ready = ctx.enter_context(nc.semaphore(tag + "max_ready"))
        self.w_pool = ctx.enter_context(nc.semaphore(tag + "w_pool"))

    def make(self, dve, i, q):
        h = 2 * i + q
        cols = slice(q * HALF, (q + 1) * HALF)
        wait(dve, self.w_pool, h - 1)
        wait_apart(dve, self.adjacency.mask_ready, h + 1, self.passed[0])
        self.nc.vector.tensor_tensor_reduce(self.t[:, q, :], self.adjacency.mask[:, q, :], self.s2b[:, cols], 1.0, -3.0e38,
                                            ALU.add, ALU.max, self.half_max[:, q:q + 1]).then_inc(self.adjacency.t_done, 1)
        dve.wait_ge(self.adjacency.t_done, h + 1)
        if q == 1:
            self.nc.vector.tensor_tensor(self.t_max[:, :], self.half_max[:, 0:1], self.half_max[:, 1:2],
                                         ALU.max).then_inc(self.max_ready, 1)
        self.nc.vector.tensor_scalar(self.r[:, q, :], self.t[:, q, :], self.neg_s1[:, bass.ds(i, 1)],
                                     (1 - self.slope) / self.slope, ALU.max, ALU.mult).then_inc(self.r_ready, 1)


def prepare(nc, tag, passed, x_sb, x_landed, adjacency, terms, ident, power, hrow, s1, s2b, a_rep, a1, w):
    with ExitStack() as ctx:
        def sem(name):
            return ctx.enter_context(nc.semaphore(tag + name))

        def buf(name, shape, dt=F32):
            return ctx.enter_context(nc.sbuf_tensor(tag + name, shape, dt))

        def psum(name, shape):
            return ctx.enter_context(nc.psum_tensor(tag + name, shape, F32))

        stats = buf("stats", [P, TILES, 6])
        mv = buf("mv", [P, TILES, 2])
        rstd = buf("rstd", [P, TILES])
        xn = buf("xn", [P, 2, GROUP, C])
        xT = buf("xT", [P, 2, GN])
        hT = buf("hT", [P, 2, GN])
        ps_t = psum("ps_t", [P, 2, GN])
        ps_s2 = psum("ps_s2", [P, 2, GN])
        ps_s1 = psum("ps_s1", [P, 2, GN])
        ps_hT = psum("ps_hT", [P, GN])
        ps_h = psum("ps_h", [P, GN])
        chain = sem("chain")
        var_ready = sem("var_ready")
        eps_added = sem("eps_added")
        rstd_ready = sem("rstd_ready")
        xn_ready = sem("xn_ready")
        turned = sem("turned")
        xT_ready = sem("xT_ready")
        hT_made = sem("hT_made")
        h_made = sem("h_made")
        hT_ready = sem("hT_ready")
        h_ready = sem("h_ready")
        s_made = sem("s_made")
        s_kept = sem("s_kept")
        block = ctx.enter_context(nc.Block())

        def tile(g, k):
            return x_sb[:, bass.ds(g * GROUP + k, 1), :].rearrange("p a c -> p (a c)")

        def flat(a, g, k):
            return a[:, bass.ds(g * GROUP + k, 1), :].rearrange("p a c -> p (a c)")

        def groups(eng, step):
            step(0, 0)
            step(1, 1)
            with eng.Fori(1, GROUPS // 2 - 2) as j:
                step(2 * j, 0)
                step(2 * j + 1, 1)
            for g in range(GROUPS - 4, GROUPS):
                step(g, g % 2)

        @block.vector
        def _(dve):
            def statistics(g):
                if x_landed and isinstance(g, int) and g in x_landed:
                    wait_apart(dve, x_landed[g], 16, passed[0])
                for k in range(GROUP):
                    last = nc.vector.bn_stats(flat(stats, g, k), tile(g, k))
                last.then_inc(chain, 1)
                wait_apart(dve, chain, 2 * g + 1, passed[0])
                for k in range(GROUP):
                    last = nc.vector.bn_aggr(flat(mv, g, k), flat(stats, g, k))
                last.then_inc(chain, 1)
                dve.wait_ge(chain, 2 * g + 2)
                nc.vector.tensor_copy(rstd[:, bass.ds(g * GROUP, GROUP)], mv[:, bass.ds(g * GROUP, GROUP), 1]).then_inc(var_ready, 1)

            def scale(g, b):
                dve.wait_ge(rstd_ready, g + 1)
                wait(dve, turned, g - 1)
                if w is None:
                    wait(dve, h_ready, g - 1)
                for k in range(GROUP):
                    last = nc.vector.tensor_scalar(xn[:, b, k, :], tile(g, k), flat(mv, g, k)[:, 0:1],
                                                   rstd[:, bass.ds(g * GROUP + k, 1)], ALU.subtract, ALU.mult)
                last.then_inc(xn_ready, 1)

            def step(g, b):
                if not (isinstance(g, int) and g == GROUPS - 1):
                    scale(g + 1, 1 - b)
                if not (isinstance(g, int) and g >= GROUPS - 3):
                    statistics(g + 3)
                if isinstance(g, int) and g == GROUPS - 1:
                    dve.wait_ge(s_kept, GROUPS // 2)
                    terms.make(dve, 0, 0)

            statistics(0)
            statistics(1)
            scale(0, 0)
            statistics(2)
            groups(dve, step)

        @block.gpsimd
        def _(pool):
            def step(g, b):
                scales = rstd[:, bass.ds(g * GROUP, GROUP)]
                wait_apart(pool, var_ready, g + 1, passed[1])
                nc.gpsimd.tensor_scalar(scales, scales, EPS, None, ALU.add).then_inc(eps_added, 1)
                pool.wait_ge(eps_added, g + 1)
                nc.gpsimd.tensor_tensor(scales, scales, power[:, 0:GROUP], ALU.pow).then_inc(rstd_ready, 1)

            groups(pool, step)
            for q in range(2):
                adjacency.make_mask(pool, 0, 0, 0, q)

        @block.sync
        def _(sp):
            adjacency.load(sp, 0, 0)
            adjacency.load(sp, 1, 1)

        @block.scalar
        def _(act):
            def take_xT(g, b):
                act.wait_ge(turned, g + 1)
                wait(act, s_made, g - 1)
                nc.scalar.copy(xT[:, b, :], ps_t[:, b, :]).then_inc(xT_ready, 1)

            def keep(g, b):
                act.wait_ge(s_made, g + 1)
                nc.scalar.copy(s1[:, bass.ds(g * GROUP, GROUP)], ps_s1[:, b, 0:GROUP])
                nc.scalar.activation(terms.neg_s1[:, bass.ds(g * GROUP, GROUP)], ps_s1[:, b, 0:GROUP], ACT.Copy, scale=-1.0)
                nc.scalar.copy(s2b[:, bass.ds(g * GN, GN)], ps_s2[:, b, :]).then_inc(s_kept, 1)

            def step(g, b):
                rows = hrow[:, bass.ds(g * GROUP, GROUP), :]
                if w is None:
                    act.wait_ge(xn_ready, g + 1)
                    nc.scalar.copy(rows, xn[:, b, :, :]).then_inc(h_ready, 1)
                if not (isinstance(g, int) and g == GROUPS - 1):
                    take_xT(g + 1, 1 - b)
                if w is not None:
                    act.wait_ge(hT_made, g + 1)
                    wait(act, s_made, g - 1)
                    nc.scalar.copy(hT[:, b, :], ps_hT[:, :]).then_inc(hT_ready, 1)
                    act.wait_ge(h_made, g + 1)
                    nc.scalar.copy(rows, ps_h[:, :].rearrange("p (k c) -> p k c", k=GROUP)).then_inc(h_ready, 1)
                if not (isinstance(g, int) and g == 0):
                    keep(g - 1, 1 - b)

            take_xT(0, 0)
            groups(act, step)
            keep(GROUPS - 1, 1)

        @block.tensor
        def _(pe):
            def turn(g, b):
                pe.wait_ge(xn_ready, g + 1)
                wait(pe, xT_ready, g - 1)
                for k in range(GROUP):
                    last = nc.tensor.transpose(ps_t[:, b, k * P:(k + 1) * P], xn[:, b, k, :], ident[:, :])
                last.then_inc(turned, 1)

            def step(g, b):
                if not (isinstance(g, int) and g == GROUPS - 1):
                    turn(g + 1, 1 - b)
                pe.wait_ge(xT_ready, g + 1)
                src = xT
                if w is not None:
                    wait(pe, hT_ready, g)
                    nc.tensor.matmul(ps_hT[:, :], w[:, :], xT[:, b, :], start=True, stop=True).then_inc(hT_made, 1)
                    wait(pe, h_ready, g)
                    for k in range(GROUP):
                        last = nc.tensor.matmul(ps_h[:, k * C:(k + 1) * C], xT[:, b, k * P:(k + 1) * P], w[:, :],
                                                start=True, stop=True)
                    last.then_inc(h_made, 1)
                    pe.wait_ge(hT_ready, g + 1)
                    src = hT
                wait(pe, s_kept, g - 1)
                nc.tensor.matmul(ps_s2[:, b, :], a_rep[:, :], src[:, b, :], start=True, stop=True)
                for k in range(GROUP):
                    last = nc.tensor.matmul(ps_s1[:, b, k:k + 1], src[:, b, k * P:(k + 1) * P], a1[:, 0:1],
                                            start=True, stop=True)
                last.then_inc(s_made, 1)

            turn(0, 0)
            groups(pe, step)


def attend(nc, tag, passed, adjacency, terms, norm, ahead, ahead_landed, x_sb, ident, hrow, s1, slope, elu):
    with ExitStack() as ctx:
        def sem(name):
            return ctx.enter_context(nc.semaphore(tag + name))

        def buf(name, shape, dt=F32):
            return ctx.enter_context(nc.sbuf_tensor(tag + name, shape, dt))

        t, r = terms.t, terms.r
        p = buf("p", [P, 4, HALF])
        pT = buf("pT", [P, 8, GN])
        oT = buf("oT", [P, 2, P])
        m_col = buf("m_col", [P, 2])
        bias = buf("bias", [P, 2])
        half_sum = buf("half_sum", [P, 2 * TILES])
        row_sum = buf("row_sum", [P, 1])
        inv_sum = buf("inv_sum", [P, 2])
        y = buf("y", [P, 2, C])
        y_neg = buf("y_neg", [P, 2, C])
        y_exp = buf("y_exp", [P, 2, C])
        z = buf("z", [P, 2, C])
        ps_pT = [ctx.enter_context(nc.psum_tensor(f"{tag}ps_pT{m}", [P, GN], F32)) for m in range(4)]
        ps_o = [ctx.enter_context(nc.psum_tensor(f"{tag}ps_o{m}", [P, GN], F32)) for m in range(2)]
        ps_row = [ctx.enter_context(nc.psum_tensor(f"{tag}ps_row{m}", [P, GN], F32)) for m in range(2)]

        w_dve = sem("w_dve")
        bias_chain = sem("bias_chain")
        sum_chain = sem("sum_chain")
        inv_ready = sem("inv_ready")
        elu_chain = sem("elu_chain")
        bias_ready = sem("bias_ready")
        p_ready = sem("p_ready")
        turned = sem("turned")
        moved = sem("moved")
        block_used = sem("block_used")
        oT_ready = sem("oT_ready")
        o_row = sem("o_row")
        o_taken = sem("o_taken")
        y_chain = sem("y_chain")
        y_exped = sem("y_exped")
        block = ctx.enter_context(nc.Block())

        @block.sync
        def _(sp):
            for view, dram in ahead:
                sp.dma_start(view, dram).then_inc(ahead_landed, 16)
            with sp.Fori(0, TILES // 2 - 1) as j:
                adjacency.load(sp, 2 * j + 2, 0)
                adjacency.load(sp, 2 * j + 3, 1)

        def slot_free(eng, h):
            wait(eng, turned, 4 * h - 12)

        @block.gpsimd
        def _(pool):
            def add(i, parity, q):
                h = 2 * i + q
                pool.wait_ge(terms.r_ready, h + 1)
                slot_free(pool, h)
                nc.gpsimd.tensor_tensor(p[:, 2 * parity + q, 0:POOL_ADDS], t[:, q, 0:POOL_ADDS], r[:, q, 0:POOL_ADDS],
                                        ALU.add).then_inc(terms.w_pool, 1)

            def step(i, pair, parity):
                for q in range(2):
                    add(i - 1, 1 - parity, q)
                    adjacency.make_mask(pool, i, pair, parity, q)

            step(1, 0, 1)
            step(2, 1, 0)
            with pool.Fori(1, TILES // 2 - 1) as j:
                step(2 * j + 1, j, 1)
                step(2 * j + 2, j + 1, 0)
            step(TILES - 1, TILES // 2 - 1, 1)
            add(TILES - 1, 1, 0)
            add(TILES - 1, 1, 1)
            norm.root(pool, 0)

        @block.scalar
        def _(act):
            def exponential(i, parity, q):
                h = 2 * i + q
                act.wait_ge(bias_ready, i + 1)
                act.wait_ge(terms.w_pool, h + 1)
                act.wait_ge(w_dve, h + 1)
                slot = p[:, 2 * parity + q, :]
                nc.scalar.activation(slot, slot, ACT.Exp, bias=bias[:, parity:parity + 1], scale=slope,
                                     accum_out=half_sum[:, bass.ds(h, 1)]).then_inc(p_ready, 1)

            def moves(i, q):
                for m in range(4):
                    act.wait_ge(turned, 8 * i + 4 * q + m + 1)
                    wait(act, block_used, 8 * i - 8 + 4 * q + m + 1)
                    nc.scalar.copy(pT[:, 4 * q + m, :], ps_pT[m][:, :]).then_inc(moved, 1)

            def take_oT(i, parity):
                act.wait_ge(block_used, 8 * i + 8)
                wait(act, o_row, i - 1)
                nc.scalar.copy(oT[:, parity, :], ps_o[parity][:, 0:P]).then_inc(oT_ready, 1)

            def y_exponential(i, parity):
                y_i, y_neg_i = y[:, parity, :], y_neg[:, parity, :]
                act.wait_ge(inv_ready, i + 1)
                act.wait_ge(o_row, i + 1)
                wait(act, elu_chain, i - 1)
                nc.scalar.activation(y_i, ps_row[parity][:, 0:C], ACT.Copy, scale=inv_sum[:, parity:parity + 1]).then_inc(o_taken, 1)
                act.wait_ge(o_taken, i + 1)
                nc.scalar.activation(y_neg_i, y_i, ACT.Relu, scale=-1.0).then_inc(y_chain, 1)
                act.wait_ge(y_chain, i + 1)
                nc.scalar.activation(y_exp[:, parity, :], y_neg_i, ACT.Exp, scale=-1.0).then_inc(y_exped, 1)

            def step(i, parity, before=1):
                exponential(i, parity, 0)
                if before >= 1:
                    moves(i - 1, 1)
                exponential(i, parity, 1)
                moves(i, 0)
                if before >= 1:
                    take_oT(i - 1, 1 - parity)
                if elu and before >= 3:
                    y_exponential(i - 3, 1 - parity)

            for i in range(6):
                step(i, i % 2, before=i)
            with act.Fori(3, TILES // 2) as j:
                step(2 * j, 0, before=3)
                step(2 * j + 1, 1, before=3)
            moves(TILES - 1, 1)
            take_oT(TILES - 1, 1)
            if elu:
                for i in range(TILES - 3, TILES):
                    y_exponential(i, i % 2)

        @block.vector
        def _(dve):
            def logits(i, parity, q):
                h = 2 * i + q
                if not (isinstance(i, int) and i == 0 and q == 0):
                    terms.make(dve, i, q)
                if q == 1:
                    link = Chain(dve, bias_chain, 2 * i)
                    one = s1[:, bass.ds(i, 1)]
                    dve.wait_ge(terms.max_ready, i + 1)
                    link(nc.vector.tensor_tensor(m_col[:, 0:1], terms.t_max[:, :], one, ALU.add))
                    link(nc.vector.scalar_tensor_tensor(m_col[:, 1:2], m_col[:, 0:1], slope, m_col[:, 0:1], ALU.mult, ALU.max))
                    wait(dve, p_ready, 2 * i - 2)
                    nc.vector.tensor_tensor(bias[:, parity:parity + 1], one, m_col[:, 1:2], ALU.subtract).then_inc(bias_ready, 1)
                dve.wait_ge(terms.r_ready, h + 1)
                slot_free(dve, h)
                nc.vector.tensor_tensor(p[:, 2 * parity + q, POOL_ADDS:HALF], t[:, q, POOL_ADDS:HALF], r[:, q, POOL_ADDS:HALF],
                                        ALU.add).then_inc(w_dve, 1)

            def inverse(i, parity):
                dve.wait_ge(p_ready, 2 * i + 2)
                if elu:
                    wait(dve, o_taken, i - 1)
                nc.vector.tensor_tensor(row_sum[:, :], half_sum[:, bass.ds(2 * i, 1)], half_sum[:, bass.ds(2 * i + 1, 1)],
                                        ALU.add).then_inc(sum_chain, 1)
                dve.wait_ge(sum_chain, i + 1)
                nc.vector.reciprocal(inv_sum[:, parity:parity + 1], row_sum[:, :]).then_inc(inv_ready, 1)

            def finish(i, parity):
                row = x_sb[:, bass.ds(i, 1), :].rearrange("p a c -> p (a c)")
                dve.wait_ge(inv_ready, i + 1)
                dve.wait_ge(o_row, i + 1)
                nc.vector.scalar_tensor_tensor(row, ps_row[parity][:, 0:C], inv_sum[:, parity:parity + 1], row, ALU.mult,
                                               ALU.add).then_inc(o_taken, 1)

            def elu_value(i, parity):
                dve.wait_ge(y_exped, i + 1)
                nc.vector.scalar_tensor_tensor(z[:, parity, :], y_exp[:, parity, :], -1.0, y[:, parity, :],
                                               ALU.add, ALU.max).then_inc(elu_chain, 1)

            def finish_elu(i, parity):
                row = x_sb[:, bass.ds(i, 1), :].rearrange("p a c -> p (a c)")
                dve.wait_ge(elu_chain, i + 1)
                nc.vector.tensor_tensor(row, z[:, parity, :], row, ALU.add)

            def step(i, parity, before=5):
                if before >= 3:
                    inverse(i - 3, 1 - parity)
                if elu and before >= 5:
                    elu_value(i - 5, 1 - parity)
                logits(i, parity, 0)
                if before >= 3 and not elu:
                    finish(i - 3, 1 - parity)
                if elu and before >= 5:
                    finish_elu(i - 5, 1 - parity)
                logits(i, parity, 1)

            for i in range(6):
                step(i, i % 2, before=i)
            with dve.Fori(3, TILES // 2) as j:
                step(2 * j, 0)
                step(2 * j + 1, 1)
            norm.statistics(dve, 0)
            for i in range(TILES - 3, TILES):
                if i == TILES - 2:
                    norm.scale(dve, 0)
                inverse(i, i % 2)
                if elu:
                    elu_value(i - 2, i % 2)
                    finish_elu(i - 2, i % 2)
                else:
                    finish(i, i % 2)
            if elu:
                for i in (TILES - 2, TILES - 1):
                    elu_value(i, i % 2)
                    finish_elu(i, i % 2)

        @block.tensor
        def _(pe):
            def turn(i, parity, q):
                h = 2 * i + q
                pe.wait_ge(p_ready, h + 1)
                for m in range(4):
                    wait(pe, moved, 4 * h - 4 + m + 1)
                    for k in range(4):
                        keys = (4 * m + k) * P
                        last = nc.tensor.transpose(ps_pT[m][:, k * P:(k + 1) * P], p[:, 2 * parity + q, keys:keys + P],
                                                   ident[:, :])
                    last.then_inc(turned, 1)

            def multiply(i, parity, q):
                h = 2 * i + q
                if q == 0:
                    wait(pe, oT_ready, i - 1)
                for m in range(4):
                    pe.wait_ge(moved, 4 * h + m + 1)
                    for k in range(4):
                        keys = 16 * q + 4 * m + k
                        last = nc.tensor.matmul(ps_o[parity][:, 0:P], hrow[:, keys, :], pT[:, 4 * q + m, k * P:(k + 1) * P],
                                                start=(keys == 0), stop=(keys == TILES - 1))
                    last.then_inc(block_used, 1)

            def back_to_rows(i, parity):
                pe.wait_ge(oT_ready, i + 1)
                wait(pe, o_taken, i - 1)
                nc.tensor.transpose(ps_row[parity][:, 0:C], oT[:, parity, :], ident[:, :]).then_inc(o_row, 1)

            def step(i, parity, first=False):
                turn(i, parity, 0)
                if not first:
                    multiply(i - 1, 1 - parity, 1)
                turn(i, parity, 1)
                multiply(i, parity, 0)
                if not first:
                    back_to_rows(i - 1, 1 - parity)

            for i in range(4):
                step(i, i % 2, first=(i == 0))
            with pe.Fori(2, TILES // 2) as j:
                step(2 * j, 0)
                step(2 * j + 1, 1)
            multiply(TILES - 1, 1, 1)
            back_to_rows(TILES - 1, 1)


def every(a):
    return a[(slice(None),) * len(a.shape)]


def three_passes(nc, out, a_hi, a_lo, b_hi, b_lo, start=True, stop=True):
    nc.tensor.matmul(out, a_hi, b_hi, start=start, stop=False)
    nc.tensor.matmul(out, a_hi, b_lo, start=False, stop=False)
    return nc.tensor.matmul(out, a_lo, b_hi, start=False, stop=stop)


class Split:

    def __init__(self, nc, sem, operands, on_pool=()):
        self.nc, self.operands, self.on_pool = nc, operands, on_pool
        self.hi_ready, self.lo_dve, self.lo_pool = sem("split_hi_ready"), sem("split_lo_dve"), sem("split_lo_pool")

    def hi(self, act, n):
        stage, hi, lo, landed, count = self.operands[n]
        act.wait_ge(landed, count)
        self.nc.scalar.copy(every(hi), every(stage)).then_inc(self.hi_ready, 1)

    def low_count(self, n):
        return sum(self.operands[k][2] is not None and (k in self.on_pool) == (n in self.on_pool) for k in range(n + 1))

    def lo(self, eng, n):
        stage, hi, lo, landed, count = self.operands[n]
        on_pool = n in self.on_pool
        maker, done = (self.nc.gpsimd, self.lo_pool) if on_pool else (self.nc.vector, self.lo_dve)
        eng.wait_ge(landed, count)
        eng.wait_ge(self.hi_ready, n + 1)
        maker.tensor_tensor(every(lo), every(stage), every(hi).bitcast(F32), ALU.subtract).then_inc(done, 1)

    def wait_for(self, pe, n):
        pe.wait_ge(self.hi_ready, n + 1)
        if self.operands[n][2] is not None:
            pe.wait_ge(self.lo_pool if n in self.on_pool else self.lo_dve, self.low_count(n))


class Normaliser:

    def __init__(self, nc, ctx, tag, passed, x_sb, power, ident):
        def buf(name, shape):
            return ctx.enter_context(nc.sbuf_tensor(tag + name, shape, F32))

        def sem(name):
            return ctx.enter_context(nc.semaphore(tag + name))

        self.nc, self.x, self.power, self.ident = nc, x_sb, power, ident
        self.stats = buf("stats", [P, GROUP, 6])
        self.mv = buf("mv", [P, GROUP, 2])
        self.rstd = buf("rstd", [P, GROUP])
        self.xn = buf("xn", [P, GROUP, C])
        self.chain = sem("norm_chain")
        self.var_ready = sem("var_ready")
        self.eps_added = sem("eps_added")
        self.rstd_ready = sem("rstd_ready")
        self.xn_ready = sem("xn_ready")
        self.turned = sem("xn_turned")
        self.xT_hi_ready = sem("xT_hi_ready")
        self.xT_lo_ready = sem("xT_lo_ready")
        self.passed = passed

    def place(self, buf, ps):
        self.ps = ps
        self.xT_hi = buf("xT_hi", [P, 2, GN], F32R)
        self.xT_lo = buf("xT_lo", [P, 2, GN], F32R)

    def tile(self, g, k):
        return self.x[:, bass.ds(g * GROUP + k, 1), :].rearrange("p a c -> p (a c)")

    def statistics(self, dve, g):
        for k in range(GROUP):
            last = self.nc.vector.bn_stats(self.stats[:, k, :], self.tile(g, k))
        last.then_inc(self.chain, 1)
        wait_apart(dve, self.chain, 2 * g + 1, self.passed[0])
        for k in range(GROUP):
            last = self.nc.vector.bn_aggr(self.mv[:, k, :], self.stats[:, k, :])
        last.then_inc(self.chain, 1)
        dve.wait_ge(self.chain, 2 * g + 2)
        self.nc.vector.tensor_copy(self.rstd[:, :], self.mv[:, :, 1]).then_inc(self.var_ready, 1)

    def root(self, pool, g):
        wait_apart(pool, self.var_ready, g + 1, self.passed[1])
        self.nc.gpsimd.tensor_scalar(self.rstd[:, :], self.rstd[:, :], EPS, None, ALU.add).then_inc(self.eps_added, 1)
        pool.wait_ge(self.eps_added, g + 1)
        self.nc.gpsimd.tensor_tensor(self.rstd[:, :], self.rstd[:, :], self.power[:, 0:GROUP], ALU.pow).then_inc(self.rstd_ready, 1)

    def scale(self, dve, g):
        dve.wait_ge(self.rstd_ready, g + 1)
        wait(dve, self.turned, g)
        for k in range(GROUP):
            last = self.nc.vector.tensor_scalar(self.xn[:, k, :], self.tile(g, k), self.mv[:, k, 0:1],
                                                self.rstd[:, k:k + 1], ALU.subtract, ALU.mult)
        last.then_inc(self.xn_ready, 1)

    def turn(self, pe, g, ps=None):
        ps = ps or self.ps
        pe.wait_ge(self.xn_ready, g + 1)
        for k in range(GROUP):
            last = self.nc.tensor.transpose(ps[:, k * P:(k + 1) * P], self.xn[:, k, :], self.ident[:, :])
        last.then_inc(self.turned, 1)

    def take_hi(self, act, g, b, ps=None):
        ps = ps or self.ps
        act.wait_ge(self.turned, g + 1)
        self.nc.scalar.copy(self.xT_hi[:, b, :], ps[:, :]).then_inc(self.xT_hi_ready, 1)

    def take_lo(self, dve, g, b, ps=None):
        ps = ps or self.ps
        dve.wait_ge(self.xT_hi_ready, g + 1)
        self.nc.vector.tensor_tensor(self.xT_lo[:, b, :], ps[:, :], self.xT_hi[:, b, :].bitcast(F32),
                                     ALU.subtract).then_inc(self.xT_lo_ready, 1)


class Gates:

    def __init__(self, nc, buf, sem, ident, rank, ps_misc, top, bias=None):
        self.nc, self.ident, self.rank, self.ps = nc, ident, rank, ps_misc
        self.top, self.bias = top, bias
        wide = [P, GROUP, E8]
        self.logits, self.e, self.probs = buf("logits", wide), buf("expo", wide), buf("probs", wide)
        self.eq, self.oh, self.rest = buf("eq", wide), buf("one_hot", wide), buf("rest", wide)
        self.oh2, self.gate = buf("one_hot2", wide), buf("gate", [P, 2, GROUP, E8])
        self.m, self.s, self.inv = buf("gmax", [P, GROUP]), buf("gsum", [P, GROUP]), buf("ginv", [P, GROUP])
        self.p1, self.p2, self.km = buf("p1", [P, GROUP]), buf("p2", [P, GROUP]), buf("kmax", [P, GROUP])
        self.logits_T = buf("logits_T", [P, GN])
        self.parts = buf("gate_parts", [P, GROUP, P], F32R)
        self.gT = buf("gate_T", [2 * E8, 2, GN], F32R)
        self.chain = sem("gate_chain")
        self.zeroed = sem("gate_parts_zeroed")
        self.logits_made = sem("logits_made")
        self.logits_taken = sem("logits_taken")
        self.logits_turned = sem("logits_turned")
        self.shifted = sem("shifted")
        self.exped = sem("gate_exped")
        self.parts_ready = sem("gate_parts_ready")
        self.turned = sem("gate_turned")
        self.gT_ready = sem("gate_T_ready")
        stages = [("shift", 1 if bias is None else 2), ("probabilities", 3), ("first", 5), ("second", 0 if top == 1 else 6),
                  ("weigh", 1 if top == 1 else 3), ("part", 1)]
        self.links = dict(stages)
        self.before = {name: sum(n for _, n in stages[:k]) for k, (name, _) in enumerate(stages)}
        self.total = sum(n for _, n in stages)

    def begin(self, dve, g, stage):
        return Chain(dve, self.chain, self.total * g + self.before[stage])

    def over(self, a):
        return a[:, :].unsqueeze(2).to_broadcast([P, GROUP, E8])

    def zero(self, dve):
        self.nc.vector.memset(self.parts[:, :, :].bitcast(F32), 0.0).then_inc(self.zeroed, 1)
        dve.wait_ge(self.zeroed, 1)

    def take_logits(self, act, g):
        act.wait_ge(self.logits_made, g + 1)
        self.nc.scalar.copy(self.logits_T[:, :], self.ps[:, :]).then_inc(self.logits_taken, 1)

    def turn_logits(self, pe, g):
        pe.wait_ge(self.logits_taken, g + 1)
        for k in range(GROUP):
            last = self.nc.tensor.transpose(self.ps[:, k * P:(k + 1) * P], self.logits_T[:, k * P:(k + 1) * P],
                                            self.ident[:, :])
        last.then_inc(self.logits_turned, 1)

    def shift(self, dve, g):
        link = self.begin(dve, g, "shift")
        v = self.nc.vector
        dve.wait_ge(self.logits_turned, g + 1)
        view = self.ps[:, :].rearrange("p (k c) -> p k c", k=GROUP)[:, :, 0:E8]
        if self.bias is not None:
            link(v.tensor_tensor(self.logits[:, :, :], view, self.bias[:, :, :], ALU.add))
            view = self.logits[:, :, :]
        link(v.tensor_reduce(self.m[:, :], view, AX.X, ALU.max))
        v.tensor_tensor(self.logits[:, :, :], view, self.over(self.m), ALU.subtract).then_inc(self.shifted, 1)
        assert link.n == self.links["shift"]

    def exponential(self, act, g):
        act.wait_ge(self.shifted, g + 1)
        self.nc.scalar.activation(self.e[:, :, :], self.logits[:, :, :], ACT.Exp).then_inc(self.exped, 1)

    def probabilities(self, dve, g):
        link = self.begin(dve, g, "probabilities")
        v = self.nc.vector
        dve.wait_ge(self.exped, g + 1)
        link(v.tensor_reduce(self.s[:, :], self.e[:, :, :], AX.X, ALU.add))
        link(v.reciprocal(self.inv[:, :], self.s[:, :]))
        link(v.tensor_tensor(self.probs[:, :, :], self.e[:, :, :], self.over(self.inv), ALU.mult))
        assert link.n == self.links["probabilities"]

    def first_largest(self, link, src, p, oh):
        v = self.nc.vector
        link(v.tensor_reduce(p[:, :], src[:, :, :], AX.X, ALU.max))
        link(v.tensor_tensor(self.eq[:, :, :], src[:, :, :], self.over(p), ALU.is_equal))
        link(v.tensor_tensor(self.eq[:, :, :], self.eq[:, :, :], self.rank[:, :, :], ALU.mult))
        link(v.tensor_reduce(self.km[:, :], self.eq[:, :, :], AX.X, ALU.max))
        link(v.tensor_tensor(oh[:, :, :], self.eq[:, :, :], self.over(self.km), ALU.is_equal))

    def first(self, dve, g):
        link = self.begin(dve, g, "first")
        self.first_largest(link, self.probs, self.p1, self.oh)
        assert link.n == self.links["first"]

    def second(self, dve, g):
        link = self.begin(dve, g, "second")
        link(self.nc.vector.scalar_tensor_tensor(self.rest[:, :, :], self.oh[:, :, :], -2.0, self.probs[:, :, :], ALU.mult, ALU.add))
        self.first_largest(link, self.rest, self.p2, self.oh2)
        assert link.n == self.links["second"]

    def weigh(self, dve, g, b):
        link = self.begin(dve, g, "weigh")
        v = self.nc.vector
        gate = self.gate[:, b, :, :]
        if self.top == 1:
            link(v.tensor_tensor(gate, self.oh[:, :, :], self.probs[:, :, :], ALU.mult))
        else:
            v.tensor_tensor(self.oh[:, :, :], self.oh[:, :, :], self.oh2[:, :, :], ALU.add)
            link(v.scalar_tensor_tensor(self.s[:, :], self.p1[:, :], 1e-9, self.p2[:, :], ALU.add, ALU.add))
            v.tensor_tensor(self.probs[:, :, :], self.oh[:, :, :], self.probs[:, :, :], ALU.mult)
            link(v.reciprocal(self.inv[:, :], self.s[:, :]))
            link(v.tensor_tensor(gate, self.probs[:, :, :], self.over(self.inv), ALU.mult))
        assert link.n == self.links["weigh"]

    def part(self, dve, g, b):
        link = self.begin(dve, g, "part")
        v = self.nc.vector
        gate = self.gate[:, b, :, :]
        wait(dve, self.turned, g)
        link(v.tensor_copy(self.parts[:, :, 0:E8], gate))
        v.tensor_tensor(self.parts[:, :, E8:2 * E8], gate, self.parts[:, :, 0:E8].bitcast(F32),
                        ALU.subtract).then_inc(self.parts_ready, 1)
        assert link.n == self.links["part"]

    def choose(self, dve, g, b):
        self.probabilities(dve, g)
        self.first(dve, g)
        if self.top == 2:
            self.second(dve, g)
        self.weigh(dve, g, b)
        self.part(dve, g, b)

    def turn(self, pe, g):
        pe.wait_ge(self.parts_ready, g + 1)
        for k in range(GROUP):
            last = self.nc.tensor.transpose(self.ps[:, k * P:(k + 1) * P], self.parts[:, k, :].bitcast(F32),
                                            self.ident[:, :])
        last.then_inc(self.turned, 1)

    def take(self, dve, g, b):
        dve.wait_ge(self.turned, g + 1)
        self.nc.vector.tensor_copy(self.gT[:, b, :], self.ps[0:2 * E8, :]).then_inc(self.gT_ready, 1)


def mix_silu(nc, norm, ins, ahead, ahead_landed, x_sb, ident, out):
    with ExitStack() as ctx:
        def sem(name):
            return ctx.enter_context(nc.semaphore("mix0_" + name))

        def buf(name, shape, dt=F32):
            return ctx.enter_context(nc.sbuf_tensor("mix0_" + name, shape, dt))

        def psum(name):
            return ctx.enter_context(nc.psum_tensor("mix0_" + name, [P, GN], F32))

        wr, w1, w3, w2 = ([buf(name + part, shape, F32R) for part in ("_hi", "_lo")] for name, shape in
                          (("wr", [P, P]), ("w1", [P, PAD0]), ("w3", [P, PAD0]), ("w2", [P, CH0, C])))
        owner = buf("owner", [2 * E8, PAD0], F32R)
        w2_stage, owner_stage = buf("w2_stage", [P, CH0, C]), buf("owner_stage", [2 * E8, PAD0])
        rank = buf("rank", [P, GROUP, E8])
        owner_landed, w2_landed = sem("owner_landed"), sem("w2_landed")
        split = Split(nc, sem, [(ahead[0], *wr, ahead_landed, 48), (ahead[1], *w1, ahead_landed, 48),
                                (ahead[2], *w3, ahead_landed, 48), (w2_stage, *w2, w2_landed, 16),
                                (owner_stage, owner, None, owner_landed, 16)], on_pool=(2, 3))
        WR, W1, W3, W2, OWNER = range(5)
        s = buf("s", [P, 2, GN])
        a = buf("a", [P, 2, GN])
        ag = buf("ag", [P, 2, GN])
        ag_hi = buf("ag_hi", [P, 4, GN], F32R)
        ag_lo = buf("ag_lo", [P, 4, GN], F32R)
        yT = buf("yT", [P, GN])
        ps_h1 = [psum(f"h1_{i}") for i in range(2)]
        ps_h3 = [psum(f"h3_{i}") for i in range(2)]
        ps_g = [psum(f"g_{i}") for i in range(2)]
        ps_y, ps_misc = psum("y"), psum("misc")
        norm.place(buf, ps_misc)
        gates = Gates(nc, buf, sem, ident, rank, ps_misc, top=2)
        rank_landed = sem("rank_landed")
        h1_made = sem("h1_made")
        h3_made = sem("h3_made")
        silu_done = sem("silu_done")
        a_done = sem("a_done")
        ag_done = sem("ag_done")
        hi_done = sem("hi_done")
        lo_done = sem("lo_done")
        y_added = sem("y_added")
        yT_ready = sem("yT_ready")
        y_turned = sem("y_turned")
        y_taken = sem("y_taken")
        block = ctx.enter_context(nc.Block())

        def groups(eng, step):
            step(0, 0, True, False)
            step(1, 1, False, False)
            with eng.Fori(1, GROUPS // 2 - 1) as j:
                step(2 * j, 0, False, False)
                step(2 * j + 1, 1, False, False)
            step(GROUPS - 2, 0, False, False)
            step(GROUPS - 1, 1, False, True)

        @block.sync
        def _(sp):
            sp.dma_start(every(owner_stage), ins["owner"]).then_inc(owner_landed, 16)
            sp.dma_start(every(w2_stage), ins["L0_ffn_w2"].rearrange("(h p) c -> p h c", p=P)).then_inc(w2_landed, 16)
            sp.dma_start(rank[:, :, :], ins["rank"]).then_inc(rank_landed, 16)

        @block.tensor
        def _(pe):
            def logits(g, b):
                pe.wait_ge(norm.xT_lo_ready, g + 1)
                three_passes(nc, ps_misc[:, :], wr[0][:, :], wr[1][:, :], norm.xT_hi[:, b, :],
                             norm.xT_lo[:, b, :]).then_inc(gates.logits_made, 1)

            def hidden(g, b, c):
                n, i = CH0 * g + c, c % 2
                units = slice(c * P, (c + 1) * P)
                if c == 0:
                    pe.wait_ge(norm.xT_lo_ready, g + 1)
                    if isinstance(g, int) and g == 0:
                        split.wait_for(pe, W1)
                        split.wait_for(pe, W3)
                wait(pe, silu_done, n - 1)
                three_passes(nc, ps_h1[i][:, :], w1[0][:, units], w1[1][:, units],
                             norm.xT_hi[:, b, :], norm.xT_lo[:, b, :]).then_inc(h1_made, 1)
                wait(pe, ag_done, n - 1)
                three_passes(nc, ps_h3[i][:, :], w3[0][:, units], w3[1][:, units],
                             norm.xT_hi[:, b, :], norm.xT_lo[:, b, :])

            def spread(g, b, c):
                if c == 0:
                    pe.wait_ge(gates.gT_ready, g + 1)
                    if isinstance(g, int) and g == 0:
                        split.wait_for(pe, OWNER)
                nc.tensor.matmul(ps_g[c % 2][:, :], owner[:, c * P:(c + 1) * P], gates.gT[:, b, :], start=True,
                                 stop=True).then_inc(h3_made, 1)

            def add(g, b, c):
                n, i = CH0 * g + c, (CH0 * b + c) % 4
                pe.wait_ge(hi_done, n + 1)
                pe.wait_ge(lo_done, n + 1)
                if c == 0:
                    wait(pe, yT_ready, g)
                    if isinstance(g, int) and g == 0:
                        split.wait_for(pe, W2)
                three_passes(nc, ps_y[:, :], w2[0][:, c, :], w2[1][:, c, :], ag_hi[:, i, :], ag_lo[:, i, :],
                             start=(c == 0), stop=(c == CH0 - 1)).then_inc(y_added, 1)

            def y_to_rows(g):
                pe.wait_ge(yT_ready, g + 1)
                for k in range(GROUP):
                    last = nc.tensor.transpose(ps_misc[:, k * P:(k + 1) * P], yT[:, k * P:(k + 1) * P], ident[:, :])
                last.then_inc(y_turned, 1)

            def step(g, b, first, last):
                for c in range(CH0):
                    if not first or c >= 2:
                        hidden(g, b, c)
                    spread(g, b, c)
                    if c >= LAG:
                        add(g, b, c - LAG)
                    elif not first:
                        add(g - 1, 1 - b, CH0 - LAG + c)
                    if c == 5 and not first:
                        y_to_rows(g - 1)
                    if last:
                        continue
                    if c == 8:
                        wait(pe, y_taken, g)
                        norm.turn(pe, g + 1)
                    if c == 11:
                        logits(g + 1, 1 - b)
                    if c == 13:
                        gates.turn_logits(pe, g + 1)
                    if c == 20:
                        gates.turn(pe, g + 1)

            norm.turn(pe, 0)
            split.wait_for(pe, WR)
            logits(0, 0)
            gates.turn_logits(pe, 0)
            hidden(0, 0, 0)
            hidden(0, 0, 1)
            gates.turn(pe, 0)
            groups(pe, step)
            for c in range(CH0 - LAG, CH0):
                add(GROUPS - 1, 1, c)
            y_to_rows(GROUPS - 1)

        @block.scalar
        def _(act):
            def split_hi(g, b, c):
                n = CH0 * g + c
                act.wait_ge(ag_done, n + 1)
                wait(act, y_added, n - 3)
                nc.scalar.copy(ag_hi[:, (CH0 * b + c) % 4, :], ag[:, c % 2, :]).then_inc(hi_done, 1)

            def step(g, b, first, last):
                for c in range(CH0):
                    n = CH0 * g + c
                    act.wait_ge(h1_made, n + 1)
                    wait(act, a_done, n - 1)
                    nc.scalar.activation(s[:, c % 2, :], ps_h1[c % 2][:, :], ACT.Silu).then_inc(silu_done, 1)
                    if c >= 1:
                        split_hi(g, b, c - 1)
                    elif not first:
                        split_hi(g - 1, 1 - b, CH0 - 1)
                    if last:
                        continue
                    if c == 9:
                        norm.take_hi(act, g + 1, 1 - b)
                    if c == 12:
                        gates.take_logits(act, g + 1)
                    if c == 15:
                        gates.exponential(act, g + 1)

            split.hi(act, WR)
            split.hi(act, W1)
            norm.take_hi(act, 0, 0)
            split.hi(act, W3)
            gates.take_logits(act, 0)
            gates.exponential(act, 0)
            split.hi(act, W2)
            split.hi(act, OWNER)
            groups(act, step)
            split_hi(GROUPS - 1, 1, CH0 - 1)

        @block.gpsimd
        def _(pool):
            def step(g, b, first, last):
                for c in range(CH0):
                    n, i = CH0 * g + c, (CH0 * b + c) % 4
                    pool.wait_ge(hi_done, n + 1)
                    wait(pool, y_added, n - 3)
                    nc.gpsimd.tensor_tensor(ag_lo[:, i, :], ag[:, c % 2, :], ag_hi[:, i, :].bitcast(F32),
                                            ALU.subtract).then_inc(lo_done, 1)
                    if c == 3 and not last:
                        norm.root(pool, g + 1)

            split.lo(pool, W3)
            split.lo(pool, W2)
            groups(pool, step)

        @block.vector
        def _(dve):
            def take_y(g):
                dve.wait_ge(y_added, CH0 * g + CH0)
                wait(dve, y_turned, g)
                nc.vector.tensor_copy(yT[:, :], ps_y[:, :]).then_inc(yT_ready, 1)

            def finish(g):
                group = x_sb[:, bass.ds(g * GROUP, GROUP), :]
                dve.wait_ge(y_turned, g + 1)
                nc.vector.tensor_tensor(group, ps_misc[:, :].rearrange("p (k c) -> p k c", k=GROUP), group,
                                        ALU.add).then_inc(y_taken, 1)

            def step(g, b, first, last):
                for c in range(CH0):
                    n, i = CH0 * g + c, c % 2
                    dve.wait_ge(silu_done, n + 1)
                    dve.wait_ge(h3_made, n + 1)
                    nc.vector.tensor_tensor(a[:, i, :], ps_h3[i][:, :], s[:, i, :], ALU.mult).then_inc(a_done, 1)
                    dve.wait_ge(a_done, n + 1)
                    wait(dve, lo_done, n - 1)
                    nc.vector.tensor_tensor(ag[:, i, :], ps_g[i][:, :], a[:, i, :], ALU.mult).then_inc(ag_done, 1)
                    if not first:
                        if c == 2:
                            take_y(g - 1)
                        if c == 6:
                            finish(g - 1)
                    if last:
                        continue
                    if c == 3:
                        norm.statistics(dve, g + 1)
                    if c == 5:
                        norm.scale(dve, g + 1)
                    if c == 10:
                        norm.take_lo(dve, g + 1, 1 - b)
                    if c == 13:
                        gates.shift(dve, g + 1)
                    if c == 15:
                        gates.probabilities(dve, g + 1)
                    if c == 16:
                        gates.first(dve, g + 1)
                    if c == 17:
                        gates.second(dve, g + 1)
                    if c == 18:
                        gates.weigh(dve, g + 1, 1 - b)
                        gates.part(dve, g + 1, 1 - b)
                    if c == 21:
                        gates.take(dve, g + 1, 1 - b)

            gates.zero(dve)
            split.lo(dve, WR)
            norm.take_lo(dve, 0, 0)
            split.lo(dve, W1)
            gates.shift(dve, 0)
            dve.wait_ge(rank_landed, 16)
            gates.choose(dve, 0, 0)
            gates.take(dve, 0, 0)
            groups(dve, step)
            take_y(GROUPS - 1)
            finish(GROUPS - 1)


def mix_gelu(nc, norm, ins, ahead, ahead_landed, x_sb, ident, out):
    with ExitStack() as ctx:
        def sem(name):
            return ctx.enter_context(nc.semaphore("mix1_" + name))

        def buf(name, shape, dt=F32):
            return ctx.enter_context(nc.sbuf_tensor("mix1_" + name, shape, dt))

        def psum(name):
            return ctx.enter_context(nc.psum_tensor("mix1_" + name, [P, GN], F32))

        w1, wg, wd_a, wd_b, bd = ([buf(name + part, stage.shape, F32R) for part in ("_hi", "_lo")]
                          for name, stage in zip(("w1", "wg", "wd_a", "wd_b", "bd"), ahead))
        wd = (wd_a, wd_b)
        split = Split(nc, sem, [(stage, *parts, ahead_landed, 16 * len(ahead))
                                for stage, parts in zip(ahead, (w1, wg, wd_a, wd_b, bd))])
        W1, WG, WD_A, WD_B, BD = range(5)
        rank = buf("rank", [P, GROUP, E8])
        b1 = buf("b1", [P, CH1])
        bg = buf("bg", [P, GROUP, E8])
        H = buf("H", [P, 2, GN])
        H_hi = buf("H_hi", [P, 2, CH1, GN], F32R)
        H_lo = buf("H_lo", [P, 2, CH1, GN], F32R)
        ps_y = [psum(f"y_{i}") for i in range(4)]
        ps_h = [psum(f"h_{i}") for i in range(2)]
        ps_misc, ps_bias = psum("misc"), psum("bias")
        norm.place(buf, ps_misc)
        gates = Gates(nc, buf, sem, ident, rank, ps_misc, top=1, bias=bg)
        small_landed = sem("small_landed")
        h_made = sem("h_made")
        gelu_done = sem("gelu_done")
        hi_done = sem("hi_done")
        lo_done = sem("lo_done")
        y_made = sem("y_made")
        y_used = sem("y_used")
        x_chain = sem("x_chain")
        bias_made = sem("bias_made")
        x_done = sem("x_done")
        out_stored = sem("out_stored")
        block = ctx.enter_context(nc.Block())

        def groups(eng, step):
            step(0, 0, True, True)
            step(1, 1, True, True)
            with eng.Fori(1, GROUPS // 2 - 1) as j:
                step(2 * j, 0, True, True)
                step(2 * j + 1, 1, True, True)
            step(GROUPS - 2, 0, True, False)
            step(GROUPS - 1, 1, False, False)

        @block.sync
        def _(sp):
            sp.dma_start(rank[:, :, :], ins["rank"]).then_inc(small_landed, 16)
            sp.dma_start(b1[:, :], ins["b1_cols"]).then_inc(small_landed, 16)
            sp.dma_start(bg[:, :, :], ins["bg_rows"]).then_inc(small_landed, 16)
            rows = out.rearrange("(t p) c -> p t c", p=P)

            def store(g):
                sp.wait_ge(x_done, g + 1)
                sp.dma_start(rows[:, bass.ds(g * GROUP, GROUP), :], x_sb[:, bass.ds(g * GROUP, GROUP), :]).then_inc(out_stored, 16)

            with sp.Fori(0, GROUPS) as g:
                store(g)
            sp.wait_ge(out_stored, 16 * GROUPS)

        @block.tensor
        def _(pe):
            def hidden(g, b, k):
                n = CH1 * g + k
                wait(pe, gelu_done, n - 1)
                if k == 0:
                    pe.wait_ge(norm.xT_lo_ready, g + 1)
                units = slice(k * P, (k + 1) * P)
                three_passes(nc, ps_h[k % 2][:, :], w1[0][:, units], w1[1][:, units], norm.xT_hi[:, b, :],
                             norm.xT_lo[:, b, :]).then_inc(h_made, 1)

            def logits(g, b):
                pe.wait_ge(hi_done, CH1 * g + CH1)
                pe.wait_ge(lo_done, CH1 * g + CH1)
                for k in range(CH1):
                    last = three_passes(nc, ps_misc[:, :], wg[0][:, k, :], wg[1][:, k, :], H_hi[:, b, k, :], H_lo[:, b, k, :],
                                        start=(k == 0), stop=(k == CH1 - 1))
                last.then_inc(gates.logits_made, 1)

            def unit(g, b, u):
                n, half = UNITS * g + u, u % 2
                wait(pe, y_used, n - 3)
                tok = slice(u // 2 * P, (u // 2 + 1) * P)
                if isinstance(g, int) and g == 0 and u < 2:
                    split.wait_for(pe, (WD_A, WD_B)[u])
                hi, lo = wd[half]
                for k in range(CH1):
                    last = three_passes(nc, ps_y[u % 4][:, :], H_hi[:, b, k, tok], H_lo[:, b, k, tok],
                                        hi[:, k, :, :].rearrange("p e c -> p (e c)"), lo[:, k, :, :].rearrange("p e c -> p (e c)"),
                                        start=(k == 0), stop=(k == CH1 - 1))
                last.then_inc(y_made, 1)

            def expert_bias(g, b):
                pe.wait_ge(gates.gT_ready, g + 1)
                wait(pe, x_done, g)
                if isinstance(g, int) and g == 0:
                    split.wait_for(pe, BD)
                for k in range(GROUP):
                    rows, gT = ps_bias[:, k * C:(k + 1) * C], gates.gT[:, b, k * P:(k + 1) * P]
                    nc.tensor.matmul(rows, gT, bd[0][:, :], start=True, stop=False)
                    last = nc.tensor.matmul(rows, gT, bd[1][:, :], start=False, stop=True)
                last.then_inc(bias_made, 1)

            def step(g, b, after, after2):
                for u in range(UNITS):
                    unit(g, b, u)
                    if isinstance(g, int) and g == 0 and u == 1:
                        gates.turn(pe, 0)
                        pe.wait_ge(gates.gT_ready, 1)
                    if u < 2 and after:
                        hidden(g + 1, 1 - b, 2 * u)
                        hidden(g + 1, 1 - b, 2 * u + 1)
                    if u == 2 and after2:
                        norm.turn(pe, g + 2)
                    if u == 3 and after:
                        if after2:
                            pe.wait_ge(norm.xT_lo_ready, g + 3)
                        logits(g + 1, 1 - b)
                    if u == 4 and after:
                        gates.turn_logits(pe, g + 1)
                    if u == 5:
                        expert_bias(g, b)
                    if u == 6 and after:
                        gates.turn(pe, g + 1)

            norm.turn(pe, 0)
            split.wait_for(pe, W1)
            for k in range(CH1):
                hidden(0, 0, k)
            norm.turn(pe, 1, ps_bias)
            pe.wait_ge(norm.xT_lo_ready, 2)
            split.wait_for(pe, WG)
            logits(0, 0)
            gates.turn_logits(pe, 0)
            groups(pe, step)

        @block.scalar
        def _(act):
            def activate(g, b, k):
                n = CH1 * g + k
                act.wait_ge(h_made, n + 1)
                wait(act, lo_done, n - 1)
                nc.scalar.activation(H[:, k % 2, :], ps_h[k % 2][:, :], ACT.Gelu, bias=b1[:, k:k + 1], scale=1.0).then_inc(gelu_done, 1)
                act.wait_ge(gelu_done, n + 1)
                nc.scalar.copy(H_hi[:, b, k, :], H[:, k % 2, :]).then_inc(hi_done, 1)

            def step(g, b, after, after2):
                for u in range(UNITS):
                    if u < 2 and after:
                        activate(g + 1, 1 - b, 2 * u)
                        activate(g + 1, 1 - b, 2 * u + 1)
                    if u == 2 and after2:
                        norm.take_hi(act, g + 2, b)
                    if u == 3 and after:
                        gates.take_logits(act, g + 1)
                    if u == 5 and after:
                        gates.exponential(act, g + 1)

            for n in (W1, WG, WD_A, WD_B, BD):
                split.hi(act, n)
            norm.take_hi(act, 0, 0)
            act.wait_ge(small_landed, 48)
            for k in range(CH1):
                activate(0, 0, k)
            norm.take_hi(act, 1, 1, ps_bias)
            gates.take_logits(act, 0)
            gates.exponential(act, 0)
            groups(act, step)

        @block.gpsimd
        def _(pool):
            def split_lo(g, b, k):
                pool.wait_ge(hi_done, CH1 * g + k + 1)
                nc.gpsimd.tensor_tensor(H_lo[:, b, k, :], H[:, k % 2, :], H_hi[:, b, k, :].bitcast(F32),
                                        ALU.subtract).then_inc(lo_done, 1)

            def step(g, b, after, after2):
                for k in range(CH1):
                    if after:
                        split_lo(g + 1, 1 - b, k)
                    if k == 0 and after2:
                        norm.root(pool, g + 2)

            norm.root(pool, 1)
            for k in range(CH1):
                split_lo(0, 0, k)
            groups(pool, step)

        @block.vector
        def _(dve):
            def use(g, b, u):
                n, k = UNITS * g + u, u // 2
                row = norm.tile(g, k)
                dve.wait_ge(y_made, n + 1)
                for e in range(E8 // 2):
                    if e > 0:
                        dve.wait_ge(x_chain, (E8 // 2 - 1) * n + e)
                    else:
                        wait(dve, y_used, n)
                    expert = (u % 2) * (E8 // 2) + e
                    last = nc.vector.scalar_tensor_tensor(row, ps_y[u % 4][:, e * C:(e + 1) * C],
                                                          gates.gate[:, b, k, expert:expert + 1], row, ALU.mult, ALU.add)
                    if e < E8 // 2 - 1:
                        last.then_inc(x_chain, 1)
                last.then_inc(y_used, 1)

            def use_bias(g):
                group = x_sb[:, bass.ds(g * GROUP, GROUP), :]
                dve.wait_ge(y_used, UNITS * g + UNITS)
                dve.wait_ge(bias_made, g + 1)
                nc.vector.tensor_tensor(group, ps_bias[:, :].rearrange("p (k c) -> p k c", k=GROUP), group,
                                        ALU.add).then_inc(x_done, 1)

            def step(g, b, after, after2):
                for u in range(UNITS):
                    use(g, b, u)
                    if u == 0 and after2:
                        norm.statistics(dve, g + 2)
                    if isinstance(g, int) and g == 0 and u == 1:
                        gates.take(dve, 0, 0)
                    if u == 1 and after2:
                        norm.scale(dve, g + 2)
                    if u == 2 and after2:
                        norm.take_lo(dve, g + 2, b)
                    if u == 4 and after:
                        gates.shift(dve, g + 1)
                    if u == 5 and after:
                        gates.choose(dve, g + 1, 1 - b)
                    if u == 6 and after:
                        gates.take(dve, g + 1, 1 - b)
                use_bias(g)

            gates.zero(dve)
            split.lo(dve, W1)
            split.lo(dve, WG)
            norm.take_lo(dve, 0, 0)
            norm.statistics(dve, 1)
            norm.scale(dve, 1)
            split.lo(dve, WD_A)
            split.lo(dve, WD_B)
            split.lo(dve, BD)
            norm.take_lo(dve, 1, 1, ps_bias)
            dve.wait_ge(small_landed, 48)
            gates.shift(dve, 0)
            gates.choose(dve, 0, 0)
            groups(dve, step)


def load_constants(nc, ins, x_sb, x_landed, ident, power, cols):
    with ExitStack() as ctx:
        landed = ctx.enter_context(nc.semaphore("constants_landed"))
        col_landed = ctx.enter_context(nc.semaphore("columns_landed"))
        power_filled = ctx.enter_context(nc.semaphore("power_filled"))
        filled = ctx.enter_context(nc.semaphore("columns_filled"))
        block = ctx.enter_context(nc.Block())

        @block.sync
        def _(sp):
            nodes = ins["x"].rearrange("(t p) c -> p t c", p=P)
            starts = sorted(x_landed)

            def load_nodes(g, end):
                tiles = slice(g * GROUP, end * GROUP)
                sp.dma_start(x_sb[:, tiles, :], nodes[:, tiles, :]).then_inc(x_landed[g], 16)

            load_nodes(starts[0], starts[1])
            for layer in ("L0", "L1"):
                a = ins[layer + "_gnn_a"]
                sp.dma_start(cols[layer + "a1"][:, :], a[0:C, :]).then_inc(col_landed, 16)
                sp.dma_start(cols[layer + "a2"][:, :], a[C:2 * C, :]).then_inc(col_landed, 16)
            sp.dma_start(ident[:, :], ins["identity"]).then_inc(landed, 16)
            sp.dma_start(cols["w"][:, :], ins["L1_gnn_W"]).then_inc(landed, 16)
            for g, end in zip(starts[1:], starts[2:] + [GROUPS]):
                load_nodes(g, end)
            sp.wait_ge(landed, 32)
            sp.wait_ge(col_landed, 64)

        @block.gpsimd
        def _(pool):
            nc.gpsimd.memset(power[:, :], -0.5).then_inc(power_filled, 1)
            pool.wait_ge(power_filled, 1)

        @block.vector
        def _(dve):
            for layer in ("L0", "L1"):
                nc.vector.memset(cols[layer + "rep"][:, :], 0.0).then_inc(filled, 1)
            dve.wait_ge(filled, 2)
            dve.wait_ge(col_landed, 64)
            for layer in ("L0", "L1"):
                nc.vector.tensor_scalar(cols[layer + "rep"][:, :], cols[layer + "rep"][:, :], cols[layer + "a2"][:, 0:1],
                                        None, ALU.add).then_inc(filled, 1)
            dve.wait_ge(filled, 4)


def build(nc, ins, out):
    with ExitStack() as ctx:
        def buf(name, shape, dt=F32):
            return ctx.enter_context(nc.sbuf_tensor(name, shape, dt))

        passed = [ctx.enter_context(nc.semaphore(name)) for name in ("passed_dve", "passed_pool")]
        x_sb = buf("x_sb", [P, TILES, C])
        ident = buf("ident", [P, P])
        power = buf("power", [P, GROUP])
        cols = {"w": buf("gnn_w", [P, C])}
        for layer in ("L0", "L1"):
            cols[layer + "a1"] = buf(layer + "a1", [P, 1])
            cols[layer + "a2"] = buf(layer + "a2", [P, 1])
            cols[layer + "rep"] = buf(layer + "rep", [P, P])
        x_landed = {g: ctx.enter_context(nc.semaphore(f"x_landed{g}")) for g in (0, 2, 4)}
        load_constants(nc, ins, x_sb, x_landed, ident, power, cols)
        for layer, slope, w in (("L0", 0.01, None), ("L1", 0.2, cols["w"])):
            with ExitStack() as outer:
                if w is None:
                    ahead = [("wr", [P, P], ins["router_wide"]), ("w1", [P, PAD0], ins["L0_ffn_w1"]),
                             ("w3", [P, PAD0], ins["L0_ffn_w3"])]
                else:
                    ahead = [("w1", [P, HID1], ins["L1_ffn_W1"]),
                             ("wg", [P, CH1, P], ins["gate_wide"].rearrange("(k p) e -> p k e", p=P)),
                             *((name, [P, CH1, E8 // 2, C], experts.rearrange("(k p) e c -> p k e c", p=P)) for name, experts in
                               (("wd_a", ins["Wd_by_unit"][:, 0:E8 // 2, :]), ("wd_b", ins["Wd_by_unit"][:, E8 // 2:E8, :]))),
                             ("bd", [2 * E8, C], ins["bd_twice"])]
                stages = [outer.enter_context(nc.sbuf_tensor(layer + "ahead_" + name, shape, F32)) for name, shape, _ in ahead]
                ahead_landed = outer.enter_context(nc.semaphore(layer + "ahead_landed"))
                loads = [(every(stage), dram) for stage, (_, _, dram) in zip(stages, ahead)]
                norm = Normaliser(nc, outer, layer + "mix_", passed, x_sb, power, ident)
                with ExitStack() as inner:
                    hrow = inner.enter_context(nc.sbuf_tensor(layer + "hrow", [P, TILES, C], F32))
                    s1 = inner.enter_context(nc.sbuf_tensor(layer + "s1", [P, TILES], F32))
                    s2b = inner.enter_context(nc.sbuf_tensor(layer + "s2b", [P, N], F32))
                    adjacency = Adjacency(nc, inner, layer, ins["adj"], passed)
                    terms = Terms(nc, inner, layer, adjacency, s2b, slope, passed)
                    prepare(nc, layer + "prep_", passed, x_sb, x_landed if w is None else None, adjacency, terms, ident,
                            power, hrow, s1, s2b, cols[layer + "rep"], cols[layer + "a1"], w)
                    attend(nc, layer + "att_", passed, adjacency, terms, norm, loads, ahead_landed, x_sb, ident, hrow, s1,
                           slope, elu=w is not None)
                mixture = mix_silu if w is None else mix_gelu
                mixture(nc, norm, ins, stages, ahead_landed, x_sb, ident, out)


def kernel(**inputs):
    import numpy as np
    import concourse.bacc as bacc
    from concourse.bass_utils import run_bass_kernel_spmd

    a = {k: np.ascontiguousarray(v) for k, v in inputs.items()}

    def filled(rows, count):
        return np.pad(rows, ((0, count - rows.shape[0]), (0, 0)))

    for name in ("w1", "w3"):
        a["L0_ffn_" + name] = np.ascontiguousarray(filled(a["L0_ffn_" + name].reshape(ROWS0, C), PAD0).T)
    a["L0_ffn_w2"] = filled(a["L0_ffn_w2"].transpose(0, 2, 1).reshape(ROWS0, C), PAD0)
    a["router_wide"] = np.ascontiguousarray(filled(a["L0_ffn_router_w"], P).T)
    a["gate_wide"] = np.ascontiguousarray(filled(a["L1_ffn_Wg"].T, P).T)
    a["identity"] = np.eye(P, dtype=np.float32)
    owner = (np.arange(PAD0) // HID0)[None, :] == np.arange(E8)[:, None]
    a["owner"] = np.concatenate([owner, owner]).astype(np.float32)
    a["Wd_by_unit"] = np.ascontiguousarray(a["L1_ffn_Wd"].transpose(1, 0, 2))
    a["bd_twice"] = np.concatenate([a["L1_ffn_bd"], a["L1_ffn_bd"]])
    a["b1_cols"] = np.ascontiguousarray(a["L1_ffn_b1"].reshape(CH1, P).T)
    a["bg_rows"] = np.ascontiguousarray(np.broadcast_to(a["L1_ffn_bg"], (P, GROUP, E8)))
    a["rank"] = np.tile(np.arange(E8, 0, -1, dtype=np.float32), (P, GROUP, 1))

    nc = bacc.Bacc("TRN2", target_bir_lowering=False, num_devices=1)
    arrays, ins = {}, {}
    for name, value in a.items():
        arrays["in_" + name] = value
        ins[name] = nc.dram_tensor("in_" + name, value.shape, mybir.dt.from_np(value.dtype), kind="ExternalInput").ap()
    out = nc.dram_tensor("out", (N, C), F32, kind="ExternalOutput").ap()
    build(nc, ins, out)
    r = run_bass_kernel_spmd(nc, [arrays], core_ids=[0])
    return r.results[0]["out"]
```
